# Optimizing a Trainium2 kernel written in Bass

```python
import numpy as np
import jax
import jax.numpy as jnp

def _softmax(x, axis=-1):
    return jax.nn.softmax(x, axis=axis)

def _gelu(x):
    return jax.nn.gelu(x, approximate=True)

def _silu(x):
    return jax.nn.silu(x)

def _sigmoid(x):
    return jax.nn.sigmoid(x)

def _layernorm(x, axis=-1, eps=1e-05):
    m = jnp.mean(x, axis=axis, keepdims=True)
    v = jnp.var(x, axis=axis, keepdims=True)
    return (x - m) / jnp.sqrt(v + eps)

def _scatter_add(tgt, idx, src, axis=0):
    return tgt.at[idx].add(src)

def _segment_sum(src, seg, n):
    return jax.ops.segment_sum(src, seg, n)
kernel_name = 'mk_vit_tower_d4_tok_img768_r4_236d19'

def setup_inputs(seed: int=0):
    np.random.seed(seed)
    _w = jnp.asarray

    def _rec_inputs():
        import jax
        import jax.numpy as jnp
        _rk = jax.random.key(seed)
        x = -0.000356955 + 1 * jax.random.normal(jax.random.fold_in(_rk, 1), (16, 3, 96, 96), jnp.float32)
        return x
    x = _rec_inputs()

    def _L0_tok_setup():
        import jax, jax.numpy as jnp
        import numpy as np
        PATCH = 16
        EMBED = 192
        key = jax.random.key(seed)
        k1, k2, k3 = jax.random.split(key, 3)
        x = jax.random.normal(k1, (128, 3, 224, 224), dtype=jnp.float32)
        patch_dim = PATCH * PATCH * 3
        W = jax.random.normal(k2, (patch_dim, EMBED), dtype=jnp.float32) / np.sqrt(patch_dim)
        b = jax.random.normal(k3, (EMBED,), dtype=jnp.float32) * 0.01
        return {'x': x, 'W': W, 'b': b}
    _L0_tok_all = _L0_tok_setup()
    _L0_tok_in = {k: v for k, v in _L0_tok_all.items() if k in ('W', 'b')}
    del _L0_tok_all

    def _L0_attn_setup():
        import jax, jax.numpy as jnp
        import numpy as np
        DIM = 192
        B, N = (8, 512)
        TEMPERATURE = 3.0
        key = jax.random.key(seed)
        ks = jax.random.split(key, 5)
        lim = 1.0 / np.sqrt(DIM)
        x = jax.random.normal(ks[0], (B, N, DIM), dtype=jnp.float32)
        w_qkv = jax.random.uniform(ks[1], (3 * DIM, DIM), minval=-lim, maxval=lim, dtype=jnp.float32)
        b_qkv = jax.random.uniform(ks[2], (3 * DIM,), minval=-lim, maxval=lim, dtype=jnp.float32)
        w_proj = jax.random.uniform(ks[3], (DIM, DIM), minval=-lim, maxval=lim, dtype=jnp.float32)
        b_proj = jax.random.uniform(ks[4], (DIM,), minval=-lim, maxval=lim, dtype=jnp.float32)
        return {'x': x, 'w_qkv': w_qkv, 'b_qkv': b_qkv, 'w_proj': w_proj, 'b_proj': b_proj}
    _L0_attn_all = _L0_attn_setup()
    _L0_attn_in = {k: v for k, v in _L0_attn_all.items() if k in ('w_qkv', 'b_qkv', 'w_proj', 'b_proj')}
    del _L0_attn_all

    def _L0_ffn_setup():
        import jax, jax.numpy as jnp
        import numpy as np
        E = 16
        TOP_K = 2
        C = 192
        I = 384
        B, T = (8, 512)

        def _expert(x, wg_e, wu_e, wd_e):
            return jax.nn.silu(x @ wg_e) * (x @ wu_e) @ wd_e
        key = jax.random.key(seed)
        ks = jax.random.split(key, 9)
        s = 0.02
        return {'x': jax.random.normal(ks[0], (B, T, C), jnp.float32), 'w_gate': jax.random.normal(ks[1], (C, E), jnp.float32) * s, 'expert_bias': jnp.zeros((E,), jnp.float32), 'wg': jax.random.normal(ks[2], (E, C, I), jnp.float32) * s, 'wu': jax.random.normal(ks[3], (E, C, I), jnp.float32) * s, 'wd': jax.random.normal(ks[4], (E, I, C), jnp.float32) * s, 'swg': jax.random.normal(ks[5], (C, I), jnp.float32) * s, 'swu': jax.random.normal(ks[6], (C, I), jnp.float32) * s, 'swd': jax.random.normal(ks[7], (I, C), jnp.float32) * s}
    _L0_ffn_all = _L0_ffn_setup()
    _L0_ffn_in = {k: v for k, v in _L0_ffn_all.items() if k in ('w_gate', 'expert_bias', 'wg', 'wu', 'wd', 'swg', 'swu', 'swd')}
    del _L0_ffn_all

    def _L1_attn_setup():
        import jax, jax.numpy as jnp
        import numpy as np
        import math
        B, S, D = (4, 1024, 192)
        key = jax.random.key(seed)
        ks = jax.random.split(key, 7)
        sc = 0.02
        return {'x': jax.random.normal(ks[0], (B, S, D), dtype=jnp.float32), 'Wq': jax.random.normal(ks[1], (D, D), dtype=jnp.float32) * sc, 'bq': jax.random.normal(ks[2], (D,), dtype=jnp.float32) * sc, 'Wk': jax.random.normal(ks[3], (D, D), dtype=jnp.float32) * sc, 'bk': jax.random.normal(ks[4], (D,), dtype=jnp.float32) * sc, 'Wv': jax.random.normal(ks[5], (D, D), dtype=jnp.float32) * sc, 'bv': jax.random.normal(ks[6], (D,), dtype=jnp.float32) * sc}
    _L1_attn_all = _L1_attn_setup()
    _L1_attn_in = {k: v for k, v in _L1_attn_all.items() if k in ('Wq', 'bq', 'Wk', 'bk', 'Wv', 'bv')}
    del _L1_attn_all

    def _L1_ffn_setup():
        import jax, jax.numpy as jnp
        import numpy as np
        DIM = 192
        HEADS = 12
        HD = DIM // HEADS
        MLP = 768
        RHD = 128
        RANK = 64
        BS = 2
        RESERVE = 1
        EPS = 1e-05

        def _ln(x, g, b):
            m = jnp.mean(x, axis=-1, keepdims=True)
            v = jnp.var(x, axis=-1, keepdims=True)
            return (x - m) / jnp.sqrt(v + EPS) * g + b

        def _gelu(t):
            return jax.nn.gelu(t, approximate=False)

        def _forward(x, wq, bq, wk, bk, wv, bv, wo, bo, ln1_g, ln1_b, ln2_g, ln2_b, fc1_w, fc1_b, fc2_w, fc2_b, r_ln_g, r_ln_b, r_in_w, r_in_b, r_o1_w, r_o1_b, r_o2_w, r_o2_b, r_o3_w, r_o3_b, lra_down, lra_up):
            B, N, _ = x.shape
            e = _gelu(_ln(x, r_ln_g, r_ln_b) @ r_in_w.T + r_in_b)
            g = jnp.mean(e[:, RESERVE:, :], axis=1, keepdims=True)
            f = jnp.concatenate([e, jnp.broadcast_to(g, e.shape)], axis=-1)
            h1 = _gelu(f @ r_o1_w.T + r_o1_b)
            h2 = _gelu(h1 @ r_o2_w.T + r_o2_b)
            logits = (h2 @ r_o3_w.T + r_o3_b).reshape(B, N, BS, 2)
            hard = jax.nn.one_hot(jnp.argmax(logits, axis=-1), 2, dtype=x.dtype)
            keep = jnp.broadcast_to(jnp.array([0.0, 1.0], dtype=x.dtype), hard[:, :RESERVE].shape)
            hard = hard.at[:, :RESERVE].set(keep)
            hard = jax.lax.stop_gradient(hard)
            bits = hard[..., 1]
            indices = (bits * jnp.array([2.0, 1.0], dtype=x.dtype)).sum(-1).astype(jnp.int32)
            indices = jax.lax.stop_gradient(indices)
            xa = _ln(x, ln1_g, ln1_b)
            q = (xa @ wq.T + bq).reshape(B, N, HEADS, HD).transpose(0, 2, 1, 3)
            k = (xa @ wk.T + bk).reshape(B, N, HEADS, HD).transpose(0, 2, 1, 3)
            v = (xa @ wv.T + bv).reshape(B, N, HEADS, HD).transpose(0, 2, 1, 3)
            s = jax.nn.softmax(jnp.einsum('bhqd,bhkd->bhqk', q, k) / np.float32(np.sqrt(HD)), axis=-1)
            o = jnp.einsum('bhqk,bhkd->bhqd', s, v).transpose(0, 2, 1, 3).reshape(B, N, DIM)
            o = o @ wo.T + bo
            h = x + bits[:, :, 0:1] * o
            xf = _ln(h, ln2_g, ln2_b)
            ff = _gelu(xf @ fc1_w.T + fc1_b) @ fc2_w.T + fc2_b
            out = h + bits[:, :, 1:2] * ff
            down = jnp.einsum('bnd,krd->bknr', out, lra_down)
            up = jnp.einsum('bknr,kdr->bknd', down, lra_up)
            sel = jax.nn.one_hot(indices, 3, dtype=x.dtype)
            out = out + jnp.einsum('bknd,bnk->bnd', up, sel)
            return out
        key = jax.random.key(seed)
        ks = iter(jax.random.split(key, 40))

        def w(shape, std=0.02):
            return (jax.random.normal(next(ks), shape) * std).astype(jnp.float32)
        B, N = (128, 197)
        inp = {'x': jax.random.normal(next(ks), (B, N, DIM), dtype=jnp.float32)}
        inp.update(wq=w((DIM, DIM)), bq=jnp.zeros((DIM,), jnp.float32), wk=w((DIM, DIM)), bk=jnp.zeros((DIM,), jnp.float32), wv=w((DIM, DIM)), bv=jnp.zeros((DIM,), jnp.float32), wo=w((DIM, DIM)), bo=jnp.zeros((DIM,), jnp.float32), ln1_g=jnp.ones((DIM,), jnp.float32), ln1_b=jnp.zeros((DIM,), jnp.float32), ln2_g=jnp.ones((DIM,), jnp.float32), ln2_b=jnp.zeros((DIM,), jnp.float32), fc1_w=w((MLP, DIM)), fc1_b=jnp.zeros((MLP,), jnp.float32), fc2_w=w((DIM, MLP)), fc2_b=jnp.zeros((DIM,), jnp.float32), r_ln_g=jnp.ones((DIM,), jnp.float32), r_ln_b=jnp.zeros((DIM,), jnp.float32), r_in_w=w((RHD, DIM)), r_in_b=jnp.zeros((RHD,), jnp.float32), r_o1_w=w((RHD, 2 * RHD)), r_o1_b=jnp.zeros((RHD,), jnp.float32), r_o2_w=w((RHD // 2, RHD)), r_o2_b=jnp.zeros((RHD // 2,), jnp.float32), r_o3_w=w((2 * BS, RHD // 2), 0.01), r_o3_b=jnp.array([0.0, 5.0, 0.0, 5.0], dtype=jnp.float32), lra_down=w((3, RANK, DIM), 0.01), lra_up=w((3, DIM, RANK), 0.01))
        return inp
    _L1_ffn_all = _L1_ffn_setup()
    _L1_ffn_in = {k: v for k, v in _L1_ffn_all.items() if k in ('wq', 'bq', 'wk', 'bk', 'wv', 'bv', 'wo', 'bo', 'ln1_g', 'ln1_b', 'ln2_g', 'ln2_b', 'fc1_w', 'fc1_b', 'fc2_w', 'fc2_b', 'r_ln_g', 'r_ln_b', 'r_in_w', 'r_in_b', 'r_o1_w', 'r_o1_b', 'r_o2_w', 'r_o2_b', 'r_o3_w', 'r_o3_b', 'lra_down', 'lra_up')}
    del _L1_ffn_all

    def _L2_attn_setup():
        import jax, jax.numpy as jnp
        import numpy as np
        Bsz, L, D, N = (2, 512, 192, 16)

        def _forward(x, A, W_delta, delta_bias, W_B, W_C):
            B, Lx, Dx = x.shape
            Nx = A.shape[1]
            delta = jax.nn.softplus(x @ W_delta.T + delta_bias)
            B_sel = (x @ W_B.T).reshape(B, Lx, Dx, Nx)
            C_sel = (x @ W_C.T).reshape(B, Lx, Dx, Nx)
            dA = delta[..., None] * A
            A_bar = jnp.exp(dA)
            B_bar = (A_bar - 1.0) / dA * delta[..., None] * B_sel
            Bx = B_bar * x[..., None]

            def step(h, inp):
                a_t, bx_t, c_t = inp
                h = a_t * h + bx_t
                y_t = jnp.sum(h * c_t, axis=-1)
                return (h, y_t)
            h0 = jnp.zeros((B, Dx, Nx), dtype=x.dtype)
            scan_in = (jnp.moveaxis(A_bar, 1, 0), jnp.moveaxis(Bx, 1, 0), jnp.moveaxis(C_sel, 1, 0))
            _, ys = jax.lax.scan(step, h0, scan_in)
            return jnp.moveaxis(ys, 0, 1)
        key = jax.random.key(seed)
        ks = jax.random.split(key, 6)
        x = jax.random.normal(ks[0], (Bsz, L, D), dtype=jnp.float32)
        A = -0.5 - 0.5 * jax.random.uniform(ks[1], (D, N), dtype=jnp.float32)
        s = 1.0 / np.sqrt(D).astype(np.float32)
        W_delta = jax.random.normal(ks[2], (D, D), dtype=jnp.float32) * s
        dt = jax.random.uniform(ks[3], (D,), dtype=jnp.float32) * 0.099 + 0.001
        delta_bias = jnp.log(jnp.expm1(dt))
        W_B = jax.random.normal(ks[4], (D * N, D), dtype=jnp.float32) * s
        W_C = jax.random.normal(ks[5], (D * N, D), dtype=jnp.float32) * s
        return {'x': x, 'A': A, 'W_delta': W_delta, 'delta_bias': delta_bias, 'W_B': W_B, 'W_C': W_C}
    _L2_attn_all = _L2_attn_setup()
    _L2_attn_in = {k: v for k, v in _L2_attn_all.items() if k in ('A', 'W_delta', 'delta_bias', 'W_B', 'W_C')}
    del _L2_attn_all

    def _L2_ffn_setup():
        import jax, jax.numpy as jnp
        import numpy as np
        E = 128
        I = 464
        IS = 928
        K = 6
        G = 1
        TG = 1
        SCALE = 2.5
        CAP = 192

        def moe_forward(hidden_states, Wg, e_bias, W_gate_up, W_down, Wsg, Wsu, Wsd):
            B, S, H = hidden_states.shape
            x = hidden_states.reshape(-1, H)
            T = x.shape[0]
            logits = x.astype(jnp.float32) @ Wg.T
            sig = jax.nn.sigmoid(logits)
            choice = sig + e_bias[None, :]
            grp = choice.reshape(T, G, E // G)
            group_scores = jax.lax.top_k(grp, 2)[0].sum(-1)
            gidx = jax.lax.top_k(group_scores, TG)[1]
            gmask = jnp.zeros((T, G), jnp.float32).at[jnp.arange(T)[:, None], gidx].set(1.0)
            smask = jnp.repeat(gmask, E // G, axis=1)
            scores_for_choice = jnp.where(smask > 0, choice, 0.0)
            topk_idx = jax.lax.top_k(scores_for_choice, K)[1]
            topk_w = jnp.take_along_axis(sig, topk_idx, axis=1)
            topk_w = topk_w / (topk_w.sum(-1, keepdims=True) + 1e-20)
            topk_w = topk_w * SCALE
            P = T * K
            flat_e = topk_idx.reshape(-1)
            order = jnp.argsort(flat_e)
            se = flat_e[order]
            counts = jax.ops.segment_sum(jnp.ones(P, jnp.int32), flat_e, num_segments=E)
            starts = jnp.cumsum(counts) - counts
            pos = jnp.arange(P) - starts[se]
            buf_idx = jnp.where(pos < CAP, se * CAP + pos, E * CAP)
            tok_of_pair = (order // K).astype(jnp.int32)
            w_of_pair = topk_w.reshape(-1)[order]
            token_buf = jnp.zeros((E * CAP,), jnp.int32).at[buf_idx].set(tok_of_pair, mode='drop')
            w_buf = jnp.zeros((E * CAP,), x.dtype).at[buf_idx].set(w_of_pair.astype(x.dtype), mode='drop')
            xb = x[token_buf].reshape(E, CAP, H)
            gu = jnp.einsum('ech,ehf->ecf', xb, W_gate_up)
            g, u = jnp.split(gu, 2, axis=-1)
            inter = jax.nn.silu(g) * u
            yb = jnp.einsum('eci,eih->ech', inter, W_down)
            yb = yb * w_buf.reshape(E, CAP, 1)
            routed = jnp.zeros((T, H), x.dtype).at[token_buf].add(yb.reshape(E * CAP, H))
            shared = jax.nn.silu(x @ Wsg) * (x @ Wsu) @ Wsd
            return (routed + shared).reshape(B, S, H)
        key = jax.random.key(seed)
        ks = jax.random.split(key, 8)
        B, S, H = (1, 512, 192)
        sc = 0.02
        return {'hidden_states': jax.random.normal(ks[0], (B, S, H), jnp.float32), 'Wg': jax.random.normal(ks[1], (E, H), jnp.float32) * sc, 'e_bias': jnp.zeros((E,), jnp.float32), 'W_gate_up': jax.random.normal(ks[2], (E, H, 2 * I), jnp.float32) * sc, 'W_down': jax.random.normal(ks[3], (E, I, H), jnp.float32) * sc, 'Wsg': jax.random.normal(ks[4], (H, IS), jnp.float32) * sc, 'Wsu': jax.random.normal(ks[5], (H, IS), jnp.float32) * sc, 'Wsd': jax.random.normal(ks[6], (IS, H), jnp.float32) * sc}
    _L2_ffn_all = _L2_ffn_setup()
    _L2_ffn_in = {k: v for k, v in _L2_ffn_all.items() if k in ('Wg', 'e_bias', 'W_gate_up', 'W_down', 'Wsg', 'Wsu', 'Wsd')}
    del _L2_ffn_all

    def _L3_attn_setup():
        import jax, jax.numpy as jnp
        import numpy as np
        B, S, E, H = (8, 256, 192, 12)
        SPARSITY = 0.4
        key = jax.random.key(seed)
        ks = jax.random.split(key, 5)
        return {'hidden_states': jax.random.normal(ks[0], (B, S, E), dtype=jnp.float32), 'W_qkv': jax.random.normal(ks[1], (E, 3 * E), dtype=jnp.float32) * E ** (-0.5), 'b_qkv': jax.random.normal(ks[2], (3 * E,), dtype=jnp.float32) * 0.02, 'W_proj': jax.random.normal(ks[3], (E, E), dtype=jnp.float32) * E ** (-0.5), 'b_proj': jax.random.normal(ks[4], (E,), dtype=jnp.float32) * 0.02}
    _L3_attn_all = _L3_attn_setup()
    _L3_attn_in = {k: v for k, v in _L3_attn_all.items() if k in ('W_qkv', 'b_qkv', 'W_proj', 'b_proj')}
    del _L3_attn_all

    def _L3_ffn_setup():
        import jax, jax.numpy as jnp
        import numpy as np
        SEQ, BATCH, EMBED = (256, 2, 192)
        E = 16
        FFN_H = 384
        K_SHARED = 1
        K_ROUTE = 3
        LN_EPS = 1e-05
        NEG_INF = -1000000000.0
        key = jax.random.key(seed)
        ks = jax.random.split(key, 4)
        x = jax.random.normal(ks[0], (SEQ, BATCH, EMBED), dtype=jnp.float32)
        gate_w = jax.random.normal(ks[1], (EMBED, E), dtype=jnp.float32) * 0.02
        gate_b = jnp.zeros((E,), jnp.float32)
        fc1_w = jax.random.normal(ks[2], (E, EMBED, FFN_H), dtype=jnp.float32) * 0.02
        fc1_b = jnp.zeros((E, FFN_H), jnp.float32)
        ln_w = jnp.ones((E, FFN_H), jnp.float32)
        ln_b = jnp.zeros((E, FFN_H), jnp.float32)
        fc2_w = jax.random.normal(ks[3], (E, FFN_H, EMBED), dtype=jnp.float32) * 0.02
        fc2_b = jnp.zeros((E, EMBED), jnp.float32)
        return {'x': x, 'gate_w': gate_w, 'gate_b': gate_b, 'fc1_w': fc1_w, 'fc1_b': fc1_b, 'ln_w': ln_w, 'ln_b': ln_b, 'fc2_w': fc2_w, 'fc2_b': fc2_b}
    _L3_ffn_all = _L3_ffn_setup()
    _L3_ffn_in = {k: v for k, v in _L3_ffn_all.items() if k in ('gate_w', 'gate_b', 'fc1_w', 'fc1_b', 'ln_w', 'ln_b', 'fc2_w', 'fc2_b')}
    del _L3_ffn_all
    return {'x': x, 'L0_tok_W': _L0_tok_in['W'], 'L0_tok_b': _L0_tok_in['b'], 'L0_attn_w_qkv': _L0_attn_in['w_qkv'], 'L0_attn_b_qkv': _L0_attn_in['b_qkv'], 'L0_attn_w_proj': _L0_attn_in['w_proj'], 'L0_attn_b_proj': _L0_attn_in['b_proj'], 'L0_ffn_w_gate': _L0_ffn_in['w_gate'], 'L0_ffn_expert_bias': _L0_ffn_in['expert_bias'], 'L0_ffn_wg': _L0_ffn_in['wg'], 'L0_ffn_wu': _L0_ffn_in['wu'], 'L0_ffn_wd': _L0_ffn_in['wd'], 'L0_ffn_swg': _L0_ffn_in['swg'], 'L0_ffn_swu': _L0_ffn_in['swu'], 'L0_ffn_swd': _L0_ffn_in['swd'], 'L1_attn_Wq': _L1_attn_in['Wq'], 'L1_attn_bq': _L1_attn_in['bq'], 'L1_attn_Wk': _L1_attn_in['Wk'], 'L1_attn_bk': _L1_attn_in['bk'], 'L1_attn_Wv': _L1_attn_in['Wv'], 'L1_attn_bv': _L1_attn_in['bv'], 'L1_ffn_wq': _L1_ffn_in['wq'], 'L1_ffn_bq': _L1_ffn_in['bq'], 'L1_ffn_wk': _L1_ffn_in['wk'], 'L1_ffn_bk': _L1_ffn_in['bk'], 'L1_ffn_wv': _L1_ffn_in['wv'], 'L1_ffn_bv': _L1_ffn_in['bv'], 'L1_ffn_wo': _L1_ffn_in['wo'], 'L1_ffn_bo': _L1_ffn_in['bo'], 'L1_ffn_ln1_g': _L1_ffn_in['ln1_g'], 'L1_ffn_ln1_b': _L1_ffn_in['ln1_b'], 'L1_ffn_ln2_g': _L1_ffn_in['ln2_g'], 'L1_ffn_ln2_b': _L1_ffn_in['ln2_b'], 'L1_ffn_fc1_w': _L1_ffn_in['fc1_w'], 'L1_ffn_fc1_b': _L1_ffn_in['fc1_b'], 'L1_ffn_fc2_w': _L1_ffn_in['fc2_w'], 'L1_ffn_fc2_b': _L1_ffn_in['fc2_b'], 'L1_ffn_r_ln_g': _L1_ffn_in['r_ln_g'], 'L1_ffn_r_ln_b': _L1_ffn_in['r_ln_b'], 'L1_ffn_r_in_w': _L1_ffn_in['r_in_w'], 'L1_ffn_r_in_b': _L1_ffn_in['r_in_b'], 'L1_ffn_r_o1_w': _L1_ffn_in['r_o1_w'], 'L1_ffn_r_o1_b': _L1_ffn_in['r_o1_b'], 'L1_ffn_r_o2_w': _L1_ffn_in['r_o2_w'], 'L1_ffn_r_o2_b': _L1_ffn_in['r_o2_b'], 'L1_ffn_r_o3_w': _L1_ffn_in['r_o3_w'], 'L1_ffn_r_o3_b': _L1_ffn_in['r_o3_b'], 'L1_ffn_lra_down': _L1_ffn_in['lra_down'], 'L1_ffn_lra_up': _L1_ffn_in['lra_up'], 'L2_attn_A': _L2_attn_in['A'], 'L2_attn_W_delta': _L2_attn_in['W_delta'], 'L2_attn_delta_bias': _L2_attn_in['delta_bias'], 'L2_attn_W_B': _L2_attn_in['W_B'], 'L2_attn_W_C': _L2_attn_in['W_C'], 'L2_ffn_Wg': _L2_ffn_in['Wg'], 'L2_ffn_e_bias': _L2_ffn_in['e_bias'], 'L2_ffn_W_gate_up': _L2_ffn_in['W_gate_up'], 'L2_ffn_W_down': _L2_ffn_in['W_down'], 'L2_ffn_Wsg': _L2_ffn_in['Wsg'], 'L2_ffn_Wsu': _L2_ffn_in['Wsu'], 'L2_ffn_Wsd': _L2_ffn_in['Wsd'], 'L3_attn_W_qkv': _L3_attn_in['W_qkv'], 'L3_attn_b_qkv': _L3_attn_in['b_qkv'], 'L3_attn_W_proj': _L3_attn_in['W_proj'], 'L3_attn_b_proj': _L3_attn_in['b_proj'], 'L3_ffn_gate_w': _L3_ffn_in['gate_w'], 'L3_ffn_gate_b': _L3_ffn_in['gate_b'], 'L3_ffn_fc1_w': _L3_ffn_in['fc1_w'], 'L3_ffn_fc1_b': _L3_ffn_in['fc1_b'], 'L3_ffn_ln_w': _L3_ffn_in['ln_w'], 'L3_ffn_ln_b': _L3_ffn_in['ln_b'], 'L3_ffn_fc2_w': _L3_ffn_in['fc2_w'], 'L3_ffn_fc2_b': _L3_ffn_in['fc2_b']}

def reference(x, L0_tok_W, L0_tok_b, L0_attn_w_qkv, L0_attn_b_qkv, L0_attn_w_proj, L0_attn_b_proj, L0_ffn_w_gate, L0_ffn_expert_bias, L0_ffn_wg, L0_ffn_wu, L0_ffn_wd, L0_ffn_swg, L0_ffn_swu, L0_ffn_swd, L1_attn_Wq, L1_attn_bq, L1_attn_Wk, L1_attn_bk, L1_attn_Wv, L1_attn_bv, L1_ffn_wq, L1_ffn_bq, L1_ffn_wk, L1_ffn_bk, L1_ffn_wv, L1_ffn_bv, L1_ffn_wo, L1_ffn_bo, L1_ffn_ln1_g, L1_ffn_ln1_b, L1_ffn_ln2_g, L1_ffn_ln2_b, L1_ffn_fc1_w, L1_ffn_fc1_b, L1_ffn_fc2_w, L1_ffn_fc2_b, L1_ffn_r_ln_g, L1_ffn_r_ln_b, L1_ffn_r_in_w, L1_ffn_r_in_b, L1_ffn_r_o1_w, L1_ffn_r_o1_b, L1_ffn_r_o2_w, L1_ffn_r_o2_b, L1_ffn_r_o3_w, L1_ffn_r_o3_b, L1_ffn_lra_down, L1_ffn_lra_up, L2_attn_A, L2_attn_W_delta, L2_attn_delta_bias, L2_attn_W_B, L2_attn_W_C, L2_ffn_Wg, L2_ffn_e_bias, L2_ffn_W_gate_up, L2_ffn_W_down, L2_ffn_Wsg, L2_ffn_Wsu, L2_ffn_Wsd, L3_attn_W_qkv, L3_attn_b_qkv, L3_attn_W_proj, L3_attn_b_proj, L3_ffn_gate_w, L3_ffn_gate_b, L3_ffn_fc1_w, L3_ffn_fc1_b, L3_ffn_ln_w, L3_ffn_ln_b, L3_ffn_fc2_w, L3_ffn_fc2_b):
    import jax
    import jax.numpy as jnp

    def _L0_tok_ref(x, W, b):
        import jax, jax.numpy as jnp
        import numpy as np
        PATCH = 16
        EMBED = 192
        B, C, H, Wd = x.shape
        p = PATCH
        nh, nw = (H // p, Wd // p)
        patches = x.reshape(B, C, nh, p, nw, p).transpose(0, 1, 2, 4, 3, 5)
        patches = patches.reshape(B, C, nh * nw, p * p).transpose(0, 2, 1, 3)
        patches = patches.reshape(B, nh * nw, C * p * p)
        return jnp.einsum('bnd,de->bne', patches, W) + b

    def _L0_attn_ref(x, w_qkv, b_qkv, w_proj, b_proj):
        import jax, jax.numpy as jnp
        import numpy as np
        DIM = 192
        B, N = (8, 512)
        TEMPERATURE = 3.0
        scale = DIM ** (-0.5)
        qkv = jnp.einsum('bnd,ed->bne', x, w_qkv) + b_qkv
        q, k, v = jnp.split(qkv, 3, axis=-1)
        scores = jnp.einsum('bnd,bmd->bnm', q, k) * scale
        attn = jax.nn.softmax(scores / TEMPERATURE, axis=-1)
        out = jnp.einsum('bnm,bmd->bnd', attn, v)
        return jnp.einsum('bnd,ed->bne', out, w_proj) + b_proj

    def _L0_ffn_ref(x, w_gate, expert_bias, wg, wu, wd, swg, swu, swd):
        import jax, jax.numpy as jnp
        import numpy as np
        E = 16
        TOP_K = 2
        C = 192
        I = 384
        B, T = (8, 512)

        def _expert(x, wg_e, wu_e, wd_e):
            return jax.nn.silu(x @ wg_e) * (x @ wu_e) @ wd_e
        Bq, Tq, Cq = x.shape
        xf = x.reshape(-1, Cq)
        n_tok = xf.shape[0]
        shared = _expert(xf, swg, swu, swd)
        logits = xf @ w_gate + expert_bias
        probs = jax.nn.softmax(logits, axis=-1)
        topk_p, topk_i = jax.lax.top_k(probs, TOP_K)
        topk_p = topk_p / jnp.sum(topk_p, axis=-1, keepdims=True)
        comb = jnp.zeros((n_tok, E), xf.dtype).at[jnp.arange(n_tok)[:, None], topk_i].add(topk_p)
        routed = jnp.zeros_like(xf)
        for e in range(E):
            routed = routed + comb[:, e:e + 1] * _expert(xf, wg[e], wu[e], wd[e])
        return (shared + routed).reshape(Bq, Tq, Cq)

    def _L1_attn_ref(x, Wq, bq, Wk, bk, Wv, bv):
        import jax, jax.numpy as jnp
        import numpy as np
        import math
        B, S, D = (4, 1024, 192)
        q = jnp.einsum('bsd,ed->bse', x, Wq) + bq
        k = jnp.einsum('bsd,ed->bse', x, Wk) + bk
        v = jnp.einsum('bsd,ed->bse', x, Wv) + bv
        scale = 1.0 / math.sqrt(x.shape[-1])
        scores = jnp.einsum('bsd,btd->bst', q, k) * scale
        return jnp.einsum('bst,btd->bsd', scores, v)

    def _L1_ffn_ref(x, wq, bq, wk, bk, wv, bv, wo, bo, ln1_g, ln1_b, ln2_g, ln2_b, fc1_w, fc1_b, fc2_w, fc2_b, r_ln_g, r_ln_b, r_in_w, r_in_b, r_o1_w, r_o1_b, r_o2_w, r_o2_b, r_o3_w, r_o3_b, lra_down, lra_up):
        import jax, jax.numpy as jnp
        import numpy as np
        DIM = 192
        HEADS = 12
        HD = DIM // HEADS
        MLP = 768
        RHD = 128
        RANK = 64
        BS = 2
        RESERVE = 1
        EPS = 1e-05

        def _ln(x, g, b):
            m = jnp.mean(x, axis=-1, keepdims=True)
            v = jnp.var(x, axis=-1, keepdims=True)
            return (x - m) / jnp.sqrt(v + EPS) * g + b

        def _gelu(t):
            return jax.nn.gelu(t, approximate=False)

        def _forward(x, wq, bq, wk, bk, wv, bv, wo, bo, ln1_g, ln1_b, ln2_g, ln2_b, fc1_w, fc1_b, fc2_w, fc2_b, r_ln_g, r_ln_b, r_in_w, r_in_b, r_o1_w, r_o1_b, r_o2_w, r_o2_b, r_o3_w, r_o3_b, lra_down, lra_up):
            B, N, _ = x.shape
            e = _gelu(_ln(x, r_ln_g, r_ln_b) @ r_in_w.T + r_in_b)
            g = jnp.mean(e[:, RESERVE:, :], axis=1, keepdims=True)
            f = jnp.concatenate([e, jnp.broadcast_to(g, e.shape)], axis=-1)
            h1 = _gelu(f @ r_o1_w.T + r_o1_b)
            h2 = _gelu(h1 @ r_o2_w.T + r_o2_b)
            logits = (h2 @ r_o3_w.T + r_o3_b).reshape(B, N, BS, 2)
            hard = jax.nn.one_hot(jnp.argmax(logits, axis=-1), 2, dtype=x.dtype)
            keep = jnp.broadcast_to(jnp.array([0.0, 1.0], dtype=x.dtype), hard[:, :RESERVE].shape)
            hard = hard.at[:, :RESERVE].set(keep)
            hard = jax.lax.stop_gradient(hard)
            bits = hard[..., 1]
            indices = (bits * jnp.array([2.0, 1.0], dtype=x.dtype)).sum(-1).astype(jnp.int32)
            indices = jax.lax.stop_gradient(indices)
            xa = _ln(x, ln1_g, ln1_b)
            q = (xa @ wq.T + bq).reshape(B, N, HEADS, HD).transpose(0, 2, 1, 3)
            k = (xa @ wk.T + bk).reshape(B, N, HEADS, HD).transpose(0, 2, 1, 3)
            v = (xa @ wv.T + bv).reshape(B, N, HEADS, HD).transpose(0, 2, 1, 3)
            s = jax.nn.softmax(jnp.einsum('bhqd,bhkd->bhqk', q, k) / np.float32(np.sqrt(HD)), axis=-1)
            o = jnp.einsum('bhqk,bhkd->bhqd', s, v).transpose(0, 2, 1, 3).reshape(B, N, DIM)
            o = o @ wo.T + bo
            h = x + bits[:, :, 0:1] * o
            xf = _ln(h, ln2_g, ln2_b)
            ff = _gelu(xf @ fc1_w.T + fc1_b) @ fc2_w.T + fc2_b
            out = h + bits[:, :, 1:2] * ff
            down = jnp.einsum('bnd,krd->bknr', out, lra_down)
            up = jnp.einsum('bknr,kdr->bknd', down, lra_up)
            sel = jax.nn.one_hot(indices, 3, dtype=x.dtype)
            out = out + jnp.einsum('bknd,bnk->bnd', up, sel)
            return out
        return _forward(x, wq, bq, wk, bk, wv, bv, wo, bo, ln1_g, ln1_b, ln2_g, ln2_b, fc1_w, fc1_b, fc2_w, fc2_b, r_ln_g, r_ln_b, r_in_w, r_in_b, r_o1_w, r_o1_b, r_o2_w, r_o2_b, r_o3_w, r_o3_b, lra_down, lra_up)

    def _L2_attn_ref(x, A, W_delta, delta_bias, W_B, W_C):
        import jax, jax.numpy as jnp
        import numpy as np
        Bsz, L, D, N = (2, 512, 192, 16)

        def _forward(x, A, W_delta, delta_bias, W_B, W_C):
            B, Lx, Dx = x.shape
            Nx = A.shape[1]
            delta = jax.nn.softplus(x @ W_delta.T + delta_bias)
            B_sel = (x @ W_B.T).reshape(B, Lx, Dx, Nx)
            C_sel = (x @ W_C.T).reshape(B, Lx, Dx, Nx)
            dA = delta[..., None] * A
            A_bar = jnp.exp(dA)
            B_bar = (A_bar - 1.0) / dA * delta[..., None] * B_sel
            Bx = B_bar * x[..., None]

            def step(h, inp):
                a_t, bx_t, c_t = inp
                h = a_t * h + bx_t
                y_t = jnp.sum(h * c_t, axis=-1)
                return (h, y_t)
            h0 = jnp.zeros((B, Dx, Nx), dtype=x.dtype)
            scan_in = (jnp.moveaxis(A_bar, 1, 0), jnp.moveaxis(Bx, 1, 0), jnp.moveaxis(C_sel, 1, 0))
            _, ys = jax.lax.scan(step, h0, scan_in)
            return jnp.moveaxis(ys, 0, 1)
        return _forward(x, A, W_delta, delta_bias, W_B, W_C)

    def _L2_ffn_ref(hidden_states, Wg, e_bias, W_gate_up, W_down, Wsg, Wsu, Wsd):
        import jax, jax.numpy as jnp
        import numpy as np
        E = 128
        I = 464
        IS = 928
        K = 6
        G = 1
        TG = 1
        SCALE = 2.5
        CAP = 192

        def moe_forward(hidden_states, Wg, e_bias, W_gate_up, W_down, Wsg, Wsu, Wsd):
            B, S, H = hidden_states.shape
            x = hidden_states.reshape(-1, H)
            T = x.shape[0]
            logits = x.astype(jnp.float32) @ Wg.T
            sig = jax.nn.sigmoid(logits)
            choice = sig + e_bias[None, :]
            grp = choice.reshape(T, G, E // G)
            group_scores = jax.lax.top_k(grp, 2)[0].sum(-1)
            gidx = jax.lax.top_k(group_scores, TG)[1]
            gmask = jnp.zeros((T, G), jnp.float32).at[jnp.arange(T)[:, None], gidx].set(1.0)
            smask = jnp.repeat(gmask, E // G, axis=1)
            scores_for_choice = jnp.where(smask > 0, choice, 0.0)
            topk_idx = jax.lax.top_k(scores_for_choice, K)[1]
            topk_w = jnp.take_along_axis(sig, topk_idx, axis=1)
            topk_w = topk_w / (topk_w.sum(-1, keepdims=True) + 1e-20)
            topk_w = topk_w * SCALE
            P = T * K
            flat_e = topk_idx.reshape(-1)
            order = jnp.argsort(flat_e)
            se = flat_e[order]
            counts = jax.ops.segment_sum(jnp.ones(P, jnp.int32), flat_e, num_segments=E)
            starts = jnp.cumsum(counts) - counts
            pos = jnp.arange(P) - starts[se]
            buf_idx = jnp.where(pos < CAP, se * CAP + pos, E * CAP)
            tok_of_pair = (order // K).astype(jnp.int32)
            w_of_pair = topk_w.reshape(-1)[order]
            token_buf = jnp.zeros((E * CAP,), jnp.int32).at[buf_idx].set(tok_of_pair, mode='drop')
            w_buf = jnp.zeros((E * CAP,), x.dtype).at[buf_idx].set(w_of_pair.astype(x.dtype), mode='drop')
            xb = x[token_buf].reshape(E, CAP, H)
            gu = jnp.einsum('ech,ehf->ecf', xb, W_gate_up)
            g, u = jnp.split(gu, 2, axis=-1)
            inter = jax.nn.silu(g) * u
            yb = jnp.einsum('eci,eih->ech', inter, W_down)
            yb = yb * w_buf.reshape(E, CAP, 1)
            routed = jnp.zeros((T, H), x.dtype).at[token_buf].add(yb.reshape(E * CAP, H))
            shared = jax.nn.silu(x @ Wsg) * (x @ Wsu) @ Wsd
            return (routed + shared).reshape(B, S, H)
        return moe_forward(hidden_states, Wg, e_bias, W_gate_up, W_down, Wsg, Wsu, Wsd)

    def _L3_attn_ref(hidden_states, W_qkv, b_qkv, W_proj, b_proj):
        import jax, jax.numpy as jnp
        import numpy as np
        B, S, E, H = (8, 256, 192, 12)
        SPARSITY = 0.4
        bsz, tgt_len, embed_dim = hidden_states.shape
        head_dim = embed_dim // H
        scale = head_dim ** (-0.5)
        qkv = (hidden_states @ W_qkv + b_qkv).reshape(bsz, tgt_len, 3, H, head_dim)
        qkv = qkv.transpose(2, 0, 3, 1, 4)
        q, k, v = (qkv[0], qkv[1], qkv[2])
        attn_weights = jnp.einsum('bhqd,bhkd->bhqk', q, k) * scale
        top_k = max(1, int(SPARSITY * tgt_len))
        top_k = min(top_k, tgt_len)
        kth = jax.lax.top_k(attn_weights, top_k)[0][..., -1:]
        min_val = jnp.finfo(attn_weights.dtype).min
        sparse_weights = jnp.where(attn_weights >= kth, attn_weights, min_val)
        attn = jax.nn.softmax(sparse_weights.astype(jnp.float32), axis=-1)
        attn = attn.astype(v.dtype)
        out = jnp.einsum('bhqk,bhkd->bqhd', attn, v).reshape(bsz, tgt_len, embed_dim)
        return out @ W_proj + b_proj

    def _L3_ffn_ref(x, gate_w, gate_b, fc1_w, fc1_b, ln_w, ln_b, fc2_w, fc2_b):
        import jax, jax.numpy as jnp
        import numpy as np
        SEQ, BATCH, EMBED = (256, 2, 192)
        E = 16
        FFN_H = 384
        K_SHARED = 1
        K_ROUTE = 3
        LN_EPS = 1e-05
        NEG_INF = -1000000000.0
        S, B, D = x.shape
        T = S * B
        xf = x.reshape(T, D)
        scores = xf @ gate_w + gate_b
        scores = scores.at[:, :K_SHARED].set(NEG_INF)
        probs = jax.nn.softmax(scores, axis=-1)
        topv, topi = jax.lax.top_k(probs, K_ROUTE)
        combine = jnp.zeros((T, E), xf.dtype)
        combine = combine.at[jnp.arange(T)[:, None], topi].add(topv)
        combine = combine.at[:, :K_SHARED].add(1.0)
        h = jnp.einsum('td,edh->eth', xf, fc1_w) + fc1_b[:, None, :]
        h = jax.nn.gelu(h, approximate=False)
        mu = h.mean(-1, keepdims=True)
        var = h.var(-1, keepdims=True)
        h = (h - mu) * jax.lax.rsqrt(var + LN_EPS) * ln_w[:, None, :] + ln_b[:, None, :]
        y = jnp.einsum('eth,ehd->etd', h, fc2_w) + fc2_b[:, None, :]
        out = jnp.einsum('te,etd->td', combine, y)
        return out.reshape(S, B, D)
    h = _L0_tok_ref(x, L0_tok_W, L0_tok_b)
    h = h + _L0_attn_ref(_layernorm(h, axis=-1), L0_attn_w_qkv, L0_attn_b_qkv, L0_attn_w_proj, L0_attn_b_proj)
    h = h + _L0_ffn_ref(_layernorm(h, axis=-1), L0_ffn_w_gate, L0_ffn_expert_bias, L0_ffn_wg, L0_ffn_wu, L0_ffn_wd, L0_ffn_swg, L0_ffn_swu, L0_ffn_swd)
    h = h + _L1_attn_ref(_layernorm(h, axis=-1), L1_attn_Wq, L1_attn_bq, L1_attn_Wk, L1_attn_bk, L1_attn_Wv, L1_attn_bv)
    h = h + _L1_ffn_ref(_layernorm(h, axis=-1), L1_ffn_wq, L1_ffn_bq, L1_ffn_wk, L1_ffn_bk, L1_ffn_wv, L1_ffn_bv, L1_ffn_wo, L1_ffn_bo, L1_ffn_ln1_g, L1_ffn_ln1_b, L1_ffn_ln2_g, L1_ffn_ln2_b, L1_ffn_fc1_w, L1_ffn_fc1_b, L1_ffn_fc2_w, L1_ffn_fc2_b, L1_ffn_r_ln_g, L1_ffn_r_ln_b, L1_ffn_r_in_w, L1_ffn_r_in_b, L1_ffn_r_o1_w, L1_ffn_r_o1_b, L1_ffn_r_o2_w, L1_ffn_r_o2_b, L1_ffn_r_o3_w, L1_ffn_r_o3_b, L1_ffn_lra_down, L1_ffn_lra_up)
    h = h + _L2_attn_ref(_layernorm(h, axis=-1), L2_attn_A, L2_attn_W_delta, L2_attn_delta_bias, L2_attn_W_B, L2_attn_W_C)
    h = h + _L2_ffn_ref(_layernorm(h, axis=-1), L2_ffn_Wg, L2_ffn_e_bias, L2_ffn_W_gate_up, L2_ffn_W_down, L2_ffn_Wsg, L2_ffn_Wsu, L2_ffn_Wsd)
    h = h + _L3_attn_ref(_layernorm(h, axis=-1), L3_attn_W_qkv, L3_attn_b_qkv, L3_attn_W_proj, L3_attn_b_proj)
    h = h + _L3_ffn_ref(_layernorm(h, axis=-1), L3_ffn_gate_w, L3_ffn_gate_b, L3_ffn_fc1_w, L3_ffn_fc1_b, L3_ffn_ln_w, L3_ffn_ln_b, L3_ffn_fc2_w, L3_ffn_fc2_b)
    return h

_drawn_inputs = setup_inputs


def setup_inputs(seed=0):
    import zlib

    import numpy as np

    out = dict(_drawn_inputs(seed))
    spreads = {'L0_ffn_expert_bias': (0.0, 0.626),
     'L1_ffn_bq': (0.0, 0.8),
     'L1_ffn_bk': (0.0, 2.0),
     'L1_ffn_bv': (0.0, 0.418),
     'L1_ffn_bo': (0.0, 0.1),
     'L1_ffn_ln1_g': (1.0, 0.6),
     'L1_ffn_ln1_b': (0.0, 0.8),
     'L1_ffn_ln2_g': (1.0, 0.6),
     'L1_ffn_ln2_b': (0.0, 0.8),
     'L1_ffn_fc1_b': (0.0, 0.379),
     'L1_ffn_fc2_b': (0.0, 0.1),
     'L1_ffn_r_ln_g': (1.0, 0.2),
     'L1_ffn_r_ln_b': (0.0, 0.1),
     'L1_ffn_r_in_b': (0.0, 0.1),
     'L1_ffn_r_o1_b': (0.0, 0.1),
     'L1_ffn_r_o2_b': (0.0, 0.1),
     'L2_ffn_e_bias': (0.0, 0.697),
     'L3_ffn_gate_b': (0.0, 2.0),
     'L3_ffn_fc1_b': (0.0, 0.38),
     'L3_ffn_ln_w': (1.0, 0.6),
     'L3_ffn_ln_b': (0.0, 0.455),
     'L3_ffn_fc2_b': (0.0, 0.494)}
    factors = {'L0_tok_b': 3.479,
     'L0_ffn_w_gate': 3.902,
     'L0_ffn_wg': 3.545,
     'L0_ffn_wu': 3.543,
     'L0_ffn_wd': 3.543,
     'L1_attn_bq': 3.562,
     'L1_attn_bk': 3.241,
     'L1_attn_bv': 3.22,
     'L1_ffn_wq': 8.0,
     'L1_ffn_wk': 8.0,
     'L1_ffn_wv': 4.544,
     'L1_ffn_wo': 2.712,
     'L2_ffn_Wg': 7.002,
     'L2_ffn_W_gate_up': 6.15,
     'L2_ffn_W_down': 6.257,
     'L2_ffn_Wsg': 4.623,
     'L2_ffn_Wsu': 4.597,
     'L2_ffn_Wsd': 4.621,
     'L3_attn_b_qkv': 14.81,
     'L3_attn_b_proj': 17.987,
     'L3_ffn_gate_w': 5.7}
    for name, (base, spread) in spreads.items():
        noise = np.random.default_rng([zlib.crc32(name.encode()), seed]).standard_normal(out[name].shape)
        drawn = base * np.exp(spread * noise) if base else spread * noise
        out[name] = jnp.asarray(drawn.astype(out[name].dtype))
    for name, factor in factors.items():
        out[name] = (out[name] * factor).astype(out[name].dtype)
    return out
```

```python
from contextlib import ExitStack

import numpy as np

import concourse.bass as bass
from concourse import mybir

F32 = mybir.dt.float32
U32 = mybir.dt.uint32
ALU = mybir.AluOpType
ACT = mybir.ActivationFunctionType
AX = mybir.AxisListType

IMAGES, SEQ, DIM = 16, 36, 192
TOKENS = IMAGES * SEQ
Q = 96
HALF = TOKENS // 2
PATCH_K = 6
PAIR = 2 * SEQ
PAIRS = TOKENS // PAIR
TILE = 96
TILES = TOKENS // TILE
HEADS, HEAD_DIM = 12, 16
KEEP = int(0.4 * SEQ)
STATES = 16
EPS = 1e-5

MOE = {
    "L0": dict(experts=16, top=2, cap=TOKENS, shared=1, width=384, chunks=3),
    "L2": dict(experts=128, top=6, cap=192, shared=2, width=464, chunks=4),
    "L3": dict(experts=16, top=3, cap=TOKENS, shared=1, width=384, chunks=3),
}
for _m in MOE.values():
    _dyn = (TOKENS * _m["top"] + _m["experts"] * (TILE - 1)) // TILE
    _m["blocks"] = (TILES * _m["shared"] + _dyn + 1) // 2 * 2
    _m["rows"] = _m["blocks"] * TILE
MAX_BLOCKS = max(_m["blocks"] for _m in MOE.values())

GROUPS = {
    "const": [("ident", 128, 128), ("ones", 128, 128), ("mean192", Q, Q), ("mean384", 128, 128),
              ("before", 128, 128), ("iota", 128, MAX_BLOCKS), ("ecol", 128, 1), ("levels", 128, TILES),
              ("spare", TILE, TILES * 6), ("apart", PAIR, PAIR), ("same", PAIR, PAIR), ("headmask", Q, 6)],
    "tok": [("tokW", 128, PATCH_K * DIM), ("tokb", Q, 2)],
    "L0a": [("l0qkv", Q, 6 * DIM), ("l0qkvb", Q, 6), ("l0proj", Q, 2 * DIM), ("l0projb", Q, 2),
            ("L0gate", Q, 32), ("L0gateb", TILE, 16)],
    "L1a": [("l1q", Q, 2 * DIM), ("l1k", Q, 2 * DIM), ("l1v", Q, 2 * DIM), ("l1qkb", Q, 4),
            ("l1vb", PAIR, DIM)],
    "L1f": [("mq", Q, 2 * DIM), ("mk", Q, 2 * DIM), ("mv", Q, 2 * DIM), ("mo", Q, 2 * DIM),
            ("mqkvb", Q, 6), ("mob", Q, 2), ("ln1", Q, 4), ("ln2", Q, 4), ("rln", Q, 4),
            ("fc1", Q, 2 * 768), ("fc1b", 128, 6), ("fc2", 128, 6 * DIM), ("fc2b", Q, 2),
            ("rin", Q, 2 * 128), ("rinb", 128, 1), ("ro1", 128, 2 * 128), ("ro1b", 128, 1),
            ("ro2", 128, 64), ("ro2b", 64, 1), ("ro3", 64, 4), ("ro3b", 128, 4),
            ("ldown", Q, 2 * DIM), ("lup01", 128, DIM), ("lup2", 64, DIM)],
    "L2a": [("sD", Q, 2 * DIM), ("sDb", Q, 2), ("L2gate", Q, 256), ("L2gateb", TILE, 128)],
    "L3a": [("aqkv", Q, 6 * DIM), ("aqkvb", Q, 6), ("aproj", Q, 2 * DIM), ("aprojb", Q, 2),
            ("L3gate", Q, 32), ("L3gateb", TILE, 16)],
}
WIDTHS = {g: sum(n for _, _, n in items) for g, items in GROUPS.items()}


class Tower:

    def __init__(self, nc, ctx, dram):
        self.nc, self.dram, self.of_layer = nc, dram, []
        self.h = ctx.enter_context(nc.sbuf_tensor("h", [Q, 2, TOKENS], F32))
        self.xn = ctx.enter_context(nc.sbuf_tensor("xn", [Q, 2, TOKENS], F32))
        self.bank = [ctx.enter_context(nc.psum_tensor(f"bank{i}", [128, 512], F32)) for i in range(8)]
        self.loaded = {g: ctx.enter_context(nc.semaphore(f"loaded_{g}")) for g in GROUPS}
        self.zeroed = ctx.enter_context(nc.semaphore("rows_zeroed"))
        self.p, self.packed = {}, {}
        for g, items in GROUPS.items():
            t = self.packed[g] = ctx.enter_context(nc.sbuf_tensor(f"par_{g}", [128, WIDTHS[g]], F32))
            at = 0
            for name, parts, n in items:
                self.p[name] = t[0:parts, at:at + n]
                at += n
        self.rows = {k: nc.dram_tensor(f"rows_{k}", [m["rows"] + TOKENS * m["top"], DIM], F32, kind="Internal").ap()
                     for k, m in MOE.items()}

    def sem(self, name):
        s = self.nc.alloc_semaphore(name)
        self.of_layer.append(s)
        return s

    def end_layer(self):
        self.nc.clear_and_free_semaphores(self.of_layer)
        self.nc.all_engine_barrier()
        self.of_layer = []


def cols(ap, n):
    return ap.rearrange("p (n m) -> p n m", n=n)


def spread(ap, axis, n):
    a = ap.unsqueeze(axis)
    shape = list(a.shape)
    shape[axis] = n
    return a.broadcast_to(shape)


def chained(eng, sem):
    count = [0]

    def link(ins):
        count[0] += 1
        ins.then_inc(sem, 1)
        eng.wait_ge(sem, count[0])

    return link


def load_all(T):
    nc = T.nc
    with ExitStack() as ctx:
        zero = ctx.enter_context(nc.sbuf_tensor("zero", [TILE, 12 * DIM], F32))
        wtok = ctx.enter_context(nc.sbuf_tensor("patches", [128, PATCH_K, TOKENS], F32))
        patches_in = T.sem("patches_in")
        zero_ready = T.sem("zero_ready")
        products = T.sem("tok_products")
        block = ctx.enter_context(nc.Block())
        W = cols(T.p["tokW"], PATCH_K)
        zeros = sum(-(-m["blocks"] // 12) for m in MOE.values())

        @block.sync
        def _(sp):
            sp.dma_start(T.packed["tok"][:, :], T.dram["tok"]).then_inc(T.loaded["tok"], 16)
            sp.dma_start(wtok[:, 0:3, :], T.dram["patches"][:, 0:3, :]).then_inc(patches_in, 16)
            sp.dma_start(wtok[:, 3:6, :], T.dram["patches"][:, 3:6, :]).then_inc(patches_in, 16)
            for g in GROUPS:
                if g != "tok":
                    sp.dma_start(T.packed[g][:, :], T.dram[g]).then_inc(T.loaded[g], 16)
            sp.wait_ge(zero_ready, 1)
            for k, m in MOE.items():
                for r in range(0, m["blocks"], 12):
                    n = min(12, m["blocks"] - r)
                    sp.dma_start(T.rows[k][TILE * r:TILE * (r + n), :].rearrange("(p a) d -> p (a d)", p=TILE),
                                 zero[:, 0:n * DIM]).then_inc(T.zeroed, 16)
            sp.wait_ge(T.zeroed, 16 * zeros)
            for g in GROUPS:
                sp.wait_ge(T.loaded[g], 16)

        @block.vector
        def _(dve):
            dve.memset(zero[:, :], 0.0).then_inc(zero_ready, 1)

        @block.tensor
        def _(pe):
            pe.wait_ge(T.loaded["tok"], 16)
            pe.wait_ge(patches_in, 32)
            for u in range(4):
                m, s = u // 2, HALF * (u % 2)
                for k in range(PATCH_K):
                    mm = pe.matmul(T.bank[u][0:Q, 0:HALF], W[:, k, Q * m:Q * m + Q], wtok[:, k, s:s + HALF],
                                   start=(k == 0), stop=(k == PATCH_K - 1))
                mm.then_inc(products, 1)

        @block.scalar
        def _(act):
            for u in range(4):
                m, s = u // 2, HALF * (u % 2)
                act.wait_ge(products, u + 1)
                act.activation(T.h[:, m, s:s + HALF], T.bank[u][0:Q, 0:HALF], ACT.Identity,
                               bias=T.p["tokb"][:, m:m + 1])


def layer_norm(T, name, x, out):
    nc = T.nc
    with ExitStack() as ctx:
        xc = ctx.enter_context(nc.sbuf_tensor(f"{name}_xc", [Q, 2, TOKENS], F32))
        sq = ctx.enter_context(nc.sbuf_tensor(f"{name}_sq", [Q, 2, TOKENS], F32))
        sd = ctx.enter_context(nc.sbuf_tensor(f"{name}_sd", [Q, 2, HALF], F32))
        eps = ctx.enter_context(nc.sbuf_tensor(f"{name}_eps", [Q, 1], F32))
        eps_set = T.sem(f"{name}_eps_set")
        means = T.sem(f"{name}_means")
        centred = T.sem(f"{name}_centred")
        squared = T.sem(f"{name}_squared")
        variances = T.sem(f"{name}_variances")
        deviations = T.sem(f"{name}_deviations")
        inverted = T.sem(f"{name}_inverted")
        block = ctx.enter_context(nc.Block())

        @block.tensor
        def _(pe):
            for s in range(2):
                for c in range(2):
                    mm = pe.matmul(T.bank[s][0:Q, 0:HALF], T.p["mean192"], x[:, c, HALF * s:HALF * s + HALF],
                                   start=(c == 0), stop=(c == 1))
                mm.then_inc(means, 1)
            for s in range(2):
                pe.wait_ge(squared, s + 1)
                for c in range(2):
                    mm = pe.matmul(T.bank[2 + s][0:Q, 0:HALF], T.p["mean192"], sq[:, c, HALF * s:HALF * s + HALF],
                                   start=(c == 0), stop=(c == 1))
                mm.then_inc(variances, 1)

        @block.vector
        def _(dve):
            dve.memset(eps[:, :], EPS).then_inc(eps_set, 1)
            for s in range(2):
                at = slice(HALF * s, HALF * s + HALF)
                dve.wait_ge(means, s + 1)
                dve.tensor_tensor(xc[:, :, at], x[:, :, at], spread(T.bank[s][0:Q, 0:HALF], 1, 2), ALU.subtract)\
                    .then_inc(centred, 1)
            for s in range(2):
                at = slice(HALF * s, HALF * s + HALF)
                dve.wait_ge(deviations, s + 1)
                dve.reciprocal(sd[:, s, :], sd[:, s, :]).then_inc(inverted, 1)
                dve.wait_ge(inverted, s + 1)
                dve.tensor_tensor(out[:, :, at], xc[:, :, at], spread(sd[:, s, :], 1, 2), ALU.mult)

        @block.scalar
        def _(act):
            for s in range(2):
                at = slice(HALF * s, HALF * s + HALF)
                act.wait_ge(centred, s + 1)
                act.activation(sq[:, :, at], xc[:, :, at], ACT.Square).then_inc(squared, 1)
            act.wait_ge(eps_set, 1)
            for s in range(2):
                act.wait_ge(variances, s + 1)
                act.activation(sd[:, s, :], T.bank[2 + s][0:Q, 0:HALF], ACT.Sqrt, bias=eps[:, 0:1])\
                    .then_inc(deviations, 1)


def linear(T, name, outs, terms, lhsT, rhs, by_act=None, by_dve=None, size=Q):
    nc = T.nc
    units = [(m, slice(HALF * s, HALF * s + HALF)) for m in range(outs) for s in range(2)]
    on_act = [by_dve is None or (by_act is not None and u % 2 == 0) for u in range(len(units))]
    with ExitStack() as ctx:
        products = T.sem(f"{name}_products")
        act_took = T.sem(f"{name}_act_took")
        dve_took = T.sem(f"{name}_dve_took")
        block = ctx.enter_context(nc.Block())

        @block.tensor
        def _(pe):
            for u, (m, at) in enumerate(units):
                if u >= 8:
                    if on_act[u - 8]:
                        pe.wait_ge(act_took, sum(on_act[:u - 7]))
                    else:
                        pe.wait_ge(dve_took, u - 7 - sum(on_act[:u - 7]))
                for k in range(terms):
                    mm = pe.matmul(T.bank[u % 8][0:size, 0:HALF], lhsT(m, k), rhs(k, at),
                                   start=(k == 0), stop=(k == terms - 1))
                mm.then_inc(products, 1)

        @block.scalar
        def _(act):
            for u, (m, at) in enumerate(units):
                if on_act[u]:
                    act.wait_ge(products, u + 1)
                    by_act(m, at, T.bank[u % 8][0:size, 0:HALF]).then_inc(act_took, 1)

        @block.vector
        def _(dve):
            for u, (m, at) in enumerate(units):
                if not on_act[u]:
                    dve.wait_ge(products, u + 1)
                    by_dve(m, at, T.bank[u % 8][0:size, 0:HALF]).then_inc(dve_took, 1)


def values_by_token(T, name, x, w, v, group, bias=None):
    nc = T.nc
    units = TOKENS // group // 2
    with ExitStack() as ctx:
        products = T.sem(f"{name}_products")
        taken = T.sem(f"{name}_taken")
        block = ctx.enter_context(nc.Block())

        @block.tensor
        def _(pe):
            for u in range(units):
                if u >= 8:
                    pe.wait_ge(taken, u - 7)
                for j in range(2):
                    at = group * (2 * u + j)
                    for c in range(2):
                        mm = pe.matmul(T.bank[u % 8][0:group, DIM * j:DIM * j + DIM], x[:, c, at:at + group], w[:, c, :],
                                       start=(c == 0), stop=(c == 1))
                mm.then_inc(products, 1)

        @block.vector
        def _(dve):
            for u in range(units):
                dve.wait_ge(products, u + 1)
                got = cols(T.bank[u % 8][0:group, 0:2 * DIM], 2)
                if bias is None:
                    dve.tensor_copy(v[:, 2 * u:2 * u + 2, :], got).then_inc(taken, 1)
                else:
                    dve.tensor_tensor(v[:, 2 * u:2 * u + 2, :], got, spread(bias, 1, 2), ALU.add).then_inc(taken, 1)


def wide_attention(T, name, qk, v, softmax_scale, linear_scale, take):
    nc = T.nc
    per = PAIRS // 2
    with ExitStack() as ctx:
        sm = ctx.enter_context(nc.sbuf_tensor(f"{name}_sm", [PAIR, PAIRS, PAIR], F32))
        probs_t = ctx.enter_context(nc.sbuf_tensor(f"{name}_pt", [PAIR, PAIRS, PAIR], F32))
        mx = ctx.enter_context(nc.sbuf_tensor(f"{name}_mx", [PAIR, PAIRS], F32))
        total = ctx.enter_context(nc.sbuf_tensor(f"{name}_total", [PAIR, PAIRS], F32))
        sem = lambda what: T.sem(f"{name}_{what}")
        scored, lowered, exps, probs, turned, turned_in, summed = map(
            sem, ("scored", "lowered", "exps", "probs", "turned", "turned_in", "summed"))
        step = sem("dve_step")
        block = ctx.enter_context(nc.Block())

        @block.tensor
        def _(pe):
            for g in range(2):
                for j in range(per):
                    at = slice(PAIR * (per * g + j), PAIR * (per * g + j) + PAIR)
                    a, b = (0, 2) if softmax_scale else (2, 0)
                    for c in range(2):
                        mm = pe.matmul(T.bank[g][0:PAIR, PAIR * j:PAIR * j + PAIR], qk[:, a + c, at], qk[:, b + c, at],
                                       start=(c == 0), stop=(c == 1))
                mm.then_inc(scored, 1)
            if softmax_scale:
                for g in range(2):
                    pe.wait_ge(probs, g + 1)
                    for j in range(per):
                        mm = pe.transpose(T.bank[2 + g][0:PAIR, PAIR * j:PAIR * j + PAIR], sm[:, per * g + j, :],
                                          T.p["ident"][0:PAIR, 0:PAIR])
                    mm.then_inc(turned, 1)
            for g in range(2):
                pe.wait_ge(turned_in, g + 1)
                for m in range(2):
                    for j in range(per):
                        i = per * g + j
                        mm = pe.matmul(T.bank[4 + 2 * g + m][0:Q, PAIR * j:PAIR * j + PAIR],
                                       v[:, i, Q * m:Q * m + Q], probs_t[:, i, :], start=True, stop=True)
                    mm.then_inc(summed, 1)

        @block.vector
        def _(dve):
            link = chained(dve, step)
            for g in range(2):
                dve.wait_ge(scored, g + 1)
                got = cols(T.bank[g][0:PAIR, 0:PAIR * per], per)
                part = sm[:, per * g:per * g + per, :]
                top = mx[:, per * g:per * g + per]
                if softmax_scale:
                    link(dve.tensor_tensor(part, got, spread(T.p["apart"], 1, per), ALU.add))
                    link(dve.tensor_reduce(top, part, AX.X, ALU.max))
                    dve.tensor_tensor(part, part, spread(top, 2, PAIR), ALU.subtract).then_inc(lowered, 1)
                else:
                    dve.scalar_tensor_tensor(probs_t[:, per * g:per * g + per, :], got, linear_scale,
                                             spread(T.p["same"], 1, per), ALU.mult, ALU.mult).then_inc(turned_in, 1)
            if softmax_scale:
                for g in range(2):
                    part = sm[:, per * g:per * g + per, :]
                    tot = total[:, per * g:per * g + per]
                    dve.wait_ge(exps, g + 1)
                    link(dve.tensor_reduce(tot, part, AX.X, ALU.add))
                    link(dve.reciprocal(tot, tot))
                    dve.tensor_tensor(part, part, spread(tot, 2, PAIR), ALU.mult).then_inc(probs, 1)
            for g in range(2):
                for m in range(2):
                    dve.wait_ge(summed, 2 * g + m + 1)
                    take(m, slice(HALF * g, HALF * g + HALF), T.bank[4 + 2 * g + m][0:Q, 0:HALF])

        @block.scalar
        def _(act):
            if softmax_scale:
                for g in range(2):
                    part = sm[:, per * g:per * g + per, :]
                    act.wait_ge(lowered, g + 1)
                    act.activation(part, part, ACT.Exp, scale=softmax_scale).then_inc(exps, 1)
                for g in range(2):
                    act.wait_ge(turned, g + 1)
                    act.copy(probs_t[:, per * g:per * g + per, :], cols(T.bank[2 + g][0:PAIR, 0:PAIR * per], per))\
                        .then_inc(turned_in, 1)


def head_attention(T, name, qk, v, vb, att, sparse):
    nc = T.nc
    H6, ROWS, GROUPS4 = 6, 3 * SEQ, 4
    NG = IMAGES * GROUPS4
    CH = NG // 2
    with ExitStack() as ctx:
        def sb(what, shape, dt=F32):
            return ctx.enter_context(nc.sbuf_tensor(f"{name}_{what}", shape, dt))

        sem = lambda what: T.sem(f"{name}_{what}")
        wide = sb("wide", [Q, 2, IMAGES, H6, SEQ])
        sc = sb("sc", [ROWS, NG, SEQ])
        kept = sb("kept", [ROWS, NG, SEQ])
        top8 = sb("top8", [ROWS, NG, 8])
        next8 = sb("next8", [ROWS, NG, 8])
        mx = sb("mx", [ROWS, NG])
        total = sb("total", [ROWS, NG])
        pt = sb("pt", [SEQ, IMAGES, HEADS * SEQ])
        spread_q, scored, sc_in, lowered, exps, probs, turned, pt_act, pt_dve, pv, pv_out, mixed, step = map(
            sem, ("spread_q", "scored", "sc_in", "lowered", "exps", "probs", "turned", "pt_act", "pt_dve", "pv",
                  "pv_out", "mixed", "dve_step"))
        block = ctx.enter_context(nc.Block())

        @block.tensor
        def _(pe):
            pe.wait_ge(spread_q, 2 * H6)
            for u in range(IMAGES // 2):
                for j in range(2):
                    b = 2 * u + j
                    for g in range(GROUPS4):
                        c, h = g // 2, 3 * (g % 2)
                        col = (j * GROUPS4 + g) * SEQ
                        mm = pe.matmul(T.bank[u][0:ROWS, col:col + SEQ], wide[:, c, b, h:h + 3, :].rearrange("p h q -> p (h q)"),
                                       qk[:, 2 + c, SEQ * b:SEQ * b + SEQ], start=True, stop=True)
                mm.then_inc(scored, 1)

            def turn(b):
                pe.wait_ge(probs, b // (IMAGES // 2) + 1)
                if b < 4:
                    pe.wait_ge(sc_in, 2 * 4)
                else:
                    pe.wait_ge(pt_act if b % 2 == 0 else pt_dve, (b - 4) // 2 + 1)
                for g in range(GROUPS4):
                    mm = pe.transpose(T.bank[b % 4][0:SEQ, ROWS * g:ROWS * g + ROWS], sc[:, GROUPS4 * b + g, :],
                                      T.p["ident"][0:ROWS, 0:ROWS])
                mm.then_inc(turned, 1)

            def apply(b):
                pe.wait_ge(pt_act if b % 2 == 0 else pt_dve, b // 2 + 1)
                if b >= 4:
                    pe.wait_ge(pv_out, b - 3)
                for c in range(2):
                    n = H6 * SEQ
                    mm = pe.matmul(T.bank[4 + b % 4][0:Q, n * c:n * c + n], v[:, b, Q * c:Q * c + Q],
                                   pt[:, b, n * c:n * c + n], start=True, stop=True)
                mm.then_inc(pv, 1)

            for b in range(IMAGES + 2):
                if b < IMAGES:
                    turn(b)
                if b >= 2:
                    apply(b - 2)

        @block.scalar
        def _(act):
            for c in range(2):
                for h in range(0, H6, 2):
                    act.activation(wide[:, c, :, h, :], cols(qk[:, c, :], IMAGES), ACT.Copy, scale=T.p["headmask"][:, h:h + 1])\
                        .then_inc(spread_q, 1)
            for u in range(IMAGES // 2):
                act.wait_ge(scored, u + 1)
                act.mul(sc[:, 8 * u:8 * u + 8, :], cols(T.bank[u][0:ROWS, 0:8 * SEQ], 8), HEAD_DIM ** -0.5)\
                    .then_inc(sc_in, 1)
            for g in range(2):
                act.wait_ge(lowered, g + 1)
                part = sc[:, CH * g:CH * g + CH, :]
                act.activation(part, part, ACT.Exp).then_inc(exps, 1)
            for b in range(0, IMAGES, 2):
                act.wait_ge(turned, b + 1)
                act.copy(pt[:, b, :], T.bank[b % 4][0:SEQ, 0:HEADS * SEQ]).then_inc(pt_act, 1)
            for c in range(2):
                act.wait_ge(mixed, c + 1)
                act.activation(att[:, c, :], att[:, c, :], ACT.Identity, bias=vb[:, c:c + 1])

        @block.vector
        def _(dve):
            for c in range(2):
                for h in range(1, H6, 2):
                    dve.tensor_scalar(wide[:, c, :, h, :], cols(qk[:, c, :], IMAGES), T.p["headmask"][:, h:h + 1], None, ALU.mult)\
                        .then_inc(spread_q, 1)
            link = chained(dve, step)
            for g in range(2):
                dve.wait_ge(sc_in, IMAGES // 4 * (g + 1))
                part = sc[:, CH * g:CH * g + CH, :]
                top = mx[:, CH * g:CH * g + CH]
                if sparse:
                    n = range(CH * g, CH * g + CH)
                    for i in n:
                        ins = dve.max(top8[:, i, :], sc[:, i, :])
                    link(ins)
                    for i in n:
                        ins = dve.match_replace(kept[:, i, :], top8[:, i, :], sc[:, i, :], -3.0e38)
                    link(ins)
                    for i in n:
                        ins = dve.max(next8[:, i, :], kept[:, i, :])
                    link(ins)
                    link(dve.tensor_copy(top, top8[:, CH * g:CH * g + CH, 0]))
                    link(dve.tensor_tensor(kept[:, CH * g:CH * g + CH, :], part,
                                           next8[:, CH * g:CH * g + CH, KEEP - 9:KEEP - 8].broadcast_to([ROWS, CH, SEQ]),
                                           ALU.is_ge))
                else:
                    link(dve.tensor_reduce(top, part, AX.X, ALU.max))
                dve.tensor_tensor(part, part, spread(top, 2, SEQ), ALU.subtract).then_inc(lowered, 1)
            for g in range(2):
                dve.wait_ge(exps, g + 1)
                part = sc[:, CH * g:CH * g + CH, :]
                tot = total[:, CH * g:CH * g + CH]
                if sparse:
                    link(dve.tensor_tensor(part, part, kept[:, CH * g:CH * g + CH, :], ALU.mult))
                link(dve.tensor_reduce(tot, part, AX.X, ALU.add))
                link(dve.reciprocal(tot, tot))
                dve.tensor_tensor(part, part, spread(tot, 2, SEQ), ALU.mult).then_inc(probs, 1)

            def own_heads(b):
                dve.wait_ge(pv, b + 1)
                got = T.bank[4 + b % 4][0:Q, 0:HEADS * SEQ].rearrange("p (c h q) -> p c h q", c=2, h=H6)
                mask = T.p["headmask"].unsqueeze(1).unsqueeze(3).broadcast_to([Q, 2, H6, SEQ])
                return dve.tensor_tensor(wide[:, :, b, :, :], got, mask, ALU.mult).then_inc(pv_out, 1)

            for b in range(1, IMAGES, 2):
                dve.wait_ge(turned, b + 1)
                dve.tensor_copy(pt[:, b, :], T.bank[b % 4][0:SEQ, 0:HEADS * SEQ]).then_inc(pt_dve, 1)
                if b >= 3:
                    own_heads(b - 3)
                    own_heads(b - 2)
            own_heads(IMAGES - 2)
            own_heads(IMAGES - 1)
            dve.wait_ge(pv_out, IMAGES)
            for c in range(2):
                dve.tensor_reduce(att[:, c, :].rearrange("p (b q) -> p b q", b=IMAGES),
                                  wide[:, c, :, :, :].rearrange("p b h q -> p b q h"), AX.X, ALU.add)\
                    .then_inc(mixed, 1)


def affine(T, name, jobs):
    nc = T.nc
    with nc.Block() as block:

        @block.vector
        def _(dve):
            for out, x, gb in jobs:
                for c in range(2):
                    dve.tensor_scalar(out[:, c, :], x[:, c, :], gb[:, c:c + 1], gb[:, 2 + c:3 + c], ALU.mult, ALU.add)


def residual(T, out, bias):
    def take(m, at, psum):
        return T.nc.vector.scalar_tensor_tensor(out[:, m, at], psum, bias[:, m:m + 1], out[:, m, at], ALU.add, ALU.add)
    return take


def biased(T, out, bias, func=ACT.Identity):
    def take(m, at, psum):
        return T.nc.scalar.activation(out[:, m, at], psum, func, bias=bias[:, m:m + 1])
    return take


def layer0_attention(T):
    nc, p = T.nc, T.p
    with ExitStack() as ctx:
        qk = ctx.enter_context(nc.sbuf_tensor("a0_qk", [Q, 4, TOKENS], F32))
        v = ctx.enter_context(nc.sbuf_tensor("a0_v", [PAIR, PAIRS, DIM], F32))
        att = ctx.enter_context(nc.sbuf_tensor("a0_att", [Q, 2, TOKENS], F32))
        w = cols(p["l0qkv"], 2)
        linear(T, "a0_qk_proj", 4, 2, lambda m, k: w[:, k, Q * m:Q * m + Q], lambda k, at: T.xn[:, k, at],
               by_act=biased(T, qk, p["l0qkvb"]))
        values_by_token(T, "a0_vals", T.xn, w[:, :, 2 * DIM:3 * DIM], v, PAIR)
        wide_attention(T, "a0_att", qk, v, DIM ** -0.5 / 3.0, None,
                       lambda m, at, psum: nc.vector.tensor_scalar(att[:, m, at], psum, p["l0qkvb"][:, 4 + m:5 + m],
                                                                   None, ALU.add))
        w2 = cols(p["l0proj"], 2)
        linear(T, "a0_proj", 2, 2, lambda m, k: w2[:, k, Q * m:Q * m + Q], lambda k, at: att[:, k, at],
               by_dve=residual(T, T.h, p["l0projb"]))


def layer1_attention(T):
    nc, p = T.nc, T.p
    with ExitStack() as ctx:
        qk = ctx.enter_context(nc.sbuf_tensor("a1_qk", [Q, 4, TOKENS], F32))
        v = ctx.enter_context(nc.sbuf_tensor("a1_v", [PAIR, PAIRS, DIM], F32))
        w = [cols(p["l1q"], 2), cols(p["l1k"], 2)]
        linear(T, "a1_qk_proj", 4, 2, lambda m, k: w[m // 2][:, k, Q * (m % 2):Q * (m % 2) + Q],
               lambda k, at: T.xn[:, k, at], by_act=biased(T, qk, p["l1qkb"]))
        values_by_token(T, "a1_vals", T.xn, cols(p["l1v"], 2), v, PAIR, bias=p["l1vb"])
        wide_attention(T, "a1_att", qk, v, None, DIM ** -0.5,
                       lambda m, at, psum: nc.vector.tensor_tensor(T.h[:, m, at], T.h[:, m, at], psum, ALU.add))


def layer1_block(T):
    nc, p = T.nc, T.p
    with ExitStack() as outer:
        x = T.xn
        res = outer.enter_context(nc.sbuf_tensor("b1_res", [Q, 2, TOKENS], F32))
        y = outer.enter_context(nc.sbuf_tensor("b1_y", [Q, 2, TOKENS], F32))
        bits = outer.enter_context(nc.sbuf_tensor("b1_bits", [128, 2, TOKENS], F32))
        layer_norm(T, "b1_ln", x, y)
        with ExitStack() as ctx:
            def sb(what, shape):
                return ctx.enter_context(nc.sbuf_tensor(f"b1_{what}", shape, F32))
            yr = sb("yr", [Q, 2, TOKENS])
            e = sb("e", [128, 1, TOKENS])
            g = sb("g", [128, IMAGES])
            gb = sb("gb", [128, 1, TOKENS])
            h1 = sb("h1", [128, 1, TOKENS])
            h2 = sb("h2", [64, 1, TOKENS])
            lg = sb("lg", [128, 4, TOKENS])
            affine(T, "b1_rln", [(yr, y, p["rln"])])
            win = cols(p["rin"], 2)
            linear(T, "b1_rin", 1, 2, lambda m, k: win[:, k, :], lambda k, at: yr[:, k, at],
                   by_act=biased(T, e, p["rinb"], ACT.Gelu), size=128)
            summed = T.sem("b1_summed")
            with nc.Block() as block:

                @block.vector
                def _(dve):
                    ev = e[:, 0, :].rearrange("p (b t) -> p b t", b=IMAGES)
                    dve.tensor_reduce(g[:, :], ev[:, :, 1:SEQ], AX.X, ALU.add).then_inc(summed, 1)
                    dve.wait_ge(summed, 1)
                    dve.tensor_scalar(gb[:, 0, :].rearrange("p (b t) -> p b t", b=IMAGES), spread(g[:, :], 2, SEQ),
                                      1.0 / (SEQ - 1), None, ALU.mult)
            wo1 = cols(p["ro1"], 2)
            linear(T, "b1_ro1", 1, 2, lambda m, k: wo1[:, k, :], lambda k, at: (e if k == 0 else gb)[:, 0, at],
                   by_act=biased(T, h1, p["ro1b"], ACT.Gelu), size=128)
            linear(T, "b1_ro2", 1, 1, lambda m, k: p["ro2"], lambda k, at: h1[:, 0, at],
                   by_act=biased(T, h2, p["ro2b"], ACT.Gelu), size=64)
            linear(T, "b1_ro3", 4, 1, lambda m, k: p["ro3"][:, m:m + 1].broadcast_to([64, 128]),
                   lambda k, at: h2[:, 0, at], by_act=biased(T, lg, p["ro3b"]), size=128)
            chosen = T.sem("b1_chosen")
            with nc.Block() as block:

                @block.vector
                def _(dve):
                    for b in range(2):
                        dve.tensor_tensor(bits[:, b, :], lg[:, 2 * b + 1, :], lg[:, 2 * b, :], ALU.is_gt)\
                            .then_inc(chosen, 1)
                    dve.wait_ge(chosen, 2)
                    for b in range(2):
                        dve.memset(bits[:, b, :].rearrange("p (b t) -> p b t", b=IMAGES)[:, :, 0:1], 1.0)
        with ExitStack() as ctx:
            def sb(what, shape):
                return ctx.enter_context(nc.sbuf_tensor(f"b1_{what}", shape, F32))
            xa = sb("xa", [Q, 2, TOKENS])
            qk = sb("qk", [Q, 4, TOKENS])
            v = sb("v", [SEQ, IMAGES, DIM])
            att = sb("att", [Q, 2, TOKENS])
            affine(T, "b1_ln1", [(xa, y, p["ln1"])])
            w = [cols(p["mq"], 2), cols(p["mk"], 2)]
            linear(T, "b1_qk", 4, 2, lambda m, k: w[m // 2][:, k, Q * (m % 2):Q * (m % 2) + Q],
                   lambda k, at: xa[:, k, at], by_act=biased(T, qk, p["mqkvb"]))
            values_by_token(T, "b1_vals", xa, cols(p["mv"], 2), v, SEQ)
            head_attention(T, "b1_att", qk, v, p["mqkvb"][:, 4:6], att, False)
            wo = cols(p["mo"], 2)
            linear(T, "b1_wo", 2, 2, lambda m, k: wo[:, k, Q * m:Q * m + Q], lambda k, at: att[:, k, at],
                   by_dve=lambda m, at, psum: nc.vector.scalar_tensor_tensor(
                       res[:, m, at], psum, p["mob"][:, m:m + 1], bits[0:Q, 0, at], ALU.add, ALU.mult))
        add_into(T, res, x)
        with ExitStack() as ctx:
            def sb(what, shape):
                return ctx.enter_context(nc.sbuf_tensor(f"b1_{what}", shape, F32))
            xf = sb("xf", [Q, 2, TOKENS])
            mid = sb("mid", [128, 6, TOKENS])
            ff = sb("ff", [Q, 2, TOKENS])
            layer_norm(T, "b1_lnf", res, y)
            affine(T, "b1_ln2", [(xf, y, p["ln2"])])
            w1, w2 = cols(p["fc1"], 2), cols(p["fc2"], 6)
            linear(T, "b1_fc1", 6, 2, lambda m, k: w1[:, k, 128 * m:128 * m + 128], lambda k, at: xf[:, k, at],
                   by_act=biased(T, mid, p["fc1b"], ACT.Gelu), size=128)
            linear(T, "b1_fc2", 2, 6, lambda m, k: w2[:, k, Q * m:Q * m + Q], lambda k, at: mid[:, k, at],
                   by_dve=lambda m, at, psum: nc.vector.scalar_tensor_tensor(
                       ff[:, m, at], psum, p["fc2b"][:, m:m + 1], bits[0:Q, 1, at], ALU.add, ALU.mult))
            add_into(T, res, ff)
        with ExitStack() as ctx:
            def sb(what, shape):
                return ctx.enter_context(nc.sbuf_tensor(f"b1_{what}", shape, F32))
            sel = sb("sel", [128, 2, TOKENS])
            inv = sb("inv", [128, 2, TOKENS])
            d01 = sb("d01", [128, TOKENS])
            d2 = sb("d2", [64, TOKENS])
            step = T.sem("b1_sel_step")
            with nc.Block() as block:

                @block.vector
                def _(dve):
                    link = chained(dve, step)
                    link(dve.tensor_scalar(inv[:, :, :], bits[:, :, :], -1.0, 1.0, ALU.mult, ALU.add))
                    dve.tensor_tensor(sel[0:64, 0, :], inv[0:64, 0, :], inv[0:64, 1, :], ALU.mult)
                    dve.tensor_tensor(sel[64:128, 0, :], inv[64:128, 0, :], bits[64:128, 1, :], ALU.mult)
                    dve.tensor_tensor(sel[0:64, 1, :], bits[0:64, 0, :], inv[0:64, 1, :], ALU.mult)
            down = cols(p["ldown"], 2)
            linear(T, "b1_down01", 1, 2, lambda m, k: down[:, k, 0:128], lambda k, at: res[:, k, at],
                   by_dve=lambda m, at, psum: nc.vector.tensor_tensor(d01[:, at], psum, sel[:, 0, at], ALU.mult),
                   size=128)
            linear(T, "b1_down2", 1, 2, lambda m, k: down[:, k, 128:192], lambda k, at: res[:, k, at],
                   by_dve=lambda m, at, psum: nc.vector.tensor_tensor(d2[:, at], psum, sel[0:64, 1, at], ALU.mult),
                   size=64)
            linear(T, "b1_up", 2, 2, lambda m, k: (p["lup01"] if k == 0 else p["lup2"])[:, Q * m:Q * m + Q],
                   lambda k, at: (d01 if k == 0 else d2)[:, at],
                   by_dve=lambda m, at, psum: nc.vector.tensor_tensor(res[:, m, at], res[:, m, at], psum, ALU.add))
            add_into(T, T.h, res)


def add_into(T, out, x):
    with T.nc.Block() as block:

        @block.vector
        def _(dve):
            dve.tensor_tensor(out[:, :, :], out[:, :, :], x[:, :, :], ALU.add)


def selective_scan(T):
    nc, p = T.nc, T.p
    FLAT = 2 * TOKENS
    with ExitStack() as ctx:
        def sb(what, shape):
            return ctx.enter_context(nc.sbuf_tensor(f"ssm_{what}", shape, F32))

        sem = lambda what: T.sem(f"ssm_{what}")
        pre, mag, delta = sb("pre", [Q, 2, TOKENS]), sb("mag", [Q, 2, TOKENS]), sb("delta", [Q, 2, TOKENS])
        inv_a = [sb(f"inv_a{i}", [Q, 2]) for i in range(2)]
        yacc = sb("y", [Q, FLAT])
        wbc = [sb(f"wbc{i}", [Q, 4 * DIM + 2]) for i in range(2)]
        decay = [sb(f"decay{i}", [Q, FLAT]) for i in range(2)]
        bsel = [sb(f"bsel{i}", [Q, FLAT]) for i in range(2)]
        drive = [sb(f"drive{i}", [Q, FLAT]) for i in range(2)]
        bx = [sb(f"bx{i}", [Q, FLAT]) for i in range(2)]
        state = [sb(f"state{i}", [Q, FLAT]) for i in range(2)]
        out = [sb(f"out{i}", [Q, FLAT]) for i in range(2)]
        wd = cols(p["sD"], 2)
        linear(T, "ssm_delta", 2, 2, lambda m, k: wd[:, k, Q * m:Q * m + Q], lambda k, at: T.xn[:, k, at],
               by_act=biased(T, pre, p["sDb"]))
        soft = sem("soft")
        with nc.Block() as block:

            @block.scalar
            def _(act):
                link = chained(act, soft)
                link(act.activation(mag[:, :, :], pre[:, :, :], ACT.Abs))
                link(act.activation(mag[:, :, :], mag[:, :, :], ACT.Exp, scale=-1.0))
                link(act.activation(mag[:, :, :], mag[:, :, :], ACT.Ln, bias=1.0))

            @block.vector
            def _(dve):
                dve.memset(yacc[:, :], 0.0)
                dve.wait_ge(soft, 3)
                dve.scalar_tensor_tensor(delta[:, :, :], pre[:, :, :], 0.0, mag[:, :, :], ALU.max, ALU.add)
        loaded = [sem(f"loaded{i}") for i in range(2)]
        inverted, b_made, c_made, decayed, b_out, driven, bx_made, scanned, read_out, added, reset = map(
            sem, ("inverted", "b_made", "c_made", "decayed", "b_out", "driven", "bx_made", "scanned", "read_out", "added", "reset"))
        block = ctx.enter_context(nc.Block())

        @block.sync
        def _(sp):
            sp.sem_inc(c_made, 8)
            sp.sem_inc(b_out, 8)
            sp.wait_ge(b_out, 8)
            with sp.Fori(0, STATES // 2) as i:
                for j in range(2):
                    sp.wait_ge(c_made, 8 * i + 4 * j + 4)
                    sp.wait_ge(b_out, 8 * i + 4 * j + 4)
                    sp.dma_start(wbc[j][:, :],
                                 T.dram["wBC"][bass.ds(2 * i + j, 1), :, :].rearrange("n p m -> (n p) m"))\
                        .then_inc(loaded[j], 16)

        @block.tensor
        def _(pe):
            pe.sem_inc(read_out, 4)
            with pe.Fori(0, STATES // 2) as i:
                for j in range(2):
                    pe.wait_ge(loaded[j], 16 * i + 16)
                    for a in range(2):
                        for u in range(4):
                            c, s = u // 2, HALF * (u % 2)
                            if a:
                                pe.wait_ge(read_out, 8 * i + 4 * j + u + 1)
                            else:
                                pe.wait_ge(b_out, 8 * i + 4 * j + u + 5)
                            for k in range(2):
                                mm = pe.matmul(T.bank[4 * a + u][0:Q, 0:HALF], wbc[j][:, DIM * (2 * a + k) + Q * c:DIM * (2 * a + k) + Q * c + Q],
                                               T.xn[:, k, s:s + HALF], start=(k == 0), stop=(k == 1))
                            mm.then_inc(c_made if a else b_made, 1)

        @block.scalar
        def _(act):
            act.sem_inc(scanned, 2)
            act.sem_inc(driven, 2)
            with act.Fori(0, STATES // 2) as i:
                for j in range(2):
                    act.wait_ge(scanned, 2 * i + j + 1)
                    act.wait_ge(loaded[j], 16 * i + 16)
                    for c in range(2):
                        act.activation(decay[j][:, TOKENS * c:TOKENS * c + TOKENS], delta[:, c, :], ACT.Exp,
                                       scale=wbc[j][:, 4 * DIM + c:4 * DIM + c + 1]).then_inc(decayed, 1)
                    act.wait_ge(driven, 2 * i + j + 1)
                    act.wait_ge(inverted, 2 * i + j + 1)
                    for u in range(4):
                        c, s = u // 2, HALF * (u % 2)
                        act.wait_ge(b_made, 8 * i + 4 * j + u + 1)
                        act.activation(bsel[j][:, HALF * u:HALF * u + HALF], T.bank[u][0:Q, 0:HALF], ACT.Copy,
                                       scale=inv_a[j][:, c:c + 1]).then_inc(b_out, 1)

        @block.gpsimd
        def _(pool):
            xflat = T.xn[:, :, :].rearrange("p c t -> p (c t)")
            with pool.Fori(0, STATES // 2) as i:
                for j in range(2):
                    pool.wait_ge(driven, 2 * i + j + 3)
                    pool.tensor_tensor(bx[j][:, :], drive[j][:, :], xflat, ALU.mult).then_inc(bx_made, 1)

        @block.vector
        def _(dve):
            dve.sem_inc(bx_made, 1)
            with dve.Fori(0, STATES // 2) as i:
                for j in range(2):
                    n = 2 * i + j
                    dve.wait_ge(loaded[j], 16 * i + 16)
                    dve.reciprocal(inv_a[j][:, :], wbc[j][:, 4 * DIM:4 * DIM + 2]).then_inc(inverted, 1)
                    dve.wait_ge(decayed, 4 * i + 2 * j + 2)
                    dve.wait_ge(b_out, 8 * i + 4 * j + 12)
                    dve.scalar_tensor_tensor(drive[j][:, :], decay[j][:, :], 1.0, bsel[j][:, :], ALU.subtract, ALU.mult)\
                        .then_inc(driven, 1)
                    dve.wait_ge(driven, n + 3)
                    first = decay[j][:, :].rearrange("p (b t) -> p b t", t=SEQ)[:, :, 0:1]
                    dve.memset(first, 0.0).then_inc(reset, 1)
                    dve.wait_ge(reset, n + 1)
                    dve.wait_ge(bx_made, n + 2)
                    dve.tensor_tensor_scan(state[j][:, :], decay[j][:, :], bx[j][:, :], 0.0, ALU.mult, ALU.add)\
                        .then_inc(scanned, 1)
                    dve.wait_ge(scanned, n + 3)
                    for u in range(4):
                        at = slice(HALF * u, HALF * u + HALF)
                        dve.wait_ge(c_made, 8 * i + 4 * j + u + 9)
                        dve.tensor_tensor(out[j][:, at], state[j][:, at], T.bank[4 + u][0:Q, 0:HALF], ALU.mult)\
                            .then_inc(read_out, 1)
                    dve.wait_ge(read_out, 8 * i + 4 * j + 8)
                    dve.tensor_tensor(yacc[:, :], yacc[:, :], out[j][:, :], ALU.add).then_inc(added, 1)
                    dve.wait_ge(added, n + 1)
            dve.tensor_tensor(T.h[:, :, :].rearrange("p c t -> p (c t)"), T.h[:, :, :].rearrange("p c t -> p (c t)"),
                              yacc[:, :], ALU.add)


def experts(T, key):
    nc, p, m = T.nc, T.p, MOE[key]
    E, K, S, B = m["experts"], m["top"], m["shared"], m["blocks"]
    FIRST = TILES * S
    rows = T.rows[key]
    with ExitStack() as ctx:
        def sb(what, shape, dt=F32):
            return ctx.enter_context(nc.sbuf_tensor(f"{key}_{what}", shape, dt))

        weight = sb("weight", [TILE, TILES, K])
        slot = sb("slot", [TILE, K, TILES], U32)
        fetch = sb("fetch", [TILE, K, TILES], U32)
        plan = sb("plan", [1, B + 2], U32)
        route(T, key, weight, slot, fetch, plan)
        dispatch(T, key, rows, slot)
        run_blocks(T, key, rows, plan)
        combine(T, key, rows, weight, fetch)


def route(T, key, weight, slot, fetch, plan):
    nc, p, m = T.nc, T.p, MOE[key]
    E, K, S, B, CAP = m["experts"], m["top"], m["shared"], m["blocks"], m["cap"]
    FIRST = TILES * S
    HT = TILES // 2
    with ExitStack() as ctx:
        def sb(what, shape, dt=F32):
            return ctx.enter_context(nc.sbuf_tensor(f"{key}_{what}", shape, dt))

        sem = lambda what: T.sem(f"{key}_{what}")
        value, choice = sb("value", [TILE, TILES, E]), sb("choice", [TILE, TILES, E])
        best, best_at, at_f = sb("best", [TILE, TILES, 8]), sb("best_at", [TILE, TILES, 8], U32), sb("at_f", [TILE, TILES, 8])
        one_hot = sb("one_hot", [TILE, K, TILES, E])
        prod = sb("prod", [TILE, TILES, E])
        before = sb("before_tile", [TILE, TILES + 1, E])
        mask = sb("mask", [TILE, TILES, E])
        row_of, pos = sb("row_of", [TILE, TILES, E]), sb("pos", [TILE, TILES, E])
        stat = sb("stat", [TILE, TILES])
        k_row, k_pos, k_w, keep = (sb(x, [TILE, K, TILES]) for x in ("k_row", "k_pos", "k_w", "keep"))
        count, over, nblk, first, last = sb("count", [128, 1]), sb("over", [128, TILES]), sb("nblk", [128, 1]), sb("first", [128, 1]), sb("last", [128, 1])
        member, member2 = sb("member", [128, B]), sb("member2", [128, B])
        start_row = sb("start_row", [TILE, E])
        logits_made, scored, soft, masked, located, counted, blocks_known, starts_made, members, planned, step = map(
            sem, ("logits_made", "scored", "soft", "masked", "located", "counted", "blocks_known", "starts_made",
                  "members", "planned", "dve_step"))
        block = ctx.enter_context(nc.Block())
        w = cols(p[f"{key}gate"], 2)

        @block.tensor
        def _(pe):
            for g in range(2):
                for j in range(HT):
                    i = HT * g + j
                    for c in range(2):
                        mm = pe.matmul(T.bank[g][0:TILE, E * j:E * j + E], T.xn[:, c, TILE * i:TILE * i + TILE],
                                       w[:, c, :], start=(c == 0), stop=(c == 1))
                mm.then_inc(logits_made, 1)
            pe.wait_ge(masked, 1)
            for g in range(2):
                for j in range(HT):
                    i = HT * g + j
                    pe.matmul(T.bank[2 + g][0:TILE, E * j:E * j + E], p["ones"][0:TILE, 0:TILE], before[:, i, :],
                              start=True, stop=False)
                    mm = pe.matmul(T.bank[2 + g][0:TILE, E * j:E * j + E], p["before"][0:TILE, 0:TILE], mask[:, i, :],
                                   start=False, stop=True)
                mm.then_inc(located, 1)
            pe.matmul(T.bank[4][0:E, 0:1], before[:, TILES, :], p["ones"][0:TILE, 0:1], start=True, stop=True)\
                .then_inc(counted, 1)
            pe.wait_ge(blocks_known, 1)
            pe.matmul(T.bank[5][0:TILE, 0:E], nblk[0:E, 0:1].broadcast_to([E, TILE]), p["before"][0:E, 0:E],
                      start=True, stop=True).then_inc(starts_made, 1)
            pe.matmul(T.bank[6][0:E, 0:1], p["before"][0:E, 0:E], nblk[0:E, 0:1], start=True, stop=True)\
                .then_inc(starts_made, 1)
            pe.wait_ge(members, 1)
            pe.matmul(T.bank[7][0:1, 0:B], p["ecol"][0:E, 0:1], member[0:E, :], start=True, stop=True)\
                .then_inc(planned, 1)
            pe.matmul(T.bank[4][0:1, 0:1], p["ones"][0:E, 0:1], nblk[0:E, 0:1], start=True, stop=True)\
                .then_inc(planned, 1)

        @block.scalar
        def _(act):
            if key == "L2":
                for g in range(2):
                    act.wait_ge(logits_made, g + 1)
                    act.activation(value[:, HT * g:HT * g + HT, :], cols(T.bank[g][0:TILE, 0:HT * E], HT), ACT.Sigmoid)\
                        .then_inc(soft, 1)
            else:
                act.wait_ge(scored, 1)
                act.activation(value[:, :, :], value[:, :, :], ACT.Exp).then_inc(soft, 1)

        @block.vector
        def _(dve):
            link = chained(dve, step)
            gate_bias = p[f"{key}gateb"]
            if key == "L2":
                dve.wait_ge(soft, 2)
                link(dve.tensor_tensor(choice[:, :, :], value[:, :, :], spread(gate_bias, 1, TILES), ALU.add))
            else:
                for g in range(2):
                    dve.wait_ge(logits_made, g + 1)
                    link(dve.tensor_tensor(value[:, HT * g:HT * g + HT, :], cols(T.bank[g][0:TILE, 0:HT * E], HT),
                                           spread(gate_bias, 1, HT), ALU.add))
                if key == "L3":
                    link(dve.memset(value[:, :, 0:1], -1.0e9))
                link(dve.tensor_reduce(stat[:, :], value[:, :, :], AX.X, ALU.max))
                dve.tensor_tensor(value[:, :, :], value[:, :, :], spread(stat[:, :], 2, E), ALU.subtract)\
                    .then_inc(scored, 1)
                dve.wait_ge(soft, 1)
                link(dve.tensor_reduce(stat[:, :], value[:, :, :], AX.X, ALU.add))
                link(dve.reciprocal(stat[:, :], stat[:, :]))
                link(dve.tensor_tensor(value[:, :, :], value[:, :, :], spread(stat[:, :], 2, E), ALU.mult))
            pick = choice if key == "L2" else value
            for i in range(TILES):
                ins = dve.max(best[:, i, :], pick[:, i, :])
            link(ins)
            for i in range(TILES):
                ins = dve.max_index(best_at[:, i, :], best[:, i, :], pick[:, i, :])
            link(ins)
            link(dve.tensor_copy(at_f[:, :, :], best_at[:, :, :]))
            for k in range(K):
                ins = dve.tensor_tensor(one_hot[:, k, :, :], spread(p["iota"][0:TILE, 0:E], 1, TILES),
                                        at_f[:, :, k:k + 1].broadcast_to([TILE, TILES, E]), ALU.is_equal)
            link(ins)
            link(dve.tensor_tensor(mask[:, :, :], one_hot[:, 0, :, :], one_hot[:, 1, :, :], ALU.add))
            for k in range(2, K):
                link(dve.tensor_tensor(mask[:, :, :], mask[:, :, :], one_hot[:, k, :, :], ALU.add))
            link(dve.memset(before[:, 0, :], 0.0))
            for i in range(TILES):
                link(dve.tensor_tensor(before[:, i + 1, :], before[:, i, :], mask[:, i, :], ALU.add))
            dve.sem_inc(masked, 1)
            for k in range(K):
                link(dve.tensor_tensor(prod[:, :, :], one_hot[:, k, :, :], value[:, :, :], ALU.mult))
                link(dve.tensor_reduce(k_w[:, k, :], prod[:, :, :], AX.X, ALU.add))
            if key != "L3":
                link(dve.tensor_reduce(stat[:, :], k_w[:, :, :].rearrange("p k i -> p i k"), AX.X, ALU.add))
                if key == "L2":
                    link(dve.tensor_scalar(stat[:, :], stat[:, :], 1e-20, None, ALU.add))
                link(dve.reciprocal(stat[:, :], stat[:, :]))
                link(dve.tensor_tensor(k_w[:, :, :], k_w[:, :, :], spread(stat[:, :], 1, K), ALU.mult))
                if key == "L2":
                    link(dve.tensor_scalar(k_w[:, :, :], k_w[:, :, :], 2.5, None, ALU.mult))
            dve.wait_ge(counted, 1)
            link(dve.tensor_scalar(count[0:E, :], T.bank[4][0:E, 0:1], float(CAP), None, ALU.min))
            link(dve.tensor_tensor(over[0:E, :], count[0:E, 0:1].broadcast_to([E, TILES]), p["levels"][0:E, :], ALU.is_gt))
            dve.tensor_reduce(nblk[0:E, :], over[0:E, :], AX.X, ALU.add).then_inc(blocks_known, 1)
            dve.wait_ge(starts_made, 2)
            link(dve.tensor_scalar(start_row[:, :], T.bank[5][0:TILE, 0:E], float(TILE), float(FIRST * TILE), ALU.mult, ALU.add))
            link(dve.tensor_scalar(first[0:E, :], T.bank[6][0:E, 0:1], float(FIRST), None, ALU.add))
            link(dve.tensor_tensor(last[0:E, :], first[0:E, :], nblk[0:E, :], ALU.add))
            link(dve.tensor_scalar(member[0:E, :], p["iota"][0:E, 0:B], first[0:E, 0:1], None, ALU.is_ge))
            link(dve.tensor_scalar(member2[0:E, :], p["iota"][0:E, 0:B], last[0:E, 0:1], None, ALU.is_lt))
            dve.tensor_tensor(member[0:E, :], member[0:E, :], member2[0:E, :], ALU.mult).then_inc(members, 1)
            for g in range(2):
                dve.wait_ge(located, g + 1)
                at = slice(HT * g, HT * g + HT)
                link(dve.tensor_copy(pos[:, at, :], cols(T.bank[2 + g][0:TILE, 0:HT * E], HT)))
            link(dve.tensor_tensor(row_of[:, :, :], pos[:, :, :], spread(start_row[:, :], 1, TILES), ALU.add))
            for k in range(K):
                link(dve.tensor_tensor(prod[:, :, :], one_hot[:, k, :, :], row_of[:, :, :], ALU.mult))
                link(dve.tensor_reduce(k_row[:, k, :], prod[:, :, :], AX.X, ALU.add))
                link(dve.tensor_tensor(prod[:, :, :], one_hot[:, k, :, :], pos[:, :, :], ALU.mult))
                link(dve.tensor_reduce(k_pos[:, k, :], prod[:, :, :], AX.X, ALU.add))
            link(dve.tensor_scalar(keep[:, :, :], k_pos[:, :, :], float(CAP), None, ALU.is_lt))
            link(dve.tensor_tensor(weight[:, :, :], k_w[:, :, :].rearrange("p k i -> p i k"),
                                   keep[:, :, :].rearrange("p k i -> p i k"), ALU.mult))
            link(dve.tensor_tensor(k_row[:, :, :], k_row[:, :, :], keep[:, :, :], ALU.mult))
            link(dve.tensor_copy(fetch[:, :, :], k_row[:, :, :]))
            link(dve.tensor_scalar(keep[:, :, :], keep[:, :, :], -1.0, 1.0, ALU.mult, ALU.add))
            spare = cols(p["spare"], 6)[:, 0:K, :]
            link(dve.tensor_scalar(k_pos[:, :, :], spare, float(B * TILE), None, ALU.add))
            link(dve.tensor_tensor(k_pos[:, :, :], k_pos[:, :, :], keep[:, :, :], ALU.mult))
            link(dve.tensor_tensor(k_row[:, :, :], k_row[:, :, :], k_pos[:, :, :], ALU.add))
            link(dve.tensor_copy(slot[:, :, :], k_row[:, :, :]))
            dve.wait_ge(planned, 2)
            link(dve.tensor_copy(plan[0:1, 0:B], T.bank[7][0:1, 0:B]))
            link(dve.tensor_scalar(plan[0:1, B:B + 1], T.bank[4][0:1, 0:1], float(FIRST), None, ALU.add))
            for s in range(S):
                link(dve.memset(plan[0:1, TILES * s:TILES * s + TILES], 0 if key == "L3" else E + s))


def dispatch(T, key, rows, slot):
    nc, p, m = T.nc, T.p, MOE[key]
    K, S = m["top"], m["shared"]
    with ExitStack() as ctx:
        xt = ctx.enter_context(nc.sbuf_tensor(f"{key}_xt", [TILE, TILES, DIM], F32))
        sem = lambda what: T.sem(f"{key}_{what}")
        turned, xt_in, stored, scattered = map(sem, ("x_turned", "xt_in", "x_stored", "x_scattered"))
        block = ctx.enter_context(nc.Block())

        @block.tensor
        def _(pe):
            for i in range(TILES):
                for c in range(2):
                    mm = pe.transpose(T.bank[i // 2][0:TILE, DIM * (i % 2) + Q * c:DIM * (i % 2) + Q * c + Q],
                                      T.xn[:, c, TILE * i:TILE * i + TILE], p["ident"][0:Q, 0:Q])
                if i % 2:
                    mm.then_inc(turned, 1)

        @block.scalar
        def _(act):
            for u in range(TILES // 2):
                act.wait_ge(turned, u + 1)
                act.copy(xt[:, 2 * u:2 * u + 2, :], cols(T.bank[u][0:TILE, 0:2 * DIM], 2)).then_inc(xt_in, 1)

        @block.sync
        def _(sp):
            sp.wait_ge(xt_in, TILES // 2)
            for s in range(S):
                sp.dma_start(rows[TOKENS * s:TOKENS * s + TOKENS, :].rearrange("(i p) d -> p i d", p=TILE), xt[:, :, :])\
                    .then_inc(stored, 16)
            sp.wait_ge(stored, 16 * S)

        @block.gpsimd
        def _(pool):
            pool.wait_ge(xt_in, TILES // 2)
            for k in range(K):
                for i in range(TILES):
                    pool.indirect_dma_start(rows[:, :], bass.IndirectOffsetOnAxis(ap=slot[:, k, i:i + 1], axis=0),
                                            xt[:, i, :], None).then_inc(scattered, 16)
            pool.wait_ge(scattered, 16 * K * TILES)


def run_blocks(T, key, rows, plan):
    nc, p, m = T.nc, T.p, MOE[key]
    B, I, C = m["blocks"], m["width"], m["chunks"]
    N = I // C
    normed = key == "L3"
    w1_d, w2_d = T.dram[f"{key}w1"], T.dram[f"{key}w2"]
    W1, W2 = w1_d.shape[2], w2_d.shape[2]
    EXPERTS = w1_d.shape[0]
    with ExitStack() as ctx:
        def sb(what, shape, dt=F32):
            return [ctx.enter_context(nc.sbuf_tensor(f"{key}_{what}{j}", shape, dt)) for j in range(2)]

        sem = lambda what: T.sem(f"{key}_{what}")
        w1, w2, xr, xt, hid, act_out, y = (sb("w1", [Q, W1]), sb("w2", [N, W2]), sb("xr", [TILE, DIM]), sb("xtb", [Q, 2, TILE]),
                                           sb("hid", [N, C, TILE]), sb("act", [N, C, TILE]), sb("yb", [TILE, DIM]))
        if normed:
            sq, sd, yb2 = sb("sq", [N, C, TILE]), sb("sd", [N, TILE]), sb("b2", [1, DIM])
            eps = ctx.enter_context(nc.sbuf_tensor(f"{key}_eps", [128, 1], F32))
        loaded = [sem(f"loaded{j}") for j in range(2)]
        stored = [sem(f"stored{j}") for j in range(2)]
        turned, xt_in, gate, up, acted, hidden, down, y_in = map(
            sem, ("turned", "xtb_in", "gate", "up", "acted", "hidden", "down", "y_in"))
        means, centred, squared, variances, deviated, inverted, scaled, eps_set = map(
            sem, ("means", "centred", "squared", "variances", "deviated", "inverted", "scaled", "eps_set"))
        all_stored = sem("all_stored")
        loads = 64 if normed else 48
        block = ctx.enter_context(nc.Block())

        def blocks_in_use(eng):
            return eng.value_load(plan[0:1, B:B + 1], min_val=TILES, max_val=B)

        @block.sync
        def _(sp):
            sp.sem_inc(down, 2)
            n = blocks_in_use(sp)
            with sp.Fori(0, B // 2) as i:
                with sp.If(2 * i < n):
                    for j in range(2):
                        b = 2 * i + j
                        e = sp.value_load(plan[0:1, bass.ds(b, 1)], min_val=0, max_val=EXPERTS - 1)
                        sp.wait_ge(down, b + 1)
                        sp.dma_start(xr[j][:, :], rows[bass.ds(b * TILE, TILE), :]).then_inc(loaded[j], 16)
                        sp.dma_start(w1[j][:, :], w1_d[bass.ds(e, 1), :, :].rearrange("e p n -> (e p) n"))\
                            .then_inc(loaded[j], 16)
                        sp.dma_start(w2[j][:, :], w2_d[bass.ds(e, 1), :, :].rearrange("e p n -> (e p) n"))\
                            .then_inc(loaded[j], 16)
                        if normed:
                            sp.dma_start(yb2[j][:, :], T.dram["L3b2"][bass.ds(e, 1), :]).then_inc(loaded[j], 16)

        @block.tensor
        def _(pe):
            pe.sem_inc(y_in, 2)
            n = blocks_in_use(pe)
            with pe.Fori(0, B // 2) as i:
                with pe.If(2 * i < n):
                    for j in range(2):
                        pe.wait_ge(loaded[j], loads * i + loads)
                        for c in range(2):
                            mm = pe.transpose(T.bank[j][0:Q, TILE * c:TILE * c + TILE], xr[j][:, Q * c:Q * c + Q],
                                              p["ident"][0:TILE, 0:TILE])
                        mm.then_inc(turned, 1)
                    for j in range(2):
                        pe.wait_ge(xt_in, 2 * i + j + 1)
                        w = cols(w1[j][:, 0:W1 - W1 % 2], 2)
                        for a in range(1 if normed else 2):
                            for f in range(C):
                                for c in range(2):
                                    mm = pe.matmul(T.bank[2 + 2 * a + j][0:N, TILE * f:TILE * f + TILE],
                                                   w[:, c, I * a + N * f:I * a + N * f + N], xt[j][:, c, :],
                                                   start=(c == 0), stop=(c == 1))
                            mm.then_inc(up if a else gate, 1)
                    if normed:
                        for j in range(2):
                            pe.wait_ge(acted, 2 * i + j + 1)
                            for f in range(C):
                                mm = pe.matmul(T.bank[4 + j][0:N, 0:TILE], p["mean384"], hid[j][:, f, :],
                                               start=(f == 0), stop=(f == C - 1))
                            mm.then_inc(means, 1)
                        for j in range(2):
                            pe.wait_ge(squared, 2 * i + j + 1)
                            for f in range(C):
                                mm = pe.matmul(T.bank[4 + j][0:N, TILE:2 * TILE], p["mean384"], sq[j][:, f, :],
                                               start=(f == 0), stop=(f == C - 1))
                            mm.then_inc(variances, 1)
                    for j in range(2):
                        pe.wait_ge(hidden, 2 * i + j + 1)
                        pe.wait_ge(y_in, 2 * i + j + 1)
                        w = cols(w2[j][:, 0:C * DIM], C)
                        if normed:
                            pe.matmul(T.bank[6 + j][0:TILE, 0:DIM], p["ones"][0:1, 0:TILE], yb2[j][:, :],
                                      start=True, stop=False)
                        for f in range(C):
                            mm = pe.matmul(T.bank[6 + j][0:TILE, 0:DIM], act_out[j][:, f, :], w[:, f, :],
                                           start=(f == 0 and not normed), stop=(f == C - 1))
                        mm.then_inc(down, 1)

        @block.scalar
        def _(act):
            for j in range(2):
                act.sem_inc(stored[j], 16)
            if normed:
                act.wait_ge(eps_set, 1)
            n = blocks_in_use(act)
            with act.Fori(0, B // 2) as i:
                with act.If(2 * i < n):
                    for j in range(2):
                        act.wait_ge(gate, 2 * i + j + 1)
                        got = cols(T.bank[2 + j][0:N, 0:C * TILE], C)
                        if not normed:
                            act.activation(hid[j][:, :, :], got, ACT.Silu).then_inc(acted, 1)
                        else:
                            for f in range(C):
                                ins = act.activation(hid[j][:, f, :], got[:, f, :], ACT.Gelu,
                                                     bias=w2[j][:, C * DIM + f:C * DIM + f + 1])
                            ins.then_inc(acted, 1)
                    if normed:
                        for j in range(2):
                            act.wait_ge(centred, 2 * i + j + 1)
                            act.activation(sq[j][:, :, :], act_out[j][:, :, :], ACT.Square).then_inc(squared, 1)
                        for j in range(2):
                            act.wait_ge(variances, 2 * i + j + 1)
                            act.activation(sd[j][:, :], T.bank[4 + j][0:N, TILE:2 * TILE], ACT.Sqrt, bias=eps[:, 0:1])\
                                .then_inc(deviated, 1)
                        for j in range(2):
                            act.wait_ge(scaled, 2 * i + j + 1)
                            for f in range(C):
                                at = C * DIM + C + f
                                ins = act.activation(act_out[j][:, f, :], hid[j][:, f, :], ACT.Identity,
                                                     scale=w2[j][:, at:at + 1], bias=w2[j][:, at + C:at + C + 1])
                            ins.then_inc(hidden, 1)
                    for j in range(2):
                        act.wait_ge(down, 2 * i + j + 3)
                        act.wait_ge(stored[j], 16 * i + 16)
                        act.copy(y[j][:, :], T.bank[6 + j][0:TILE, 0:DIM]).then_inc(y_in, 1)
                        act.wait_ge(y_in, 2 * i + j + 3)
                        act.dma_start(rows[bass.ds((2 * i + j) * TILE, TILE), :], y[j][:, :]).then_inc(stored[j], 16)
            for j in range(2):
                act.wait_ge(stored[j], (n + 1) // 2 * 16 + 16)
                act.sem_inc(all_stored, 1)

        @block.vector
        def _(dve):
            if normed:
                dve.memset(eps[:, :], EPS).then_inc(eps_set, 1)
            n = blocks_in_use(dve)
            with dve.Fori(0, B // 2) as i:
                with dve.If(2 * i < n):
                    for j in range(2):
                        dve.wait_ge(turned, 2 * i + j + 1)
                        dve.tensor_copy(xt[j][:, :, :], cols(T.bank[j][0:Q, 0:2 * TILE], 2)).then_inc(xt_in, 1)
                    if not normed:
                        for j in range(2):
                            dve.wait_ge(acted, 2 * i + j + 1)
                            dve.wait_ge(up, 2 * i + j + 1)
                            dve.tensor_tensor(act_out[j][:, :, :], hid[j][:, :, :], cols(T.bank[4 + j][0:N, 0:C * TILE], C),
                                              ALU.mult).then_inc(hidden, 1)
                    else:
                        for j in range(2):
                            dve.wait_ge(means, 2 * i + j + 1)
                            dve.tensor_tensor(act_out[j][:, :, :], hid[j][:, :, :],
                                              spread(T.bank[4 + j][0:N, 0:TILE], 1, C), ALU.subtract).then_inc(centred, 1)
                        for j in range(2):
                            dve.wait_ge(deviated, 2 * i + j + 1)
                            dve.reciprocal(sd[j][:, :], sd[j][:, :]).then_inc(inverted, 1)
                            dve.wait_ge(inverted, 2 * i + j + 1)
                            dve.tensor_tensor(hid[j][:, :, :], act_out[j][:, :, :], spread(sd[j][:, :], 1, C), ALU.mult)\
                                .then_inc(scaled, 1)


def combine(T, key, rows, weight, fetch):
    nc, p, m = T.nc, T.p, MOE[key]
    K, S, B = m["top"], m["shared"], m["blocks"]
    with ExitStack() as ctx:
        def sb(what, shape):
            return ctx.enter_context(nc.sbuf_tensor(f"{key}_{what}", shape, F32))

        sem = lambda what: T.sem(f"{key}_{what}")
        shared = sb("shared_y", [TILE, S, TILES, DIM])
        got = sb("got", [TILE, K, TILES, DIM])
        shared_in, added, turned = map(sem, ("shared_in", "added", "y_turned"))
        fetched = [sem(f"fetched{k}") for k in range(K)]
        block = ctx.enter_context(nc.Block())
        acc = shared[:, 0, :, :]

        @block.sync
        def _(sp):
            for s in range(S):
                sp.dma_start(shared[:, s, :, :], rows[TOKENS * s:TOKENS * s + TOKENS, :].rearrange("(i p) d -> p i d", p=TILE))\
                    .then_inc(shared_in, 16)

        @block.gpsimd
        def _(pool):
            for k in range(K):
                for i in range(TILES):
                    pool.indirect_dma_start(got[:, k, i, :], None, rows[0:B * TILE, :],
                                            bass.IndirectOffsetOnAxis(ap=fetch[:, k, i:i + 1], axis=0))\
                        .then_inc(fetched[k], 16)

        @block.vector
        def _(dve):
            dve.wait_ge(shared_in, 16 * S)
            n = 0
            for s in range(1, S):
                dve.tensor_tensor(acc, acc, shared[:, s, :, :], ALU.add).then_inc(added, 1)
                n += 1
                dve.wait_ge(added, n)
            for k in range(K):
                dve.wait_ge(fetched[k], 16 * TILES)
                for i in range(TILES):
                    dve.scalar_tensor_tensor(shared[:, 0, i, :], got[:, k, i, :], weight[:, i, k:k + 1], shared[:, 0, i, :],
                                             ALU.mult, ALU.add).then_inc(added, 1)
                    n += 1
                dve.wait_ge(added, n)
            for u in range(4):
                c, s = u // 2, HALF * (u % 2)
                dve.wait_ge(turned, u + 1)
                dve.tensor_tensor(T.h[:, c, s:s + HALF], T.h[:, c, s:s + HALF], T.bank[u][0:Q, 0:HALF], ALU.add)

        @block.tensor
        def _(pe):
            pe.wait_ge(added, S - 1 + K * TILES)
            for u in range(4):
                c, half = u // 2, u % 2
                for j in range(TILES // 2):
                    mm = pe.transpose(T.bank[u][0:Q, TILE * j:TILE * j + TILE],
                                      shared[:, 0, TILES // 2 * half + j, Q * c:Q * c + Q], p["ident"][0:TILE, 0:TILE])
                mm.then_inc(turned, 1)


def layer3_attention(T):
    nc, p = T.nc, T.p
    with ExitStack() as ctx:
        def sb(what, shape):
            return ctx.enter_context(nc.sbuf_tensor(f"a3_{what}", shape, F32))
        qk, v, att = sb("qk", [Q, 4, TOKENS]), sb("v", [SEQ, IMAGES, DIM]), sb("att", [Q, 2, TOKENS])
        w = cols(p["aqkv"], 2)
        linear(T, "a3_qk", 4, 2, lambda m, k: w[:, k, Q * m:Q * m + Q], lambda k, at: T.xn[:, k, at],
               by_act=biased(T, qk, p["aqkvb"]))
        values_by_token(T, "a3_vals", T.xn, w[:, :, 2 * DIM:3 * DIM], v, SEQ)
        head_attention(T, "a3_att", qk, v, p["aqkvb"][:, 4:6], att, True)
        w2 = cols(p["aproj"], 2)
        linear(T, "a3_proj", 2, 2, lambda m, k: w2[:, k, Q * m:Q * m + Q], lambda k, at: att[:, k, at],
               by_dve=residual(T, T.h, p["aprojb"]))


def store_output(T):
    nc, p = T.nc, T.p
    with ExitStack() as ctx:
        out = ctx.enter_context(nc.sbuf_tensor("out_rows", [TILE, TILES, DIM], F32))
        turned = T.sem("out_turned")
        taken = T.sem("out_taken")
        stored = T.sem("out_stored")
        block = ctx.enter_context(nc.Block())

        @block.tensor
        def _(pe):
            for i in range(TILES):
                for c in range(2):
                    mm = pe.transpose(T.bank[i // 2][0:TILE, DIM * (i % 2) + Q * c:DIM * (i % 2) + Q * c + Q],
                                      T.h[:, c, TILE * i:TILE * i + TILE], p["ident"][0:Q, 0:Q])
                if i % 2:
                    mm.then_inc(turned, 1)

        @block.vector
        def _(dve):
            for u in range(TILES // 2):
                dve.wait_ge(turned, u + 1)
                dve.tensor_copy(out[:, 2 * u:2 * u + 2, :], cols(T.bank[u][0:TILE, 0:2 * DIM], 2)).then_inc(taken, 1)

        @block.sync
        def _(sp):
            sp.wait_ge(taken, TILES // 2)
            sp.dma_start(T.dram["out"].rearrange("(i p) d -> p i d", p=TILE), out[:, :, :]).then_inc(stored, 16)
            sp.wait_ge(stored, 16)


STAGES = ["tok", "L0a", "L0f", "L1a", "L1f", "L2a", "L2f", "L3a", "L3f"]


def build(nc, dram, stages=STAGES):
    with ExitStack() as ctx:
        T = Tower(nc, ctx, dram)
        load_all(T)
        T.end_layer()
        layers = {"L0a": layer0_attention, "L0f": lambda t: experts(t, "L0"), "L1a": layer1_attention,
                  "L1f": layer1_block, "L2a": selective_scan, "L2f": lambda t: experts(t, "L2"),
                  "L3a": layer3_attention, "L3f": lambda t: experts(t, "L3")}
        for s in stages:
            if s in layers:
                layer_norm(T, f"{s}_ln", T.h, T.xn)
                layers[s](T)
                T.end_layer()
        store_output(T)


def fm(w):
    return np.concatenate([w[:Q], w[Q:]], axis=1)


def vec(*bs):
    return np.concatenate([b.reshape(-1, Q).T for b in bs], axis=1)


def chunks(w, n):
    return w.reshape(-1, n, w.shape[1]).transpose(1, 0, 2).reshape(n, -1)


def constants():
    i = np.arange(128)
    pair = np.arange(PAIR) // SEQ
    same = (pair[:, None] == pair[None, :])
    k, t, q = np.meshgrid(np.arange(6), np.arange(TILES), np.arange(TILE), indexing="ij")
    return {
        "ident": np.eye(128), "ones": np.ones((128, 128)), "mean192": np.full((Q, Q), 1 / DIM),
        "mean384": np.full((128, 128), 1 / 384), "before": i[:, None] < i[None, :],
        "iota": np.broadcast_to(np.arange(MAX_BLOCKS), (128, MAX_BLOCKS)), "ecol": i[:, None],
        "levels": np.broadcast_to(TILE * np.arange(TILES), (128, TILES)),
        "spare": (TOKENS * k + TILE * t + q).transpose(2, 0, 1).reshape(TILE, -1),
        "apart": np.where(same, 0.0, -1.0e30), "same": same,
        "headmask": (np.arange(Q) // HEAD_DIM)[:, None] == np.arange(6)[None, :],
    }


def layout(x):
    def rows(b, n):
        return np.broadcast_to(b.reshape(1, -1), (n, b.size))

    f = constants()
    f.update(tokW=chunks(x["L0_tok_W"], 128), tokb=vec(x["L0_tok_b"]),
             l0qkv=fm(x["L0_attn_w_qkv"].T), l0qkvb=vec(x["L0_attn_b_qkv"]), l0proj=fm(x["L0_attn_w_proj"].T),
             l0projb=vec(x["L0_attn_b_proj"]), L0gate=fm(x["L0_ffn_w_gate"]), L0gateb=rows(x["L0_ffn_expert_bias"], TILE),
             l1q=fm(x["L1_attn_Wq"].T), l1k=fm(x["L1_attn_Wk"].T), l1v=fm(x["L1_attn_Wv"].T),
             l1qkb=vec(x["L1_attn_bq"], x["L1_attn_bk"]), l1vb=rows(x["L1_attn_bv"], PAIR))
    b = {k[7:]: v for k, v in x.items() if k.startswith("L1_ffn_")}
    f.update(mq=fm(b["wq"].T), mk=fm(b["wk"].T), mv=fm(b["wv"].T), mo=fm(b["wo"].T), mqkvb=vec(b["bq"], b["bk"], b["bv"]),
             mob=vec(b["bo"]), ln1=vec(b["ln1_g"], b["ln1_b"]), ln2=vec(b["ln2_g"], b["ln2_b"]),
             rln=vec(b["r_ln_g"], b["r_ln_b"]), fc1=fm(b["fc1_w"].T), fc1b=b["fc1_b"].reshape(6, 128).T,
             fc2=chunks(b["fc2_w"].T, 128), fc2b=vec(b["fc2_b"]), rin=fm(b["r_in_w"].T), rinb=b["r_in_b"][:, None],
             ro1=chunks(b["r_o1_w"].T, 128), ro1b=b["r_o1_b"][:, None], ro2=b["r_o2_w"].T, ro2b=b["r_o2_b"][:, None],
             ro3=b["r_o3_w"].T, ro3b=rows(b["r_o3_b"], 128), ldown=fm(b["lra_down"].reshape(192, DIM).T),
             lup01=b["lra_up"][:2].transpose(0, 2, 1).reshape(128, DIM), lup2=b["lra_up"][2].T)
    A = x["L2_attn_A"]
    f.update(sD=fm(x["L2_attn_W_delta"].T), sDb=vec(x["L2_attn_delta_bias"]),
             L2gate=fm(x["L2_ffn_Wg"].T), L2gateb=rows(x["L2_ffn_e_bias"], TILE),
             aqkv=fm(x["L3_attn_W_qkv"]), aqkvb=vec(x["L3_attn_b_qkv"]), aproj=fm(x["L3_attn_W_proj"]),
             aprojb=vec(x["L3_attn_b_proj"]), L3gate=fm(x["L3_ffn_gate_w"]), L3gateb=rows(x["L3_ffn_gate_b"], TILE))
    out = {}
    for g, items in GROUPS.items():
        t = out[g] = np.zeros((128, WIDTHS[g]), np.float32)
        at = 0
        for name, parts, n in items:
            t[0:parts, at:at + n] = f[name]
            at += n
    im = x["x"].reshape(IMAGES, 3, 6, 16, 6, 16).transpose(1, 3, 5, 0, 2, 4).reshape(PATCH_K, 128, TOKENS)
    out["patches"] = np.ascontiguousarray(im.transpose(1, 0, 2))
    bc = np.stack([x["L2_attn_W_B"], x["L2_attn_W_C"]]).reshape(2, DIM, STATES, 2, Q)
    bc = bc.transpose(2, 4, 0, 3, 1).reshape(STATES, Q, 4 * DIM)
    out["wBC"] = np.concatenate([bc, A.reshape(2, Q, STATES).transpose(2, 1, 0)], axis=2)

    def first(w):
        return w.reshape(w.shape[0], 2, Q, w.shape[2]).transpose(0, 2, 1, 3).reshape(w.shape[0], Q, -1)

    def second(w, n):
        return w.reshape(w.shape[0], -1, n, DIM).transpose(0, 2, 1, 3).reshape(w.shape[0], n, -1)

    gu = np.concatenate([x["L0_ffn_wg"], x["L0_ffn_wu"]], axis=2)
    sgu = np.concatenate([x["L0_ffn_swg"], x["L0_ffn_swu"]], axis=1)[None]
    out["L0w1"] = first(np.concatenate([gu, sgu]))
    out["L0w2"] = second(np.concatenate([x["L0_ffn_wd"], x["L0_ffn_swd"][None]]), 128)
    I = MOE["L2"]["width"]
    sgu = [np.concatenate([x["L2_ffn_Wsg"][:, I * s:I * s + I], x["L2_ffn_Wsu"][:, I * s:I * s + I]], axis=1) for s in range(2)]
    out["L2w1"] = first(np.concatenate([x["L2_ffn_W_gate_up"], np.stack(sgu)]))
    out["L2w2"] = second(np.concatenate([x["L2_ffn_W_down"], x["L2_ffn_Wsd"].reshape(2, I, DIM)]), 116)
    out["L3w1"] = first(x["L3_ffn_fc1_w"])
    cols3 = [x[k].reshape(16, 3, 128).transpose(0, 2, 1) for k in ("L3_ffn_fc1_b", "L3_ffn_ln_w", "L3_ffn_ln_b")]
    out["L3w2"] = np.concatenate([second(x["L3_ffn_fc2_w"], 128)] + cols3, axis=2)
    out["L3b2"] = x["L3_ffn_fc2_b"]
    return {k: np.ascontiguousarray(v) for k, v in out.items()}


def kernel(**inputs):
    import concourse.bacc as bacc
    from concourse.bass_utils import run_bass_kernel_spmd

    nc = bacc.Bacc("TRN2", target_bir_lowering=False, num_devices=1)
    arrays = layout({k: np.asarray(v) for k, v in inputs.items()})
    dram = {k: nc.dram_tensor(f"in_{k}", a.shape, F32, kind="ExternalInput").ap() for k, a in arrays.items()}
    dram["out"] = nc.dram_tensor("out_h", (TOKENS, DIM), F32, kind="ExternalOutput").ap()
    build(nc, dram)
    r = run_bass_kernel_spmd(nc, [{f"in_{k}": a for k, a in arrays.items()}], core_ids=[0])
    return r.results[0]["out_h"].reshape(IMAGES, SEQ, DIM)
```

```python
from contextlib import ExitStack

import numpy as np

import concourse.bass as bass
from concourse import mybir

F32 = mybir.dt.float32
U32 = mybir.dt.uint32
ALU = mybir.AluOpType
ACT = mybir.ActivationFunctionType
AX = mybir.AxisListType

IMAGES, SEQ, DIM = 16, 36, 192
TOKENS = IMAGES * SEQ
Q = 96
HALF = TOKENS // 2
PATCH_K = 6
PAIR = 2 * SEQ
PAIRS = TOKENS // PAIR
TILE = 96
TILES = TOKENS // TILE
HEADS, HEAD_DIM = 12, 16
KEEP = int(0.4 * SEQ)
STATES = 16
EPS = 1e-5

MOE = {
    "L0": dict(experts=16, top=2, cap=TOKENS, shared=1, width=384, chunks=3),
    "L2": dict(experts=128, top=6, cap=192, shared=2, width=464, chunks=4),
    "L3": dict(experts=16, top=3, cap=TOKENS, shared=1, width=384, chunks=3),
}
for _m in MOE.values():
    _most = (TOKENS * _m["top"] + _m["experts"] * (TILE - 1)) // TILE
    _m["blocks"] = (_most + 3) // 4 * 4
    _m["rows"] = _m["blocks"] * TILE
MAX_BLOCKS = max(_m["blocks"] for _m in MOE.values())

GROUPS = {
    "const": [("ident", 128, 128), ("ones", 128, 128), ("mean192", Q, Q), ("mean384", 128, 128),
              ("before", 128, 128), ("iota", 128, MAX_BLOCKS), ("ecol", 128, 1), ("levels", 128, TILES),
              ("spare", TILE, TILES * 6), ("apart", PAIR, PAIR), ("same", PAIR, PAIR), ("headmask", Q, 6)],
    "tok": [("tokW", 128, PATCH_K * DIM), ("tokb", Q, 2)],
    "L0a": [("l0qkv", Q, 6 * DIM), ("l0qkvb", Q, 6), ("l0proj", Q, 2 * DIM), ("l0projb", Q, 2),
            ("L0gate", Q, 32), ("L0gateb", TILE, 16)],
    "L1a": [("l1q", Q, 2 * DIM), ("l1k", Q, 2 * DIM), ("l1v", Q, 2 * DIM), ("l1qkb", Q, 4),
            ("l1vb", PAIR, DIM)],
    "L1f": [("mq", Q, 2 * DIM), ("mk", Q, 2 * DIM), ("mv", Q, 2 * DIM), ("mo", Q, 2 * DIM),
            ("mqkvb", Q, 6), ("mob", Q, 2), ("ln1", Q, 4), ("ln2", Q, 4), ("rln", Q, 4),
            ("fc1", Q, 2 * 768), ("fc1b", 128, 6), ("fc2", 128, 6 * DIM), ("fc2b", Q, 2),
            ("rin", Q, 2 * 128), ("rinb", 128, 1), ("ro1", 128, 2 * 128), ("ro1b", 128, 1),
            ("ro2", 128, 64), ("ro2b", 64, 1), ("ro3", 64, 4), ("ro3b", 128, 4),
            ("ldown", Q, 2 * DIM), ("lup01", 128, DIM), ("lup2", 64, DIM)],
    "L2a": [("sD", Q, 2 * DIM), ("sDb", Q, 2), ("L2gate", Q, 256), ("L2gateb", TILE, 128)],
    "L3a": [("aqkv", Q, 6 * DIM), ("aqkvb", Q, 6), ("aproj", Q, 2 * DIM), ("aprojb", Q, 2),
            ("L3gate", Q, 32), ("L3gateb", TILE, 16), ("L3b2v", Q, 2)],
}
WIDTHS = {g: sum(n for _, _, n in items) for g, items in GROUPS.items()}


class Tower:

    def __init__(self, nc, ctx, dram):
        self.nc, self.dram, self.of_layer = nc, dram, []
        self.h = ctx.enter_context(nc.sbuf_tensor("h", [Q, 2, TOKENS], F32))
        self.xn = ctx.enter_context(nc.sbuf_tensor("xn", [Q, 2, TOKENS], F32))
        self.bank = [ctx.enter_context(nc.psum_tensor(f"bank{i}", [128, 512], F32)) for i in range(8)]
        self.loaded = {g: ctx.enter_context(nc.semaphore(f"loaded_{g}")) for g in GROUPS}
        self.zero = ctx.enter_context(nc.sbuf_tensor("zero", [TILE, 12 * DIM], F32))
        self.zeroed = ctx.enter_context(nc.semaphore("rows_zeroed"))
        self.p, self.packed = {}, {}
        for g, items in GROUPS.items():
            t = self.packed[g] = ctx.enter_context(nc.sbuf_tensor(f"par_{g}", [128, WIDTHS[g]], F32))
            at = 0
            for name, parts, n in items:
                self.p[name] = t[0:parts, at:at + n]
                at += n
        self.rows = {k: nc.dram_tensor(f"rows_{k}", [m["rows"] + TOKENS * m["top"], DIM], F32, kind="Internal").ap()
                     for k, m in MOE.items()}

    def sem(self, name):
        s = self.nc.alloc_semaphore(name)
        self.of_layer.append(s)
        return s

    def end_layer(self):
        self.nc.clear_and_free_semaphores(self.of_layer)
        self.nc.all_engine_barrier()
        self.of_layer = []


def cols(ap, n):
    return ap.rearrange("p (n m) -> p n m", n=n)


def spread(ap, axis, n):
    a = ap.unsqueeze(axis)
    shape = list(a.shape)
    shape[axis] = n
    return a.broadcast_to(shape)


def chained(eng, sem):
    count = [0]

    def link(ins):
        count[0] += 1
        ins.then_inc(sem, 1)
        eng.wait_ge(sem, count[0])

    return link


def load_all(T):
    nc = T.nc
    with ExitStack() as ctx:
        wtok = ctx.enter_context(nc.sbuf_tensor("patches", [128, PATCH_K, TOKENS], F32))
        patches_in = T.sem("patches_in")
        zero_ready = T.sem("zero_ready")
        products = T.sem("tok_products")
        block = ctx.enter_context(nc.Block())
        W = cols(T.p["tokW"], PATCH_K)

        @block.sync
        def _(sp):
            sp.dma_start(T.packed["tok"][:, :], T.dram["tok"]).then_inc(T.loaded["tok"], 16)
            sp.dma_start(wtok[:, 0:3, :], T.dram["patches"][:, 0:3, :]).then_inc(patches_in, 16)
            sp.dma_start(wtok[:, 3:6, :], T.dram["patches"][:, 3:6, :]).then_inc(patches_in, 16)
            for g in GROUPS:
                if g != "tok":
                    sp.dma_start(T.packed[g][:, :], T.dram[g]).then_inc(T.loaded[g], 16)
            sp.wait_ge(zero_ready, 1)
            for k, m in MOE.items():
                for r in range(0, m["blocks"], 12):
                    n = min(12, m["blocks"] - r)
                    sp.dma_start(T.rows[k][TILE * r:TILE * (r + n), :].rearrange("(p a) d -> p (a d)", p=TILE),
                                 T.zero[:, 0:n * DIM]).then_inc(T.zeroed, 16)
            sp.wait_ge(T.loaded["const"], 16)

        @block.vector
        def _(dve):
            dve.memset(T.zero[:, :], 0.0).then_inc(zero_ready, 1)

        @block.tensor
        def _(pe):
            pe.wait_ge(T.loaded["tok"], 16)
            pe.wait_ge(patches_in, 32)
            for u in range(4):
                m, s = u // 2, HALF * (u % 2)
                for k in range(PATCH_K):
                    mm = pe.matmul(T.bank[u][0:Q, 0:HALF], W[:, k, Q * m:Q * m + Q], wtok[:, k, s:s + HALF],
                                   start=(k == 0), stop=(k == PATCH_K - 1))
                mm.then_inc(products, 1)

        @block.scalar
        def _(act):
            for u in range(4):
                m, s = u // 2, HALF * (u % 2)
                act.wait_ge(products, u + 1)
                act.activation(T.h[:, m, s:s + HALF], T.bank[u][0:Q, 0:HALF], ACT.Identity,
                               bias=T.p["tokb"][:, m:m + 1])


def layer_norm(T, name, x, out, meanwhile=None):
    nc = T.nc
    with ExitStack() as ctx:
        xc = ctx.enter_context(nc.sbuf_tensor(f"{name}_xc", [Q, 2, TOKENS], F32))
        sq = ctx.enter_context(nc.sbuf_tensor(f"{name}_sq", [Q, 2, TOKENS], F32))
        sd = ctx.enter_context(nc.sbuf_tensor(f"{name}_sd", [Q, 2, HALF], F32))
        eps = ctx.enter_context(nc.sbuf_tensor(f"{name}_eps", [Q, 1], F32))
        eps_set = T.sem(f"{name}_eps_set")
        means = T.sem(f"{name}_means")
        centred = T.sem(f"{name}_centred")
        squared = T.sem(f"{name}_squared")
        variances = T.sem(f"{name}_variances")
        deviations = T.sem(f"{name}_deviations")
        inverted = T.sem(f"{name}_inverted")
        block = ctx.enter_context(nc.Block())

        if meanwhile:
            @block.sync
            def _(sp):
                meanwhile(sp)

        @block.tensor
        def _(pe):
            for s in range(2):
                for c in range(2):
                    mm = pe.matmul(T.bank[s][0:Q, 0:HALF], T.p["mean192"], x[:, c, HALF * s:HALF * s + HALF],
                                   start=(c == 0), stop=(c == 1))
                mm.then_inc(means, 1)
            for s in range(2):
                pe.wait_ge(squared, s + 1)
                for c in range(2):
                    mm = pe.matmul(T.bank[2 + s][0:Q, 0:HALF], T.p["mean192"], sq[:, c, HALF * s:HALF * s + HALF],
                                   start=(c == 0), stop=(c == 1))
                mm.then_inc(variances, 1)

        @block.vector
        def _(dve):
            dve.memset(eps[:, :], EPS).then_inc(eps_set, 1)
            for s in range(2):
                at = slice(HALF * s, HALF * s + HALF)
                dve.wait_ge(means, s + 1)
                dve.tensor_tensor(xc[:, :, at], x[:, :, at], spread(T.bank[s][0:Q, 0:HALF], 1, 2), ALU.subtract)\
                    .then_inc(centred, 1)
            for s in range(2):
                at = slice(HALF * s, HALF * s + HALF)
                dve.wait_ge(deviations, s + 1)
                dve.reciprocal(sd[:, s, :], sd[:, s, :]).then_inc(inverted, 1)
                dve.wait_ge(inverted, s + 1)
                dve.tensor_tensor(out[:, :, at], xc[:, :, at], spread(sd[:, s, :], 1, 2), ALU.mult)

        @block.scalar
        def _(act):
            for s in range(2):
                at = slice(HALF * s, HALF * s + HALF)
                act.wait_ge(centred, s + 1)
                act.activation(sq[:, :, at], xc[:, :, at], ACT.Square).then_inc(squared, 1)
            act.wait_ge(eps_set, 1)
            for s in range(2):
                act.wait_ge(variances, s + 1)
                act.activation(sd[:, s, :], T.bank[2 + s][0:Q, 0:HALF], ACT.Sqrt, bias=eps[:, 0:1])\
                    .then_inc(deviations, 1)


def linear(T, name, outs, terms, lhsT, rhs, by_act=None, by_dve=None, size=Q):
    nc = T.nc
    units = [(m, slice(HALF * s, HALF * s + HALF)) for m in range(outs) for s in range(2)]
    on_act = [by_dve is None or (by_act is not None and u % 2 == 0) for u in range(len(units))]
    with ExitStack() as ctx:
        products = T.sem(f"{name}_products")
        act_took = T.sem(f"{name}_act_took")
        dve_took = T.sem(f"{name}_dve_took")
        block = ctx.enter_context(nc.Block())

        @block.tensor
        def _(pe):
            for u, (m, at) in enumerate(units):
                if u >= 8:
                    if on_act[u - 8]:
                        pe.wait_ge(act_took, sum(on_act[:u - 7]))
                    else:
                        pe.wait_ge(dve_took, u - 7 - sum(on_act[:u - 7]))
                for k in range(terms):
                    mm = pe.matmul(T.bank[u % 8][0:size, 0:HALF], lhsT(m, k), rhs(k, at),
                                   start=(k == 0), stop=(k == terms - 1))
                mm.then_inc(products, 1)

        @block.scalar
        def _(act):
            for u, (m, at) in enumerate(units):
                if on_act[u]:
                    act.wait_ge(products, u + 1)
                    by_act(m, at, T.bank[u % 8][0:size, 0:HALF]).then_inc(act_took, 1)

        @block.vector
        def _(dve):
            for u, (m, at) in enumerate(units):
                if not on_act[u]:
                    dve.wait_ge(products, u + 1)
                    by_dve(m, at, T.bank[u % 8][0:size, 0:HALF]).then_inc(dve_took, 1)


def values_by_token(T, name, x, w, v, group, bias=None):
    nc = T.nc
    units = TOKENS // group // 2
    with ExitStack() as ctx:
        products = T.sem(f"{name}_products")
        taken = T.sem(f"{name}_taken")
        block = ctx.enter_context(nc.Block())

        @block.tensor
        def _(pe):
            for u in range(units):
                if u >= 8:
                    pe.wait_ge(taken, u - 7)
                for j in range(2):
                    at = group * (2 * u + j)
                    for c in range(2):
                        mm = pe.matmul(T.bank[u % 8][0:group, DIM * j:DIM * j + DIM], x[:, c, at:at + group], w[:, c, :],
                                       start=(c == 0), stop=(c == 1))
                mm.then_inc(products, 1)

        @block.vector
        def _(dve):
            for u in range(units):
                dve.wait_ge(products, u + 1)
                got = cols(T.bank[u % 8][0:group, 0:2 * DIM], 2)
                if bias is None:
                    dve.tensor_copy(v[:, 2 * u:2 * u + 2, :], got).then_inc(taken, 1)
                else:
                    dve.tensor_tensor(v[:, 2 * u:2 * u + 2, :], got, spread(bias, 1, 2), ALU.add).then_inc(taken, 1)


def wide_attention(T, name, qk, v, softmax_scale, linear_scale, take):
    nc = T.nc
    per = PAIRS // 2
    with ExitStack() as ctx:
        sm = ctx.enter_context(nc.sbuf_tensor(f"{name}_sm", [PAIR, PAIRS, PAIR], F32))
        probs_t = ctx.enter_context(nc.sbuf_tensor(f"{name}_pt", [PAIR, PAIRS, PAIR], F32))
        mx = ctx.enter_context(nc.sbuf_tensor(f"{name}_mx", [PAIR, PAIRS], F32))
        total = ctx.enter_context(nc.sbuf_tensor(f"{name}_total", [PAIR, PAIRS], F32))
        sem = lambda what: T.sem(f"{name}_{what}")
        scored, lowered, exps, probs, turned, turned_in, summed = map(
            sem, ("scored", "lowered", "exps", "probs", "turned", "turned_in", "summed"))
        step = sem("dve_step")
        block = ctx.enter_context(nc.Block())

        @block.tensor
        def _(pe):
            for g in range(2):
                for j in range(per):
                    at = slice(PAIR * (per * g + j), PAIR * (per * g + j) + PAIR)
                    a, b = (0, 2) if softmax_scale else (2, 0)
                    for c in range(2):
                        mm = pe.matmul(T.bank[g][0:PAIR, PAIR * j:PAIR * j + PAIR], qk[:, a + c, at], qk[:, b + c, at],
                                       start=(c == 0), stop=(c == 1))
                mm.then_inc(scored, 1)
            if softmax_scale:
                for g in range(2):
                    pe.wait_ge(probs, g + 1)
                    for j in range(per):
                        mm = pe.transpose(T.bank[2 + g][0:PAIR, PAIR * j:PAIR * j + PAIR], sm[:, per * g + j, :],
                                          T.p["ident"][0:PAIR, 0:PAIR])
                    mm.then_inc(turned, 1)
            for g in range(2):
                pe.wait_ge(turned_in, g + 1)
                for m in range(2):
                    for j in range(per):
                        i = per * g + j
                        mm = pe.matmul(T.bank[4 + 2 * g + m][0:Q, PAIR * j:PAIR * j + PAIR],
                                       v[:, i, Q * m:Q * m + Q], probs_t[:, i, :], start=True, stop=True)
                    mm.then_inc(summed, 1)

        @block.vector
        def _(dve):
            link = chained(dve, step)
            for g in range(2):
                dve.wait_ge(scored, g + 1)
                got = cols(T.bank[g][0:PAIR, 0:PAIR * per], per)
                part = sm[:, per * g:per * g + per, :]
                top = mx[:, per * g:per * g + per]
                if softmax_scale:
                    link(dve.tensor_tensor(part, got, spread(T.p["apart"], 1, per), ALU.add))
                    link(dve.tensor_reduce(top, part, AX.X, ALU.max))
                    dve.tensor_tensor(part, part, spread(top, 2, PAIR), ALU.subtract).then_inc(lowered, 1)
                else:
                    dve.scalar_tensor_tensor(probs_t[:, per * g:per * g + per, :], got, linear_scale,
                                             spread(T.p["same"], 1, per), ALU.mult, ALU.mult).then_inc(turned_in, 1)
            if softmax_scale:
                for g in range(2):
                    part = sm[:, per * g:per * g + per, :]
                    tot = total[:, per * g:per * g + per]
                    dve.wait_ge(exps, g + 1)
                    link(dve.tensor_reduce(tot, part, AX.X, ALU.add))
                    link(dve.reciprocal(tot, tot))
                    dve.tensor_tensor(part, part, spread(tot, 2, PAIR), ALU.mult).then_inc(probs, 1)
            for g in range(2):
                for m in range(2):
                    dve.wait_ge(summed, 2 * g + m + 1)
                    take(m, slice(HALF * g, HALF * g + HALF), T.bank[4 + 2 * g + m][0:Q, 0:HALF])

        @block.scalar
        def _(act):
            if softmax_scale:
                for g in range(2):
                    part = sm[:, per * g:per * g + per, :]
                    act.wait_ge(lowered, g + 1)
                    act.activation(part, part, ACT.Exp, scale=softmax_scale).then_inc(exps, 1)
                for g in range(2):
                    act.wait_ge(turned, g + 1)
                    act.copy(probs_t[:, per * g:per * g + per, :], cols(T.bank[2 + g][0:PAIR, 0:PAIR * per], per))\
                        .then_inc(turned_in, 1)


def head_attention(T, name, qk, v, vb, att, sparse):
    nc = T.nc
    H6, ROWS, GROUPS4 = 6, 3 * SEQ, 4
    NG = IMAGES * GROUPS4
    CH = NG // 2
    with ExitStack() as ctx:
        def sb(what, shape, dt=F32):
            return ctx.enter_context(nc.sbuf_tensor(f"{name}_{what}", shape, dt))

        sem = lambda what: T.sem(f"{name}_{what}")
        wide = sb("wide", [Q, 2, IMAGES, H6, SEQ])
        sc = sb("sc", [ROWS, NG, SEQ])
        kept = sb("kept", [ROWS, NG, SEQ])
        top8 = sb("top8", [ROWS, NG, 8])
        next8 = sb("next8", [ROWS, NG, 8])
        mx = sb("mx", [ROWS, NG])
        total = sb("total", [ROWS, NG])
        pt = sb("pt", [SEQ, IMAGES, HEADS * SEQ])
        spread_q, scored, sc_in, lowered, exps, probs, turned, pt_act, pt_dve, pv, pv_out, mixed, step = map(
            sem, ("spread_q", "scored", "sc_in", "lowered", "exps", "probs", "turned", "pt_act", "pt_dve", "pv",
                  "pv_out", "mixed", "dve_step"))
        block = ctx.enter_context(nc.Block())

        @block.tensor
        def _(pe):
            pe.wait_ge(spread_q, 2 * H6)
            for u in range(IMAGES // 2):
                for j in range(2):
                    b = 2 * u + j
                    for g in range(GROUPS4):
                        c, h = g // 2, 3 * (g % 2)
                        col = (j * GROUPS4 + g) * SEQ
                        mm = pe.matmul(T.bank[u][0:ROWS, col:col + SEQ], wide[:, c, b, h:h + 3, :].rearrange("p h q -> p (h q)"),
                                       qk[:, 2 + c, SEQ * b:SEQ * b + SEQ], start=True, stop=True)
                mm.then_inc(scored, 1)

            def turn(b):
                pe.wait_ge(probs, b // (IMAGES // 2) + 1)
                if b < 4:
                    pe.wait_ge(sc_in, 2 * 4)
                else:
                    pe.wait_ge(pt_act if b % 2 == 0 else pt_dve, (b - 4) // 2 + 1)
                for g in range(GROUPS4):
                    mm = pe.transpose(T.bank[b % 4][0:SEQ, ROWS * g:ROWS * g + ROWS], sc[:, GROUPS4 * b + g, :],
                                      T.p["ident"][0:ROWS, 0:ROWS])
                mm.then_inc(turned, 1)

            def apply(b):
                pe.wait_ge(pt_act if b % 2 == 0 else pt_dve, b // 2 + 1)
                if b >= 4:
                    pe.wait_ge(pv_out, b - 3)
                for c in range(2):
                    n = H6 * SEQ
                    mm = pe.matmul(T.bank[4 + b % 4][0:Q, n * c:n * c + n], v[:, b, Q * c:Q * c + Q],
                                   pt[:, b, n * c:n * c + n], start=True, stop=True)
                mm.then_inc(pv, 1)

            for b in range(IMAGES + 2):
                if b < IMAGES:
                    turn(b)
                if b >= 2:
                    apply(b - 2)

        @block.scalar
        def _(act):
            for c in range(2):
                for h in range(0, H6, 2):
                    act.activation(wide[:, c, :, h, :], cols(qk[:, c, :], IMAGES), ACT.Copy, scale=T.p["headmask"][:, h:h + 1])\
                        .then_inc(spread_q, 1)
            for u in range(IMAGES // 2):
                act.wait_ge(scored, u + 1)
                act.mul(sc[:, 8 * u:8 * u + 8, :], cols(T.bank[u][0:ROWS, 0:8 * SEQ], 8), HEAD_DIM ** -0.5)\
                    .then_inc(sc_in, 1)
            for g in range(2):
                act.wait_ge(lowered, g + 1)
                part = sc[:, CH * g:CH * g + CH, :]
                act.activation(part, part, ACT.Exp).then_inc(exps, 1)
            for b in range(0, IMAGES, 2):
                act.wait_ge(turned, b + 1)
                act.copy(pt[:, b, :], T.bank[b % 4][0:SEQ, 0:HEADS * SEQ]).then_inc(pt_act, 1)
            for c in range(2):
                act.wait_ge(mixed, c + 1)
                act.activation(att[:, c, :], att[:, c, :], ACT.Identity, bias=vb[:, c:c + 1])

        @block.vector
        def _(dve):
            for c in range(2):
                for h in range(1, H6, 2):
                    dve.tensor_scalar(wide[:, c, :, h, :], cols(qk[:, c, :], IMAGES), T.p["headmask"][:, h:h + 1], None, ALU.mult)\
                        .then_inc(spread_q, 1)
            link = chained(dve, step)
            for g in range(2):
                dve.wait_ge(sc_in, IMAGES // 4 * (g + 1))
                part = sc[:, CH * g:CH * g + CH, :]
                top = mx[:, CH * g:CH * g + CH]
                if sparse:
                    n = range(CH * g, CH * g + CH)
                    for i in n:
                        ins = dve.max(top8[:, i, :], sc[:, i, :])
                    link(ins)
                    for i in n:
                        ins = dve.match_replace(kept[:, i, :], top8[:, i, :], sc[:, i, :], -3.0e38)
                    link(ins)
                    for i in n:
                        ins = dve.max(next8[:, i, :], kept[:, i, :])
                    link(ins)
                    link(dve.tensor_copy(top, top8[:, CH * g:CH * g + CH, 0]))
                    link(dve.tensor_tensor(kept[:, CH * g:CH * g + CH, :], part,
                                           next8[:, CH * g:CH * g + CH, KEEP - 9:KEEP - 8].broadcast_to([ROWS, CH, SEQ]),
                                           ALU.is_ge))
                else:
                    link(dve.tensor_reduce(top, part, AX.X, ALU.max))
                dve.tensor_tensor(part, part, spread(top, 2, SEQ), ALU.subtract).then_inc(lowered, 1)
            for g in range(2):
                dve.wait_ge(exps, g + 1)
                part = sc[:, CH * g:CH * g + CH, :]
                tot = total[:, CH * g:CH * g + CH]
                if sparse:
                    link(dve.tensor_tensor(part, part, kept[:, CH * g:CH * g + CH, :], ALU.mult))
                link(dve.tensor_reduce(tot, part, AX.X, ALU.add))
                link(dve.reciprocal(tot, tot))
                dve.tensor_tensor(part, part, spread(tot, 2, SEQ), ALU.mult).then_inc(probs, 1)

            def own_heads(b):
                dve.wait_ge(pv, b + 1)
                got = T.bank[4 + b % 4][0:Q, 0:HEADS * SEQ].rearrange("p (c h q) -> p c h q", c=2, h=H6)
                mask = T.p["headmask"].unsqueeze(1).unsqueeze(3).broadcast_to([Q, 2, H6, SEQ])
                return dve.tensor_tensor(wide[:, :, b, :, :], got, mask, ALU.mult).then_inc(pv_out, 1)

            for b in range(1, IMAGES, 2):
                dve.wait_ge(turned, b + 1)
                dve.tensor_copy(pt[:, b, :], T.bank[b % 4][0:SEQ, 0:HEADS * SEQ]).then_inc(pt_dve, 1)
                if b >= 3:
                    own_heads(b - 3)
                    own_heads(b - 2)
            own_heads(IMAGES - 2)
            own_heads(IMAGES - 1)
            dve.wait_ge(pv_out, IMAGES)
            for c in range(2):
                dve.tensor_reduce(att[:, c, :].rearrange("p (b q) -> p b q", b=IMAGES),
                                  wide[:, c, :, :, :].rearrange("p b h q -> p b q h"), AX.X, ALU.add)\
                    .then_inc(mixed, 1)


def affine(T, name, jobs):
    nc = T.nc
    with nc.Block() as block:

        @block.vector
        def _(dve):
            for out, x, gb in jobs:
                for c in range(2):
                    dve.tensor_scalar(out[:, c, :], x[:, c, :], gb[:, c:c + 1], gb[:, 2 + c:3 + c], ALU.mult, ALU.add)


def residual(T, out, bias):
    def take(m, at, psum):
        return T.nc.vector.scalar_tensor_tensor(out[:, m, at], psum, bias[:, m:m + 1], out[:, m, at], ALU.add, ALU.add)
    return take


def biased(T, out, bias, func=ACT.Identity):
    def take(m, at, psum):
        return T.nc.scalar.activation(out[:, m, at], psum, func, bias=bias[:, m:m + 1])
    return take


def layer0_attention(T):
    nc, p = T.nc, T.p
    with ExitStack() as ctx:
        qk = ctx.enter_context(nc.sbuf_tensor("a0_qk", [Q, 4, TOKENS], F32))
        v = ctx.enter_context(nc.sbuf_tensor("a0_v", [PAIR, PAIRS, DIM], F32))
        att = ctx.enter_context(nc.sbuf_tensor("a0_att", [Q, 2, TOKENS], F32))
        w = cols(p["l0qkv"], 2)
        linear(T, "a0_qk_proj", 4, 2, lambda m, k: w[:, k, Q * m:Q * m + Q], lambda k, at: T.xn[:, k, at],
               by_act=biased(T, qk, p["l0qkvb"]))
        values_by_token(T, "a0_vals", T.xn, w[:, :, 2 * DIM:3 * DIM], v, PAIR)
        wide_attention(T, "a0_att", qk, v, DIM ** -0.5 / 3.0, None,
                       lambda m, at, psum: nc.vector.tensor_scalar(att[:, m, at], psum, p["l0qkvb"][:, 4 + m:5 + m],
                                                                   None, ALU.add))
        w2 = cols(p["l0proj"], 2)
        linear(T, "a0_proj", 2, 2, lambda m, k: w2[:, k, Q * m:Q * m + Q], lambda k, at: att[:, k, at],
               by_dve=residual(T, T.h, p["l0projb"]))


def layer1_attention(T):
    nc, p = T.nc, T.p
    with ExitStack() as ctx:
        qk = ctx.enter_context(nc.sbuf_tensor("a1_qk", [Q, 4, TOKENS], F32))
        v = ctx.enter_context(nc.sbuf_tensor("a1_v", [PAIR, PAIRS, DIM], F32))
        w = [cols(p["l1q"], 2), cols(p["l1k"], 2)]
        linear(T, "a1_qk_proj", 4, 2, lambda m, k: w[m // 2][:, k, Q * (m % 2):Q * (m % 2) + Q],
               lambda k, at: T.xn[:, k, at], by_act=biased(T, qk, p["l1qkb"]))
        values_by_token(T, "a1_vals", T.xn, cols(p["l1v"], 2), v, PAIR, bias=p["l1vb"])
        wide_attention(T, "a1_att", qk, v, None, DIM ** -0.5,
                       lambda m, at, psum: nc.vector.tensor_tensor(T.h[:, m, at], T.h[:, m, at], psum, ALU.add))


def layer1_block(T):
    nc, p = T.nc, T.p
    with ExitStack() as outer:
        x = T.xn
        res = outer.enter_context(nc.sbuf_tensor("b1_res", [Q, 2, TOKENS], F32))
        y = outer.enter_context(nc.sbuf_tensor("b1_y", [Q, 2, TOKENS], F32))
        bits = outer.enter_context(nc.sbuf_tensor("b1_bits", [128, 2, TOKENS], F32))
        layer_norm(T, "b1_ln", x, y)
        with ExitStack() as ctx:
            def sb(what, shape):
                return ctx.enter_context(nc.sbuf_tensor(f"b1_{what}", shape, F32))
            yr = sb("yr", [Q, 2, TOKENS])
            e = sb("e", [128, 1, TOKENS])
            g = sb("g", [128, IMAGES])
            gb = sb("gb", [128, 1, TOKENS])
            h1 = sb("h1", [128, 1, TOKENS])
            h2 = sb("h2", [64, 1, TOKENS])
            lg = sb("lg", [128, 4, TOKENS])
            affine(T, "b1_rln", [(yr, y, p["rln"])])
            win = cols(p["rin"], 2)
            linear(T, "b1_rin", 1, 2, lambda m, k: win[:, k, :], lambda k, at: yr[:, k, at],
                   by_act=biased(T, e, p["rinb"], ACT.Gelu), size=128)
            summed = T.sem("b1_summed")
            with nc.Block() as block:

                @block.vector
                def _(dve):
                    ev = e[:, 0, :].rearrange("p (b t) -> p b t", b=IMAGES)
                    dve.tensor_reduce(g[:, :], ev[:, :, 1:SEQ], AX.X, ALU.add).then_inc(summed, 1)
                    dve.wait_ge(summed, 1)
                    dve.tensor_scalar(gb[:, 0, :].rearrange("p (b t) -> p b t", b=IMAGES), spread(g[:, :], 2, SEQ),
                                      1.0 / (SEQ - 1), None, ALU.mult)
            wo1 = cols(p["ro1"], 2)
            linear(T, "b1_ro1", 1, 2, lambda m, k: wo1[:, k, :], lambda k, at: (e if k == 0 else gb)[:, 0, at],
                   by_act=biased(T, h1, p["ro1b"], ACT.Gelu), size=128)
            linear(T, "b1_ro2", 1, 1, lambda m, k: p["ro2"], lambda k, at: h1[:, 0, at],
                   by_act=biased(T, h2, p["ro2b"], ACT.Gelu), size=64)
            linear(T, "b1_ro3", 4, 1, lambda m, k: p["ro3"][:, m:m + 1].broadcast_to([64, 128]),
                   lambda k, at: h2[:, 0, at], by_act=biased(T, lg, p["ro3b"]), size=128)
            chosen = T.sem("b1_chosen")
            with nc.Block() as block:

                @block.vector
                def _(dve):
                    for b in range(2):
                        dve.tensor_tensor(bits[:, b, :], lg[:, 2 * b + 1, :], lg[:, 2 * b, :], ALU.is_gt)\
                            .then_inc(chosen, 1)
                    dve.wait_ge(chosen, 2)
                    for b in range(2):
                        dve.memset(bits[:, b, :].rearrange("p (b t) -> p b t", b=IMAGES)[:, :, 0:1], 1.0)
        with ExitStack() as ctx:
            def sb(what, shape):
                return ctx.enter_context(nc.sbuf_tensor(f"b1_{what}", shape, F32))
            xa = sb("xa", [Q, 2, TOKENS])
            qk = sb("qk", [Q, 4, TOKENS])
            v = sb("v", [SEQ, IMAGES, DIM])
            att = sb("att", [Q, 2, TOKENS])
            affine(T, "b1_ln1", [(xa, y, p["ln1"])])
            w = [cols(p["mq"], 2), cols(p["mk"], 2)]
            linear(T, "b1_qk", 4, 2, lambda m, k: w[m // 2][:, k, Q * (m % 2):Q * (m % 2) + Q],
                   lambda k, at: xa[:, k, at], by_act=biased(T, qk, p["mqkvb"]))
            values_by_token(T, "b1_vals", xa, cols(p["mv"], 2), v, SEQ)
            head_attention(T, "b1_att", qk, v, p["mqkvb"][:, 4:6], att, False)
            wo = cols(p["mo"], 2)
            linear(T, "b1_wo", 2, 2, lambda m, k: wo[:, k, Q * m:Q * m + Q], lambda k, at: att[:, k, at],
                   by_dve=lambda m, at, psum: nc.vector.scalar_tensor_tensor(
                       res[:, m, at], psum, p["mob"][:, m:m + 1], bits[0:Q, 0, at], ALU.add, ALU.mult))
        add_into(T, res, x)
        with ExitStack() as ctx:
            def sb(what, shape):
                return ctx.enter_context(nc.sbuf_tensor(f"b1_{what}", shape, F32))
            xf = sb("xf", [Q, 2, TOKENS])
            mid = sb("mid", [128, 6, TOKENS])
            ff = sb("ff", [Q, 2, TOKENS])
            layer_norm(T, "b1_lnf", res, y)
            affine(T, "b1_ln2", [(xf, y, p["ln2"])])
            w1, w2 = cols(p["fc1"], 2), cols(p["fc2"], 6)
            linear(T, "b1_fc1", 6, 2, lambda m, k: w1[:, k, 128 * m:128 * m + 128], lambda k, at: xf[:, k, at],
                   by_act=biased(T, mid, p["fc1b"], ACT.Gelu), size=128)
            linear(T, "b1_fc2", 2, 6, lambda m, k: w2[:, k, Q * m:Q * m + Q], lambda k, at: mid[:, k, at],
                   by_dve=lambda m, at, psum: nc.vector.scalar_tensor_tensor(
                       ff[:, m, at], psum, p["fc2b"][:, m:m + 1], bits[0:Q, 1, at], ALU.add, ALU.mult))
            add_into(T, res, ff)
        with ExitStack() as ctx:
            def sb(what, shape):
                return ctx.enter_context(nc.sbuf_tensor(f"b1_{what}", shape, F32))
            sel = sb("sel", [128, 2, TOKENS])
            inv = sb("inv", [128, 2, TOKENS])
            d01 = sb("d01", [128, TOKENS])
            d2 = sb("d2", [64, TOKENS])
            step = T.sem("b1_sel_step")
            with nc.Block() as block:

                @block.vector
                def _(dve):
                    link = chained(dve, step)
                    link(dve.tensor_scalar(inv[:, :, :], bits[:, :, :], -1.0, 1.0, ALU.mult, ALU.add))
                    dve.tensor_tensor(sel[0:64, 0, :], inv[0:64, 0, :], inv[0:64, 1, :], ALU.mult)
                    dve.tensor_tensor(sel[64:128, 0, :], inv[64:128, 0, :], bits[64:128, 1, :], ALU.mult)
                    dve.tensor_tensor(sel[0:64, 1, :], bits[0:64, 0, :], inv[0:64, 1, :], ALU.mult)
            down = cols(p["ldown"], 2)
            linear(T, "b1_down01", 1, 2, lambda m, k: down[:, k, 0:128], lambda k, at: res[:, k, at],
                   by_dve=lambda m, at, psum: nc.vector.tensor_tensor(d01[:, at], psum, sel[:, 0, at], ALU.mult),
                   size=128)
            linear(T, "b1_down2", 1, 2, lambda m, k: down[:, k, 128:192], lambda k, at: res[:, k, at],
                   by_dve=lambda m, at, psum: nc.vector.tensor_tensor(d2[:, at], psum, sel[0:64, 1, at], ALU.mult),
                   size=64)
            linear(T, "b1_up", 2, 2, lambda m, k: (p["lup01"] if k == 0 else p["lup2"])[:, Q * m:Q * m + Q],
                   lambda k, at: (d01 if k == 0 else d2)[:, at],
                   by_dve=lambda m, at, psum: nc.vector.tensor_tensor(res[:, m, at], res[:, m, at], psum, ALU.add))
            add_into(T, T.h, res)


def add_into(T, out, x):
    with T.nc.Block() as block:

        @block.vector
        def _(dve):
            dve.tensor_tensor(out[:, :, :], out[:, :, :], x[:, :, :], ALU.add)


def selective_scan(T):
    nc, p = T.nc, T.p
    FLAT = 2 * TOKENS
    with ExitStack() as ctx:
        def sb(what, shape):
            return ctx.enter_context(nc.sbuf_tensor(f"ssm_{what}", shape, F32))

        sem = lambda what: T.sem(f"ssm_{what}")
        pre, mag, delta = sb("pre", [Q, 2, TOKENS]), sb("mag", [Q, 2, TOKENS]), sb("delta", [Q, 2, TOKENS])
        inv_a = [sb(f"inv_a{i}", [Q, 2]) for i in range(2)]
        yacc = sb("y", [Q, FLAT])
        wbc = [sb(f"wbc{i}", [Q, 4 * DIM + 2]) for i in range(2)]
        decay = [sb(f"decay{i}", [Q, FLAT]) for i in range(2)]
        bsel = [sb(f"bsel{i}", [Q, FLAT]) for i in range(2)]
        drive = [sb(f"drive{i}", [Q, FLAT]) for i in range(2)]
        bx = [sb(f"bx{i}", [Q, FLAT]) for i in range(2)]
        state = [sb(f"state{i}", [Q, FLAT]) for i in range(2)]
        out = [sb(f"out{i}", [Q, FLAT]) for i in range(2)]
        wd = cols(p["sD"], 2)
        linear(T, "ssm_delta", 2, 2, lambda m, k: wd[:, k, Q * m:Q * m + Q], lambda k, at: T.xn[:, k, at],
               by_act=biased(T, pre, p["sDb"]))
        soft = sem("soft")
        with nc.Block() as block:

            @block.scalar
            def _(act):
                link = chained(act, soft)
                link(act.activation(mag[:, :, :], pre[:, :, :], ACT.Abs))
                link(act.activation(mag[:, :, :], mag[:, :, :], ACT.Exp, scale=-1.0))
                link(act.activation(mag[:, :, :], mag[:, :, :], ACT.Ln, bias=1.0))

            @block.vector
            def _(dve):
                dve.memset(yacc[:, :], 0.0)
                dve.wait_ge(soft, 3)
                dve.scalar_tensor_tensor(delta[:, :, :], pre[:, :, :], 0.0, mag[:, :, :], ALU.max, ALU.add)
        loaded = [sem(f"loaded{i}") for i in range(2)]
        inverted, b_made, c_made, decayed, b_out, driven, bx_made, scanned, read_out, added, reset = map(
            sem, ("inverted", "b_made", "c_made", "decayed", "b_out", "driven", "bx_made", "scanned", "read_out", "added", "reset"))
        block = ctx.enter_context(nc.Block())

        @block.sync
        def _(sp):
            sp.sem_inc(c_made, 8)
            sp.sem_inc(b_out, 8)
            sp.wait_ge(b_out, 8)
            with sp.Fori(0, STATES // 2) as i:
                for j in range(2):
                    sp.wait_ge(c_made, 8 * i + 4 * j + 4)
                    sp.wait_ge(b_out, 8 * i + 4 * j + 4)
                    sp.dma_start(wbc[j][:, :],
                                 T.dram["wBC"][bass.ds(2 * i + j, 1), :, :].rearrange("n p m -> (n p) m"))\
                        .then_inc(loaded[j], 16)

        @block.tensor
        def _(pe):
            pe.sem_inc(read_out, 4)
            with pe.Fori(0, STATES // 2) as i:
                for j in range(2):
                    pe.wait_ge(loaded[j], 16 * i + 16)
                    for a in range(2):
                        for u in range(4):
                            c, s = u // 2, HALF * (u % 2)
                            if a:
                                pe.wait_ge(read_out, 8 * i + 4 * j + u + 1)
                            else:
                                pe.wait_ge(b_out, 8 * i + 4 * j + u + 5)
                            for k in range(2):
                                mm = pe.matmul(T.bank[4 * a + u][0:Q, 0:HALF], wbc[j][:, DIM * (2 * a + k) + Q * c:DIM * (2 * a + k) + Q * c + Q],
                                               T.xn[:, k, s:s + HALF], start=(k == 0), stop=(k == 1))
                            mm.then_inc(c_made if a else b_made, 1)

        @block.scalar
        def _(act):
            act.sem_inc(scanned, 2)
            act.sem_inc(driven, 2)
            with act.Fori(0, STATES // 2) as i:
                for j in range(2):
                    act.wait_ge(scanned, 2 * i + j + 1)
                    act.wait_ge(loaded[j], 16 * i + 16)
                    for c in range(2):
                        act.activation(decay[j][:, TOKENS * c:TOKENS * c + TOKENS], delta[:, c, :], ACT.Exp,
                                       scale=wbc[j][:, 4 * DIM + c:4 * DIM + c + 1]).then_inc(decayed, 1)
                    act.wait_ge(driven, 2 * i + j + 1)
                    act.wait_ge(inverted, 2 * i + j + 1)
                    for u in range(4):
                        c, s = u // 2, HALF * (u % 2)
                        act.wait_ge(b_made, 8 * i + 4 * j + u + 1)
                        act.activation(bsel[j][:, HALF * u:HALF * u + HALF], T.bank[u][0:Q, 0:HALF], ACT.Copy,
                                       scale=inv_a[j][:, c:c + 1]).then_inc(b_out, 1)

        @block.gpsimd
        def _(pool):
            xflat = T.xn[:, :, :].rearrange("p c t -> p (c t)")
            with pool.Fori(0, STATES // 2) as i:
                for j in range(2):
                    pool.wait_ge(driven, 2 * i + j + 3)
                    pool.tensor_tensor(bx[j][:, :], drive[j][:, :], xflat, ALU.mult).then_inc(bx_made, 1)

        @block.vector
        def _(dve):
            dve.sem_inc(bx_made, 1)
            with dve.Fori(0, STATES // 2) as i:
                for j in range(2):
                    n = 2 * i + j
                    dve.wait_ge(loaded[j], 16 * i + 16)
                    dve.reciprocal(inv_a[j][:, :], wbc[j][:, 4 * DIM:4 * DIM + 2]).then_inc(inverted, 1)
                    dve.wait_ge(decayed, 4 * i + 2 * j + 2)
                    dve.wait_ge(b_out, 8 * i + 4 * j + 12)
                    dve.scalar_tensor_tensor(drive[j][:, :], decay[j][:, :], 1.0, bsel[j][:, :], ALU.subtract, ALU.mult)\
                        .then_inc(driven, 1)
                    dve.wait_ge(driven, n + 3)
                    first = decay[j][:, :].rearrange("p (b t) -> p b t", t=SEQ)[:, :, 0:1]
                    dve.memset(first, 0.0).then_inc(reset, 1)
                    dve.wait_ge(reset, n + 1)
                    dve.wait_ge(bx_made, n + 2)
                    dve.tensor_tensor_scan(state[j][:, :], decay[j][:, :], bx[j][:, :], 0.0, ALU.mult, ALU.add)\
                        .then_inc(scanned, 1)
                    dve.wait_ge(scanned, n + 3)
                    for u in range(4):
                        at = slice(HALF * u, HALF * u + HALF)
                        dve.wait_ge(c_made, 8 * i + 4 * j + u + 9)
                        dve.tensor_tensor(out[j][:, at], state[j][:, at], T.bank[4 + u][0:Q, 0:HALF], ALU.mult)\
                            .then_inc(read_out, 1)
                    dve.wait_ge(read_out, 8 * i + 4 * j + 8)
                    dve.tensor_tensor(yacc[:, :], yacc[:, :], out[j][:, :], ALU.add).then_inc(added, 1)
                    dve.wait_ge(added, n + 1)
            dve.tensor_tensor(T.h[:, :, :].rearrange("p c t -> p (c t)"), T.h[:, :, :].rearrange("p c t -> p (c t)"),
                              yacc[:, :], ALU.add)


def experts(T, key):
    nc, m = T.nc, MOE[key]
    K, B, N = m["top"], m["blocks"], m["width"] // m["chunks"]
    C = m["chunks"] * m["shared"]
    with ExitStack() as ctx:
        def sb(what, shape, dt=F32):
            return ctx.enter_context(nc.sbuf_tensor(f"{key}_{what}", shape, dt))

        weight = sb("weight", [TILE, TILES, K])
        slot = sb("slot", [TILE, K, TILES], U32)
        fetch = sb("fetch", [TILE, K, TILES], U32)
        plan = sb("plan", [1, B + 2], U32)
        shared_in = T.sem(f"{key}_shared_in")
        with ExitStack() as inner:
            first, second = T.dram[f"{key}s1"], T.dram[f"{key}s2"]
            s1 = inner.enter_context(nc.sbuf_tensor(f"{key}_s1", list(first.shape), F32))
            s2 = inner.enter_context(nc.sbuf_tensor(f"{key}_s2", list(second.shape), F32))

            def meanwhile(sp):
                sp.dma_start(s1[:, :], first).then_inc(shared_in, 16)
                sp.dma_start(s2[:, :], second).then_inc(shared_in, 16)
                sp.wait_ge(T.loaded[f"{key}a"], 16)
                sp.wait_ge(T.zeroed, 16 * sum(-(-x["blocks"] // 12) for x in MOE.values()))
                sp.wait_ge(shared_in, 32)

            layer_norm(T, f"{key}f_ln", T.h, T.xn, meanwhile)
            route(T, key, weight, slot, fetch, plan, s1, s2)
        run_blocks(T, key, T.rows[key], plan)
        combine(T, key, T.rows[key], weight, fetch)


def route(T, key, weight, slot, fetch, plan, s1, s2):
    nc, p, m = T.nc, T.p, MOE[key]
    E, K, B, CAP = m["experts"], m["top"], m["blocks"], m["cap"]
    N = m["width"] // m["chunks"]
    C = m["chunks"] * m["shared"]
    normed = key == "L3"
    HT = TILES // 2
    rows = T.rows[key]
    BIG = float(2 ** 20)
    RING = 5
    parts = 1 if normed else 2
    units = [(f, s, a) for f in range(C) for s in range(2) for a in range(parts)]
    with ExitStack() as ctx:
        def sb(what, shape, dt=F32):
            return ctx.enter_context(nc.sbuf_tensor(f"{key}_{what}", shape, dt))

        sem = lambda what: T.sem(f"{key}_{what}")
        xt = sb("xt", [TILE, TILES, DIM])
        value = sb("value", [TILE, TILES, E])
        choice = sb("choice", [TILE, TILES, E]) if key == "L2" else value
        best, best_at, at_f = sb("best", [TILE, TILES, 8]), sb("best_at", [TILE, TILES, 8], U32), sb("at_f", [TILE, TILES, 8])
        one_hot = sb("one_hot", [TILE, K, TILES, E])
        prod = sb("prod", [TILE, TILES, E])
        before = sb("before_tile", [TILE, TILES + 1, E])
        mask = sb("mask", [TILE, TILES, E])
        row_of, late = sb("row_of", [TILE, TILES, E]), sb("late", [TILE, TILES, E])
        stat = sb("stat", [TILE, TILES])
        k_row, k_w, keep, k_spare = (sb(x, [TILE, K, TILES]) for x in ("k_row", "k_w", "keep", "k_spare"))
        count, over, nblk, first, last = sb("count", [128, 1]), sb("over", [128, TILES]), sb("nblk", [128, 1]), sb("first", [128, 1]), sb("last", [128, 1])
        member, member2 = sb("member", [128, B]), sb("member2", [128, B])
        start_row = sb("start_row", [TILE, E])
        hid = sb("s_hid", [N, C, TOKENS])
        upv = sb("s_up", [N, C, TOKENS]) if not normed else sb("s_xc", [N, C, TOKENS])
        if normed:
            stat_s, eps = sb("s_stat", [N, 2, HALF]), sb("s_eps", [128, 1])
            mean_made, mean_in, centred, squared, var_made, dev_in, inverted, scaled, eps_set = map(
                sem, ("s_mean_made", "s_mean_in", "s_centred", "s_squared", "s_var_made", "s_dev_in", "s_inverted",
                      "s_scaled", "s_eps_set"))
        (x_turned, xt_in, logits_made, scored, soft, masked, located, counted, blocks_known, starts_made, members,
         planned, step, s_made, s_out, s_hidden, s_down, slots_known, scattered) = map(
            sem, ("x_turned", "xt_in", "logits_made", "scored", "soft", "masked", "located", "counted", "blocks_known",
                  "starts_made", "members", "planned", "dve_step", "s_made", "s_out", "s_hidden", "s_down",
                  "slots_known", "scattered"))
        block = ctx.enter_context(nc.Block())
        w = cols(p[f"{key}gate"], 2)
        w1 = cols(s1[:, :], 2)
        w2 = cols(s2[:, 0:C * DIM], C)
        WIDE = C * N

        @block.tensor
        def _(pe):
            for g in range(2):
                for j in range(HT):
                    i = HT * g + j
                    for c in range(2):
                        mm = pe.matmul(T.bank[g][0:TILE, E * j:E * j + E], T.xn[:, c, TILE * i:TILE * i + TILE],
                                       w[:, c, :], start=(c == 0), stop=(c == 1))
                mm.then_inc(logits_made, 1)
            for i in range(TILES):
                for c in range(2):
                    mm = pe.transpose(T.bank[5 + i // 2][0:TILE, DIM * (i % 2) + Q * c:DIM * (i % 2) + Q * c + Q],
                                      T.xn[:, c, TILE * i:TILE * i + TILE], p["ident"][0:Q, 0:Q])
                if i % 2:
                    mm.then_inc(x_turned, 1)

            def shared_units(a, b):
                for u in range(a, min(b, len(units))):
                    f, s, part = units[u]
                    if 2 <= u < RING:
                        pe.wait_ge(xt_in, u - 1)
                    if u >= RING:
                        pe.wait_ge(s_out, u - RING + 1)
                    for c in range(2):
                        mm = pe.matmul(T.bank[3 + u % RING][0:N, 0:HALF],
                                       w1[:, c, WIDE * part + N * f:WIDE * part + N * f + N],
                                       T.xn[:, c, HALF * s:HALF * s + HALF], start=(c == 0), stop=(c == 1))
                    mm.then_inc(s_made, 1)

            def positions():
                pe.wait_ge(masked, 1)
                pe.matmul(T.bank[2][0:E, 0:1], before[:, TILES, :], p["ones"][0:TILE, 0:1], start=True, stop=True)\
                    .then_inc(counted, 1)
                for g in range(2):
                    for j in range(HT):
                        i = HT * g + j
                        pe.matmul(T.bank[g][0:TILE, E * j:E * j + E], p["ones"][0:TILE, 0:TILE], before[:, i, :],
                                  start=True, stop=False)
                        mm = pe.matmul(T.bank[g][0:TILE, E * j:E * j + E], p["before"][0:TILE, 0:TILE], mask[:, i, :],
                                       start=False, stop=True)
                    mm.then_inc(located, 1)

            def starts():
                pe.wait_ge(blocks_known, 1)
                pe.matmul(T.bank[2][0:TILE, 0:E], nblk[0:E, 0:1].broadcast_to([E, TILE]), p["before"][0:E, 0:E],
                          start=True, stop=True)
                pe.matmul(T.bank[2][0:E, 128:129], p["before"][0:E, 0:E], nblk[0:E, 0:1], start=True, stop=True)\
                    .then_inc(starts_made, 1)

            def plans():
                pe.wait_ge(members, 1)
                pe.matmul(T.bank[2][0:1, 0:B], p["ecol"][0:E, 0:1], member[0:E, :], start=True, stop=True)
                pe.matmul(T.bank[2][0:1, B:B + 1], p["ones"][0:E, 0:1], nblk[0:E, 0:1], start=True, stop=True)\
                    .then_inc(planned, 1)

            half = len(units) // 2
            shared_units(0, half)
            positions()
            shared_units(half, half + 2)
            starts()
            shared_units(half + 2, half + 4)
            plans()
            shared_units(half + 4, len(units))
            if normed:
                for s in range(2):
                    pe.wait_ge(s_out, len(units))
                    for f in range(C):
                        mm = pe.matmul(T.bank[3 + s][0:N, 0:HALF], p["mean384"], hid[:, f, HALF * s:HALF * s + HALF],
                                       start=(f == 0), stop=(f == C - 1))
                    mm.then_inc(mean_made, 1)
                for s in range(2):
                    pe.wait_ge(squared, s + 1)
                    for f in range(C):
                        mm = pe.matmul(T.bank[3 + s][0:N, 0:HALF], p["mean384"], hid[:, f, HALF * s:HALF * s + HALF],
                                       start=(f == 0), stop=(f == C - 1))
                    mm.then_inc(var_made, 1)
            for u in range(4):
                mo, s = u // 2, u % 2
                if u < 2:
                    pe.wait_ge(s_hidden, 2 * C if not normed else 2)
                for f in range(C):
                    mm = pe.matmul(T.bank[4 + u][0:Q, 0:HALF], w2[:, f, Q * mo:Q * mo + Q],
                                   upv[:, f, HALF * s:HALF * s + HALF], start=(f == 0), stop=(f == C - 1))
                mm.then_inc(s_down, 1)

        @block.scalar
        def _(act):
            if key == "L2":
                for g in range(2):
                    act.wait_ge(logits_made, g + 1)
                    act.activation(value[:, HT * g:HT * g + HT, :], cols(T.bank[g][0:TILE, 0:HT * E], HT), ACT.Sigmoid)\
                        .then_inc(soft, 1)
            for u in range(TILES // 2):
                act.wait_ge(x_turned, u + 1)
                act.copy(xt[:, 2 * u:2 * u + 2, :], cols(T.bank[5 + u][0:TILE, 0:2 * DIM], 2)).then_inc(xt_in, 1)
            if key != "L2":
                act.wait_ge(scored, 1)
                act.activation(value[:, :, :], value[:, :, :], ACT.Exp).then_inc(soft, 1)
            for u, (f, s, part) in enumerate(units):
                at = slice(HALF * s, HALF * s + HALF)
                act.wait_ge(s_made, u + 1)
                got = T.bank[3 + u % RING][0:N, 0:HALF]
                if normed:
                    act.activation(hid[:, f, at], got, ACT.Gelu, bias=s2[:, C * DIM + f:C * DIM + f + 1]).then_inc(s_out, 1)
                elif part == 0:
                    act.activation(hid[:, f, at], got, ACT.Silu).then_inc(s_out, 1)
                else:
                    act.copy(upv[:, f, at], got).then_inc(s_out, 1)
            if normed:
                act.wait_ge(eps_set, 1)
                for s in range(2):
                    act.wait_ge(mean_made, s + 1)
                    act.copy(stat_s[:, s, :], T.bank[3 + s][0:N, 0:HALF]).then_inc(mean_in, 1)
                for s in range(2):
                    at = slice(HALF * s, HALF * s + HALF)
                    act.wait_ge(centred, s + 1)
                    act.activation(hid[:, :, at], upv[:, :, at], ACT.Square).then_inc(squared, 1)
                for s in range(2):
                    act.wait_ge(var_made, s + 1)
                    act.activation(stat_s[:, s, :], T.bank[3 + s][0:N, 0:HALF], ACT.Sqrt, bias=eps[0:N, 0:1]).then_inc(dev_in, 1)
                for s in range(2):
                    at = slice(HALF * s, HALF * s + HALF)
                    act.wait_ge(scaled, s + 1)
                    for f in range(C):
                        gain = C * DIM + C + f
                        ins = act.activation(upv[:, f, at], hid[:, f, at], ACT.Identity, scale=s2[:, gain:gain + 1],
                                             bias=s2[:, gain + C:gain + C + 1])
                    ins.then_inc(s_hidden, 1)

        @block.gpsimd
        def _(pool):
            if not normed:
                for f in range(C):
                    for s in range(2):
                        at = slice(HALF * s, HALF * s + HALF)
                        pool.wait_ge(s_out, 2 * (2 * f + s) + 2)
                        pool.tensor_tensor(upv[:, f, at], hid[:, f, at], upv[:, f, at], ALU.mult).then_inc(s_hidden, 1)
            else:
                for s in range(2):
                    at = slice(HALF * s, HALF * s + HALF)
                    pool.wait_ge(mean_in, s + 1)
                    pool.tensor_tensor(upv[:, :, at], hid[:, :, at], spread(stat_s[:, s, :], 1, C), ALU.subtract)\
                        .then_inc(centred, 1)
                for s in range(2):
                    at = slice(HALF * s, HALF * s + HALF)
                    pool.wait_ge(inverted, s + 1)
                    pool.tensor_tensor(hid[:, :, at], upv[:, :, at], spread(stat_s[:, s, :], 1, C), ALU.mult)\
                        .then_inc(scaled, 1)
            pool.wait_ge(xt_in, TILES // 2)
            pool.wait_ge(slots_known, 1)
            for k in range(K):
                for i in range(TILES):
                    pool.indirect_dma_start(rows[:, :], bass.IndirectOffsetOnAxis(ap=slot[:, k, i:i + 1], axis=0),
                                            xt[:, i, :], None).then_inc(scattered, 16)
            pool.wait_ge(scattered, 16 * K * TILES)

        @block.vector
        def _(dve):
            link = chained(dve, step)
            if normed:
                dve.memset(eps[:, :], EPS).then_inc(eps_set, 1)
            gate_bias = p[f"{key}gateb"]
            if key == "L2":
                dve.wait_ge(soft, 2)
                link(dve.tensor_tensor(choice[:, :, :], value[:, :, :], spread(gate_bias, 1, TILES), ALU.add))
            else:
                for g in range(2):
                    dve.wait_ge(logits_made, g + 1)
                    link(dve.tensor_tensor(value[:, HT * g:HT * g + HT, :], cols(T.bank[g][0:TILE, 0:HT * E], HT),
                                           spread(gate_bias, 1, HT), ALU.add))
                if key == "L3":
                    link(dve.memset(value[:, :, 0:1], -1.0e9))
                link(dve.tensor_reduce(stat[:, :], value[:, :, :], AX.X, ALU.max))
                dve.tensor_tensor(value[:, :, :], value[:, :, :], spread(stat[:, :], 2, E), ALU.subtract)\
                    .then_inc(scored, 1)
                dve.wait_ge(soft, 1)
                link(dve.tensor_reduce(stat[:, :], value[:, :, :], AX.X, ALU.add))
                link(dve.reciprocal(stat[:, :], stat[:, :]))
                link(dve.tensor_tensor(value[:, :, :], value[:, :, :], spread(stat[:, :], 2, E), ALU.mult))
            for i in range(TILES):
                ins = dve.max(best[:, i, :], choice[:, i, :])
            link(ins)
            for i in range(TILES):
                ins = dve.max_index(best_at[:, i, :], best[:, i, :], choice[:, i, :])
            link(ins)
            link(dve.tensor_copy(at_f[:, :, :], best_at[:, :, :]))
            for k in range(K):
                ins = dve.tensor_tensor(one_hot[:, k, :, :], spread(p["iota"][0:TILE, 0:E], 1, TILES),
                                        at_f[:, :, k:k + 1].broadcast_to([TILE, TILES, E]), ALU.is_equal)
            link(ins)
            link(dve.tensor_tensor(mask[:, :, :], one_hot[:, 0, :, :], one_hot[:, 1, :, :], ALU.add))
            for k in range(2, K):
                link(dve.tensor_tensor(mask[:, :, :], mask[:, :, :], one_hot[:, k, :, :], ALU.add))
            link(dve.memset(before[:, 0, :], 0.0))
            for i in range(TILES):
                link(dve.tensor_tensor(before[:, i + 1, :], before[:, i, :], mask[:, i, :], ALU.add))
            dve.sem_inc(masked, 1)
            if key == "L2":
                for k in range(K):
                    link(dve.tensor_tensor(prod[:, :, :], one_hot[:, k, :, :], value[:, :, :], ALU.mult))
                    link(dve.tensor_reduce(k_w[:, k, :], prod[:, :, :], AX.X, ALU.add))
            else:
                link(dve.tensor_copy(k_w[:, :, :], best[:, :, 0:K].rearrange("p i k -> p k i")))
            if key != "L3":
                link(dve.tensor_reduce(stat[:, :], k_w[:, :, :].rearrange("p k i -> p i k"), AX.X, ALU.add))
                if key == "L2":
                    link(dve.tensor_scalar(stat[:, :], stat[:, :], 1e-20, None, ALU.add))
                link(dve.reciprocal(stat[:, :], stat[:, :]))
                link(dve.tensor_tensor(k_w[:, :, :], k_w[:, :, :], spread(stat[:, :], 1, K), ALU.mult))
                if key == "L2":
                    link(dve.tensor_scalar(k_w[:, :, :], k_w[:, :, :], 2.5, None, ALU.mult))
            dve.wait_ge(counted, 1)
            link(dve.tensor_scalar(count[0:E, :], T.bank[2][0:E, 0:1], float(CAP), None, ALU.min))
            link(dve.tensor_tensor(over[0:E, :], count[0:E, 0:1].broadcast_to([E, TILES]), p["levels"][0:E, :], ALU.is_gt))
            dve.tensor_reduce(nblk[0:E, :], over[0:E, :], AX.X, ALU.add).then_inc(blocks_known, 1)
            dve.wait_ge(starts_made, 1)
            link(dve.tensor_scalar(start_row[:, :], T.bank[2][0:TILE, 0:E], float(TILE), None, ALU.mult))
            link(dve.tensor_copy(first[0:E, :], T.bank[2][0:E, 128:129]))
            link(dve.tensor_tensor(last[0:E, :], first[0:E, :], nblk[0:E, :], ALU.add))
            link(dve.tensor_scalar(member[0:E, :], p["iota"][0:E, 0:B], first[0:E, 0:1], None, ALU.is_ge))
            link(dve.tensor_scalar(member2[0:E, :], p["iota"][0:E, 0:B], last[0:E, 0:1], None, ALU.is_lt))
            dve.tensor_tensor(member[0:E, :], member[0:E, :], member2[0:E, :], ALU.mult).then_inc(members, 1)
            for g in range(2):
                dve.wait_ge(located, g + 1)
                at = slice(HT * g, HT * g + HT)
                got = cols(T.bank[g][0:TILE, 0:HT * E], HT)
                link(dve.tensor_tensor(row_of[:, at, :], got, spread(start_row[:, :], 1, HT), ALU.add))
                if CAP < TOKENS:
                    link(dve.tensor_scalar(late[:, at, :], got, float(CAP), BIG, ALU.is_ge, ALU.mult))
                    link(dve.tensor_tensor(row_of[:, at, :], row_of[:, at, :], late[:, at, :], ALU.add))
            for k in range(K):
                link(dve.tensor_tensor(prod[:, :, :], one_hot[:, k, :, :], row_of[:, :, :], ALU.mult))
                link(dve.tensor_reduce(k_row[:, k, :], prod[:, :, :], AX.X, ALU.add))
            link(dve.tensor_scalar(keep[:, :, :], k_row[:, :, :], BIG, None, ALU.is_lt))
            link(dve.tensor_tensor(weight[:, :, :], k_w[:, :, :].rearrange("p k i -> p i k"),
                                   keep[:, :, :].rearrange("p k i -> p i k"), ALU.mult))
            link(dve.tensor_tensor(k_row[:, :, :], k_row[:, :, :], keep[:, :, :], ALU.mult))
            link(dve.tensor_copy(fetch[:, :, :], k_row[:, :, :]))
            link(dve.tensor_scalar(keep[:, :, :], keep[:, :, :], -1.0, 1.0, ALU.mult, ALU.add))
            link(dve.tensor_scalar(k_spare[:, :, :], cols(p["spare"], 6)[:, 0:K, :], float(B * TILE), None, ALU.add))
            link(dve.tensor_tensor(k_spare[:, :, :], k_spare[:, :, :], keep[:, :, :], ALU.mult))
            link(dve.tensor_tensor(k_row[:, :, :], k_row[:, :, :], k_spare[:, :, :], ALU.add))
            dve.tensor_copy(slot[:, :, :], k_row[:, :, :]).then_inc(slots_known, 1)
            dve.wait_ge(planned, 1)
            dve.tensor_copy(plan[0:1, 0:B + 1], T.bank[2][0:1, 0:B + 1])
            if normed:
                for s in range(2):
                    dve.wait_ge(dev_in, s + 1)
                    dve.reciprocal(stat_s[:, s, :], stat_s[:, s, :]).then_inc(inverted, 1)
            for u in range(4):
                mo, s = u // 2, u % 2
                at = slice(HALF * s, HALF * s + HALF)
                dve.wait_ge(s_down, u + 1)
                got = T.bank[4 + u][0:Q, 0:HALF]
                if normed:
                    dve.scalar_tensor_tensor(T.h[:, mo, at], got, p["L3b2v"][:, mo:mo + 1], T.h[:, mo, at], ALU.add, ALU.add)
                else:
                    dve.tensor_tensor(T.h[:, mo, at], T.h[:, mo, at], got, ALU.add)


def run_blocks(T, key, rows, plan):
    nc, p, m = T.nc, T.p, MOE[key]
    B, I, C = m["blocks"], m["width"], m["chunks"]
    N = I // C
    normed = key == "L3"
    w1_d, w2_d = T.dram[f"{key}w1"], T.dram[f"{key}w2"]
    W1, W2 = w1_d.shape[2], w2_d.shape[2]
    EXPERTS = w1_d.shape[0]
    with ExitStack() as ctx:
        def sb(what, shape, n=2):
            return [ctx.enter_context(nc.sbuf_tensor(f"{key}_{what}{j}", shape, F32)) for j in range(n)]

        sem = lambda what: T.sem(f"{key}_{what}")
        w1, w2, xr, xt, hid, act_out, y = (sb("w1", [Q, W1], 4), sb("w2", [N, W2], 4), sb("xr", [TILE, DIM], 4), sb("xtb", [Q, 2, TILE]),
                                           sb("hid", [N, C, TILE]), sb("act", [N, C, TILE]), sb("yb", [TILE, DIM]))
        if normed:
            sq, sd, yb2 = sb("sq", [N, C, TILE]), sb("sd", [N, TILE]), sb("b2", [1, DIM], 4)
            eps = ctx.enter_context(nc.sbuf_tensor(f"{key}_eps", [128, 1], F32))
        loaded = [sem(f"loaded{j}") for j in range(4)]
        stored = [sem(f"stored{j}") for j in range(2)]
        turned, xt_in, gate, up, acted, hidden, down, y_in = map(
            sem, ("turned", "xtb_in", "gate", "up", "acted", "hidden", "down", "y_in"))
        means, centred, squared, variances, deviated, inverted, scaled, eps_set = map(
            sem, ("means", "centred", "squared", "variances", "deviated", "inverted", "scaled", "eps_set"))
        all_stored = sem("all_stored")
        loads = 64 if normed else 48
        block = ctx.enter_context(nc.Block())

        def blocks_in_use(eng):
            return eng.value_load(plan[0:1, B:B + 1], min_val=1, max_val=B)

        @block.sync
        def _(sp):
            sp.sem_inc(down, 4)
            n = blocks_in_use(sp)
            with sp.Fori(0, B // 4) as i:
              for h in range(2):
                with sp.If(4 * i + 2 * h < n):
                    for j in range(2):
                        b = 4 * i + 2 * h + j
                        e = sp.value_load(plan[0:1, bass.ds(b, 1)], min_val=0, max_val=EXPERTS - 1)
                        sp.wait_ge(down, b + 1)
                        sp.dma_start(xr[2 * h + j][:, :], rows[bass.ds(b * TILE, TILE), :]).then_inc(loaded[2 * h + j], 16)
                        sp.dma_start(w1[2 * h + j][:, :], w1_d[bass.ds(e, 1), :, :].rearrange("e p n -> (e p) n"))\
                            .then_inc(loaded[2 * h + j], 16)
                        sp.dma_start(w2[2 * h + j][:, :], w2_d[bass.ds(e, 1), :, :].rearrange("e p n -> (e p) n"))\
                            .then_inc(loaded[2 * h + j], 16)
                        if normed:
                            sp.dma_start(yb2[2 * h + j][:, :], T.dram["L3b2"][bass.ds(e, 1), :]).then_inc(loaded[2 * h + j], 16)

        @block.tensor
        def _(pe):
            pe.sem_inc(y_in, 2)
            n = blocks_in_use(pe)
            with pe.Fori(0, B // 4) as i:
              for h in range(2):
                with pe.If(4 * i + 2 * h < n):
                    for j in range(2):
                        pe.wait_ge(loaded[2 * h + j], loads * i + loads)
                        for c in range(2):
                            mm = pe.transpose(T.bank[j][0:Q, TILE * c:TILE * c + TILE], xr[2 * h + j][:, Q * c:Q * c + Q],
                                              p["ident"][0:TILE, 0:TILE])
                        mm.then_inc(turned, 1)
                    for j in range(2):
                        pe.wait_ge(xt_in, 4 * i + 2 * h + j + 1)
                        w = cols(w1[2 * h + j][:, 0:W1 - W1 % 2], 2)
                        for a in range(1 if normed else 2):
                            for f in range(C):
                                for c in range(2):
                                    mm = pe.matmul(T.bank[2 + 2 * a + j][0:N, TILE * f:TILE * f + TILE],
                                                   w[:, c, I * a + N * f:I * a + N * f + N], xt[j][:, c, :],
                                                   start=(c == 0), stop=(c == 1))
                            mm.then_inc(up if a else gate, 1)
                    if normed:
                        for j in range(2):
                            pe.wait_ge(acted, 4 * i + 2 * h + j + 1)
                            for f in range(C):
                                mm = pe.matmul(T.bank[4 + j][0:N, 0:TILE], p["mean384"], hid[j][:, f, :],
                                               start=(f == 0), stop=(f == C - 1))
                            mm.then_inc(means, 1)
                        for j in range(2):
                            pe.wait_ge(squared, 4 * i + 2 * h + j + 1)
                            for f in range(C):
                                mm = pe.matmul(T.bank[4 + j][0:N, TILE:2 * TILE], p["mean384"], sq[j][:, f, :],
                                               start=(f == 0), stop=(f == C - 1))
                            mm.then_inc(variances, 1)
                    for j in range(2):
                        pe.wait_ge(hidden, 4 * i + 2 * h + j + 1)
                        pe.wait_ge(y_in, 4 * i + 2 * h + j + 1)
                        w = cols(w2[2 * h + j][:, 0:C * DIM], C)
                        if normed:
                            pe.matmul(T.bank[6 + j][0:TILE, 0:DIM], p["ones"][0:1, 0:TILE], yb2[2 * h + j][:, :],
                                      start=True, stop=False)
                        for f in range(C):
                            mm = pe.matmul(T.bank[6 + j][0:TILE, 0:DIM], act_out[j][:, f, :], w[:, f, :],
                                           start=(f == 0 and not normed), stop=(f == C - 1))
                        mm.then_inc(down, 1)

        @block.scalar
        def _(act):
            for j in range(2):
                act.sem_inc(stored[j], 16)
            if normed:
                act.wait_ge(eps_set, 1)
            n = blocks_in_use(act)
            with act.Fori(0, B // 4) as i:
              for h in range(2):
                with act.If(4 * i + 2 * h < n):
                    for j in range(2):
                        act.wait_ge(gate, 4 * i + 2 * h + j + 1)
                        got = cols(T.bank[2 + j][0:N, 0:C * TILE], C)
                        if not normed:
                            act.activation(hid[j][:, :, :], got, ACT.Silu).then_inc(acted, 1)
                        else:
                            for f in range(C):
                                ins = act.activation(hid[j][:, f, :], got[:, f, :], ACT.Gelu,
                                                     bias=w2[2 * h + j][:, C * DIM + f:C * DIM + f + 1])
                            ins.then_inc(acted, 1)
                    if normed:
                        for j in range(2):
                            act.wait_ge(centred, 4 * i + 2 * h + j + 1)
                            act.activation(sq[j][:, :, :], act_out[j][:, :, :], ACT.Square).then_inc(squared, 1)
                        for j in range(2):
                            act.wait_ge(variances, 4 * i + 2 * h + j + 1)
                            act.activation(sd[j][:, :], T.bank[4 + j][0:N, TILE:2 * TILE], ACT.Sqrt, bias=eps[:, 0:1])\
                                .then_inc(deviated, 1)
                        for j in range(2):
                            act.wait_ge(scaled, 4 * i + 2 * h + j + 1)
                            for f in range(C):
                                at = C * DIM + C + f
                                ins = act.activation(act_out[j][:, f, :], hid[j][:, f, :], ACT.Identity,
                                                     scale=w2[2 * h + j][:, at:at + 1], bias=w2[2 * h + j][:, at + C:at + C + 1])
                            ins.then_inc(hidden, 1)
                    for j in range(2):
                        act.wait_ge(down, 4 * i + 2 * h + j + 5)
                        act.wait_ge(stored[j], 32 * i + 16 * h + 16)
                        act.copy(y[j][:, :], T.bank[6 + j][0:TILE, 0:DIM]).then_inc(y_in, 1)
                        act.wait_ge(y_in, 4 * i + 2 * h + j + 3)
                        act.dma_start(rows[bass.ds((4 * i + 2 * h + j) * TILE, TILE), :], y[j][:, :]).then_inc(stored[j], 16)
            for j in range(2):
                act.wait_ge(stored[j], (n + 1) // 2 * 16 + 16)
                act.sem_inc(all_stored, 1)

        @block.vector
        def _(dve):
            if normed:
                dve.memset(eps[:, :], EPS).then_inc(eps_set, 1)
            n = blocks_in_use(dve)
            with dve.Fori(0, B // 4) as i:
              for h in range(2):
                with dve.If(4 * i + 2 * h < n):
                    for j in range(2):
                        dve.wait_ge(turned, 4 * i + 2 * h + j + 1)
                        dve.tensor_copy(xt[j][:, :, :], cols(T.bank[j][0:Q, 0:2 * TILE], 2)).then_inc(xt_in, 1)
                    if not normed:
                        for j in range(2):
                            dve.wait_ge(acted, 4 * i + 2 * h + j + 1)
                            dve.wait_ge(up, 4 * i + 2 * h + j + 1)
                            dve.tensor_tensor(act_out[j][:, :, :], hid[j][:, :, :], cols(T.bank[4 + j][0:N, 0:C * TILE], C),
                                              ALU.mult).then_inc(hidden, 1)
                    else:
                        for j in range(2):
                            dve.wait_ge(means, 4 * i + 2 * h + j + 1)
                            dve.tensor_tensor(act_out[j][:, :, :], hid[j][:, :, :],
                                              spread(T.bank[4 + j][0:N, 0:TILE], 1, C), ALU.subtract).then_inc(centred, 1)
                        for j in range(2):
                            dve.wait_ge(deviated, 4 * i + 2 * h + j + 1)
                            dve.reciprocal(sd[j][:, :], sd[j][:, :]).then_inc(inverted, 1)
                            dve.wait_ge(inverted, 4 * i + 2 * h + j + 1)
                            dve.tensor_tensor(hid[j][:, :, :], act_out[j][:, :, :], spread(sd[j][:, :], 1, C), ALU.mult)\
                                .then_inc(scaled, 1)


def combine(T, key, rows, weight, fetch):
    nc, p, m = T.nc, T.p, MOE[key]
    K, B = m["top"], m["blocks"]
    with ExitStack() as ctx:
        def sb(what, shape):
            return ctx.enter_context(nc.sbuf_tensor(f"{key}_{what}", shape, F32))

        sem = lambda what: T.sem(f"{key}_{what}")
        acc = sb("acc", [TILE, TILES, DIM])
        got = sb("got", [TILE, K, TILES, DIM])
        added, turned = map(sem, ("added", "y_turned"))
        fetched = [sem(f"fetched{k}") for k in range(K)]
        block = ctx.enter_context(nc.Block())

        @block.gpsimd
        def _(pool):
            for k in range(K):
                for i in range(TILES):
                    pool.indirect_dma_start(got[:, k, i, :], None, rows[0:B * TILE, :],
                                            bass.IndirectOffsetOnAxis(ap=fetch[:, k, i:i + 1], axis=0))\
                        .then_inc(fetched[k], 16)

        @block.vector
        def _(dve):
            for i in range(TILES):
                dve.wait_ge(fetched[0], 16 * TILES)
                dve.tensor_scalar(acc[:, i, :], got[:, 0, i, :], weight[:, i, 0:1], None, ALU.mult).then_inc(added, 1)
            for k in range(1, K):
                dve.wait_ge(added, k * TILES)
                dve.wait_ge(fetched[k], 16 * TILES)
                for i in range(TILES):
                    dve.scalar_tensor_tensor(acc[:, i, :], got[:, k, i, :], weight[:, i, k:k + 1], acc[:, i, :],
                                             ALU.mult, ALU.add).then_inc(added, 1)
            for u in range(4):
                c, s = u // 2, HALF * (u % 2)
                dve.wait_ge(turned, u + 1)
                dve.tensor_tensor(T.h[:, c, s:s + HALF], T.h[:, c, s:s + HALF], T.bank[u][0:Q, 0:HALF], ALU.add)

        @block.tensor
        def _(pe):
            pe.wait_ge(added, K * TILES)
            for u in range(4):
                c, half = u // 2, u % 2
                for j in range(TILES // 2):
                    mm = pe.transpose(T.bank[u][0:Q, TILE * j:TILE * j + TILE],
                                      acc[:, TILES // 2 * half + j, Q * c:Q * c + Q], p["ident"][0:TILE, 0:TILE])
                mm.then_inc(turned, 1)


def layer3_attention(T):
    nc, p = T.nc, T.p
    with ExitStack() as ctx:
        def sb(what, shape):
            return ctx.enter_context(nc.sbuf_tensor(f"a3_{what}", shape, F32))
        qk, v, att = sb("qk", [Q, 4, TOKENS]), sb("v", [SEQ, IMAGES, DIM]), sb("att", [Q, 2, TOKENS])
        w = cols(p["aqkv"], 2)
        linear(T, "a3_qk", 4, 2, lambda m, k: w[:, k, Q * m:Q * m + Q], lambda k, at: T.xn[:, k, at],
               by_act=biased(T, qk, p["aqkvb"]))
        values_by_token(T, "a3_vals", T.xn, w[:, :, 2 * DIM:3 * DIM], v, SEQ)
        head_attention(T, "a3_att", qk, v, p["aqkvb"][:, 4:6], att, True)
        w2 = cols(p["aproj"], 2)
        linear(T, "a3_proj", 2, 2, lambda m, k: w2[:, k, Q * m:Q * m + Q], lambda k, at: att[:, k, at],
               by_dve=residual(T, T.h, p["aprojb"]))


def store_output(T):
    nc, p = T.nc, T.p
    with ExitStack() as ctx:
        out = ctx.enter_context(nc.sbuf_tensor("out_rows", [TILE, TILES, DIM], F32))
        turned = T.sem("out_turned")
        taken = T.sem("out_taken")
        stored = T.sem("out_stored")
        block = ctx.enter_context(nc.Block())

        @block.tensor
        def _(pe):
            for i in range(TILES):
                for c in range(2):
                    mm = pe.transpose(T.bank[i // 2][0:TILE, DIM * (i % 2) + Q * c:DIM * (i % 2) + Q * c + Q],
                                      T.h[:, c, TILE * i:TILE * i + TILE], p["ident"][0:Q, 0:Q])
                if i % 2:
                    mm.then_inc(turned, 1)

        @block.vector
        def _(dve):
            for u in range(TILES // 2):
                dve.wait_ge(turned, u + 1)
                dve.tensor_copy(out[:, 2 * u:2 * u + 2, :], cols(T.bank[u][0:TILE, 0:2 * DIM], 2)).then_inc(taken, 1)

        @block.sync
        def _(sp):
            sp.wait_ge(taken, TILES // 2)
            sp.dma_start(T.dram["out"].rearrange("(i p) d -> p i d", p=TILE), out[:, :, :]).then_inc(stored, 16)
            sp.wait_ge(stored, 16)


STAGES = ["tok", "L0a", "L0f", "L1a", "L1f", "L2a", "L2f", "L3a", "L3f"]


def build(nc, dram, stages=STAGES):
    with ExitStack() as ctx:
        T = Tower(nc, ctx, dram)
        load_all(T)
        T.end_layer()
        plain = {"L0a": layer0_attention, "L1a": layer1_attention, "L1f": layer1_block, "L2a": selective_scan,
                 "L3a": layer3_attention}
        for s in stages:
            if s in plain:
                layer_norm(T, f"{s}_ln", T.h, T.xn, lambda sp: sp.wait_ge(T.loaded[s], 16))
                plain[s](T)
                T.end_layer()
            elif s.endswith("f"):
                experts(T, s[:2])
                T.end_layer()
        store_output(T)


def fm(w):
    return np.concatenate([w[:Q], w[Q:]], axis=1)


def vec(*bs):
    return np.concatenate([b.reshape(-1, Q).T for b in bs], axis=1)


def chunks(w, n):
    return w.reshape(-1, n, w.shape[1]).transpose(1, 0, 2).reshape(n, -1)


def constants():
    i = np.arange(128)
    pair = np.arange(PAIR) // SEQ
    same = (pair[:, None] == pair[None, :])
    k, t, q = np.meshgrid(np.arange(6), np.arange(TILES), np.arange(TILE), indexing="ij")
    return {
        "ident": np.eye(128), "ones": np.ones((128, 128)), "mean192": np.full((Q, Q), 1 / DIM),
        "mean384": np.full((128, 128), 1 / 384), "before": i[:, None] < i[None, :],
        "iota": np.broadcast_to(np.arange(MAX_BLOCKS), (128, MAX_BLOCKS)), "ecol": i[:, None],
        "levels": np.broadcast_to(TILE * np.arange(TILES), (128, TILES)),
        "spare": (TOKENS * k + TILE * t + q).transpose(2, 0, 1).reshape(TILE, -1),
        "apart": np.where(same, 0.0, -1.0e30), "same": same,
        "headmask": (np.arange(Q) // HEAD_DIM)[:, None] == np.arange(6)[None, :],
    }


def layout(x):
    def rows(b, n):
        return np.broadcast_to(b.reshape(1, -1), (n, b.size))

    f = constants()
    f.update(tokW=chunks(x["L0_tok_W"], 128), tokb=vec(x["L0_tok_b"]),
             l0qkv=fm(x["L0_attn_w_qkv"].T), l0qkvb=vec(x["L0_attn_b_qkv"]), l0proj=fm(x["L0_attn_w_proj"].T),
             l0projb=vec(x["L0_attn_b_proj"]), L0gate=fm(x["L0_ffn_w_gate"]), L0gateb=rows(x["L0_ffn_expert_bias"], TILE),
             l1q=fm(x["L1_attn_Wq"].T), l1k=fm(x["L1_attn_Wk"].T), l1v=fm(x["L1_attn_Wv"].T),
             l1qkb=vec(x["L1_attn_bq"], x["L1_attn_bk"]), l1vb=rows(x["L1_attn_bv"], PAIR))
    b = {k[7:]: v for k, v in x.items() if k.startswith("L1_ffn_")}
    f.update(mq=fm(b["wq"].T), mk=fm(b["wk"].T), mv=fm(b["wv"].T), mo=fm(b["wo"].T), mqkvb=vec(b["bq"], b["bk"], b["bv"]),
             mob=vec(b["bo"]), ln1=vec(b["ln1_g"], b["ln1_b"]), ln2=vec(b["ln2_g"], b["ln2_b"]),
             rln=vec(b["r_ln_g"], b["r_ln_b"]), fc1=fm(b["fc1_w"].T), fc1b=b["fc1_b"].reshape(6, 128).T,
             fc2=chunks(b["fc2_w"].T, 128), fc2b=vec(b["fc2_b"]), rin=fm(b["r_in_w"].T), rinb=b["r_in_b"][:, None],
             ro1=chunks(b["r_o1_w"].T, 128), ro1b=b["r_o1_b"][:, None], ro2=b["r_o2_w"].T, ro2b=b["r_o2_b"][:, None],
             ro3=b["r_o3_w"].T, ro3b=rows(b["r_o3_b"], 128), ldown=fm(b["lra_down"].reshape(192, DIM).T),
             lup01=b["lra_up"][:2].transpose(0, 2, 1).reshape(128, DIM), lup2=b["lra_up"][2].T)
    A = x["L2_attn_A"]
    f.update(sD=fm(x["L2_attn_W_delta"].T), sDb=vec(x["L2_attn_delta_bias"]),
             L2gate=fm(x["L2_ffn_Wg"].T), L2gateb=rows(x["L2_ffn_e_bias"], TILE),
             aqkv=fm(x["L3_attn_W_qkv"]), aqkvb=vec(x["L3_attn_b_qkv"]), aproj=fm(x["L3_attn_W_proj"]),
             aprojb=vec(x["L3_attn_b_proj"]), L3gate=fm(x["L3_ffn_gate_w"]), L3gateb=rows(x["L3_ffn_gate_b"], TILE), L3b2v=vec(x["L3_ffn_fc2_b"][0]))
    out = {}
    for g, items in GROUPS.items():
        t = out[g] = np.zeros((128, WIDTHS[g]), np.float32)
        at = 0
        for name, parts, n in items:
            t[0:parts, at:at + n] = f[name]
            at += n
    im = x["x"].reshape(IMAGES, 3, 6, 16, 6, 16).transpose(1, 3, 5, 0, 2, 4).reshape(PATCH_K, 128, TOKENS)
    out["patches"] = np.ascontiguousarray(im.transpose(1, 0, 2))
    bc = np.stack([x["L2_attn_W_B"], x["L2_attn_W_C"]]).reshape(2, DIM, STATES, 2, Q)
    bc = bc.transpose(2, 4, 0, 3, 1).reshape(STATES, Q, 4 * DIM)
    out["wBC"] = np.concatenate([bc, A.reshape(2, Q, STATES).transpose(2, 1, 0)], axis=2)

    def first(w):
        return w.reshape(w.shape[0], 2, Q, w.shape[2]).transpose(0, 2, 1, 3).reshape(w.shape[0], Q, -1)

    def second(w, n):
        return w.reshape(w.shape[0], -1, n, DIM).transpose(0, 2, 1, 3).reshape(w.shape[0], n, -1)

    out["L0w1"] = first(np.concatenate([x["L0_ffn_wg"], x["L0_ffn_wu"]], axis=2))
    out["L0w2"] = second(x["L0_ffn_wd"], 128)
    out["L0s1"] = first(np.concatenate([x["L0_ffn_swg"], x["L0_ffn_swu"]], axis=1)[None])[0]
    out["L0s2"] = second(x["L0_ffn_swd"][None], 128)[0]
    out["L2w1"] = first(x["L2_ffn_W_gate_up"])
    out["L2w2"] = second(x["L2_ffn_W_down"], 116)
    out["L2s1"] = first(np.concatenate([x["L2_ffn_Wsg"], x["L2_ffn_Wsu"]], axis=1)[None])[0]
    out["L2s2"] = second(x["L2_ffn_Wsd"][None], 116)[0]
    out["L3w1"] = first(x["L3_ffn_fc1_w"])
    cols3 = [x[k].reshape(16, 3, 128).transpose(0, 2, 1) for k in ("L3_ffn_fc1_b", "L3_ffn_ln_w", "L3_ffn_ln_b")]
    out["L3w2"] = np.concatenate([second(x["L3_ffn_fc2_w"], 128)] + cols3, axis=2)
    out["L3s1"], out["L3s2"] = out["L3w1"][0], out["L3w2"][0]
    out["L3b2"] = x["L3_ffn_fc2_b"]
    return {k: np.ascontiguousarray(v) for k, v in out.items()}


def kernel(**inputs):
    import concourse.bacc as bacc
    from concourse.bass_utils import run_bass_kernel_spmd

    nc = bacc.Bacc("TRN2", target_bir_lowering=False, num_devices=1)
    arrays = layout({k: np.asarray(v) for k, v in inputs.items()})
    dram = {k: nc.dram_tensor(f"in_{k}", a.shape, F32, kind="ExternalInput").ap() for k, a in arrays.items()}
    dram["out"] = nc.dram_tensor("out_h", (TOKENS, DIM), F32, kind="ExternalOutput").ap()
    build(nc, dram)
    r = run_bass_kernel_spmd(nc, [{f"in_{k}": a for k, a in arrays.items()}], core_ids=[0])
    return r.results[0]["out_h"].reshape(IMAGES, SEQ, DIM)
```

```python
from contextlib import ExitStack

import numpy as np

import concourse.bass as bass
from concourse import mybir

F32 = mybir.dt.float32
F32R = mybir.dt.float32r
U32 = mybir.dt.uint32
ALU = mybir.AluOpType
ACT = mybir.ActivationFunctionType
AX = mybir.AxisListType

IMAGES, SEQ, DIM = 16, 36, 192
TOKENS = IMAGES * SEQ
Q = 96
HALF = TOKENS // 2
PATCH_K = 6
PAIR = 2 * SEQ
PAIRS = TOKENS // PAIR
TILE = 96
TILES = TOKENS // TILE
HEADS, HEAD_DIM = 12, 16
KEEP = int(0.4 * SEQ)
STATES = 16
WARM = 6
LN_WARM = (1, 2)
BRIDGE = 2
STEP = 4
ZEROS = 9
SETS = 2
EPS = 1e-5

MOE = {
    "L0": dict(experts=16, top=2, cap=TOKENS, shared=1, width=384, chunks=3, block=128, group=3, early=1),
    "L2": dict(experts=128, top=6, cap=192, shared=2, width=464, chunks=4, block=96, group=3, early=4),
    "L3": dict(experts=16, top=3, cap=TOKENS, shared=1, width=384, chunks=3, block=128, group=4, early=2),
}
for _m in MOE.values():
    _most = (TOKENS * _m["top"] + _m["experts"] * (_m["block"] - 1)) // _m["block"]
    _m["groups"] = -(-_most // (SETS * STEP * _m["group"]))
    _m["blocks"] = SETS * STEP * _m["group"] * _m["groups"]
    _m["rows"] = _m["blocks"] * _m["block"]
MAX_BLOCKS = max(_m["blocks"] for _m in MOE.values())

GROUPS = {
    "const": [("ident", 128, 128), ("ones", 128, 128), ("mean192", Q, Q), ("mean384", 128, 128),
              ("before", 128, 128), ("iota", 128, MAX_BLOCKS), ("ecol", 128, 1), ("levels96", 128, TILES), ("levels128", 128, TILES),
              ("spare", TILE, TILES * 6), ("apart", PAIR, PAIR), ("same", PAIR, PAIR), ("headmask", Q, 6)],
    "tok": [("tokW", 128, PATCH_K * DIM), ("tokb", Q, 2)],
    "L0a": [("l0qkv", Q, 6 * DIM), ("l0qkvb", Q, 6), ("l0proj", Q, 2 * DIM), ("l0projb", Q, 2),
            ("L0gate", Q, 32), ("L0gateb", TILE, 16)],
    "L1a": [("l1q", Q, 2 * DIM), ("l1k", Q, 2 * DIM), ("l1v", Q, 2 * DIM), ("l1qkb", Q, 4),
            ("l1vb", PAIR, DIM)],
    "L1f": [("mq", Q, 2 * DIM), ("mk", Q, 2 * DIM), ("mv", Q, 2 * DIM), ("mo", Q, 2 * DIM),
            ("mqkvb", Q, 6), ("mob", Q, 2), ("ln1", Q, 4), ("ln2", Q, 4), ("rln", Q, 4),
            ("fc1", Q, 2 * 768), ("fc1b", 128, 6), ("fc2", 128, 6 * DIM), ("fc2b", Q, 2),
            ("rin", Q, 2 * 128), ("rinb", 128, 1), ("ro1", 128, 2 * 128), ("ro1b", 128, 1),
            ("ro2", 128, 64), ("ro2b", 64, 1), ("ro3", 64, 4), ("ro3b", 128, 4),
            ("ldown", Q, 2 * DIM), ("lup01", 128, DIM), ("lup2", 64, DIM)],
    "L2a": [("sD", Q, 2 * DIM), ("sDb", Q, 2), ("sA", Q, 2 * STATES), ("L2gate", Q, 256), ("L2gateb", TILE, 128)],
    "L3a": [("aqkv", Q, 6 * DIM), ("aqkvb", Q, 6), ("aproj", Q, 2 * DIM), ("aprojb", Q, 2),
            ("L3gate", Q, 32), ("L3gateb", TILE, 16), ("L3b2v", Q, 2)],
}
WIDTHS = {g: sum(n for _, _, n in items) for g, items in GROUPS.items()}


class Tower:

    def __init__(self, nc, ctx, dram):
        self.nc, self.dram, self.of_layer = nc, dram, []
        self.h = ctx.enter_context(nc.sbuf_tensor("h", [Q, 2, TOKENS], F32))
        self.x_full = ctx.enter_context(nc.sbuf_tensor("xn", [128, 2, TOKENS], F32))
        self.xn = self.x_full[0:Q, :, :]
        self.bank = [ctx.enter_context(nc.psum_tensor(f"bank{i}", [128, 512], F32)) for i in range(8)]
        self.loaded = {g: ctx.enter_context(nc.semaphore(f"loaded_{g}")) for g in GROUPS}
        self.zero = ctx.enter_context(nc.sbuf_tensor("zero", [128, ZEROS * DIM], F32))
        self.unread = ctx.enter_context(nc.sbuf_tensor("unread", [128, 64], F32))
        self.table_loads = 0
        self.zeroed = ctx.enter_context(nc.semaphore("rows_zeroed"))
        self.p, self.full, self.packed = {}, {}, {}
        for g, items in GROUPS.items():
            t = self.packed[g] = ctx.enter_context(nc.sbuf_tensor(f"par_{g}", [128, WIDTHS[g]], F32))
            at = 0
            for name, parts, n in items:
                self.p[name] = t[0:parts, at:at + n]
                self.full[name] = t[:, at:at + n]
                at += n
        self.rows = {k: nc.dram_tensor(f"rows_{k}", [m["rows"] + TOKENS * m["top"], DIM], F32, kind="Internal").ap()
                     for k, m in MOE.items()}

    def sem(self, name):
        s = self.nc.alloc_semaphore(name)
        self.of_layer.append(s)
        return s

    def load_table(self, func):
        at = self.table_loads
        self.table_loads += 1
        self.nc.scalar.activation(self.unread[:, at:at + 1], self.p["ones"][:, 0:1], func)

    def end_layer(self):
        self.nc.clear_and_free_semaphores(self.of_layer)
        self.nc.all_engine_barrier()
        self.of_layer = []


def cols(ap, n):
    return ap.rearrange("p (n m) -> p n m", n=n)


def spread(ap, axis, n):
    a = ap.unsqueeze(axis)
    shape = list(a.shape)
    shape[axis] = n
    return a.broadcast_to(shape)


def chained(eng, sem):
    count = [0]

    def link(ins):
        count[0] += 1
        ins.then_inc(sem, 1)
        eng.wait_ge(sem, count[0])

    return link


def load_all(T):
    nc = T.nc
    with ExitStack() as ctx:
        wtok = ctx.enter_context(nc.sbuf_tensor("patches", [128, PATCH_K, TOKENS], F32))
        patches_in = T.sem("patches_in")
        zero_ready = T.sem("zero_ready")
        products = T.sem("tok_products")
        block = ctx.enter_context(nc.Block())
        W = cols(T.p["tokW"], PATCH_K)

        @block.sync
        def _(sp):
            sp.dma_start(T.packed["tok"][:, :], T.dram["tok"]).then_inc(T.loaded["tok"], 16)
            sp.dma_start(wtok[:, 0:3, :], T.dram["patches"][:, 0:3, :]).then_inc(patches_in, 16)
            sp.dma_start(wtok[:, 3:6, :], T.dram["patches"][:, 3:6, :]).then_inc(patches_in, 16)
            for g in GROUPS:
                if g != "tok":
                    sp.dma_start(T.packed[g][:, :], T.dram[g]).then_inc(T.loaded[g], 16)
            sp.wait_ge(zero_ready, 1)
            for k, m in MOE.items():
                for r in range(0, m["rows"] // 128, ZEROS):
                    n = min(ZEROS, m["rows"] // 128 - r)
                    sp.dma_start(T.rows[k][128 * r:128 * (r + n), :].rearrange("(p a) d -> p (a d)", p=128),
                                 T.zero[:, 0:n * DIM]).then_inc(T.zeroed, 16)
            sp.wait_ge(T.loaded["const"], 16)

        @block.vector
        def _(dve):
            dve.memset(T.zero[:, :], 0.0).then_inc(zero_ready, 1)
            dve.memset(T.x_full[Q:128, :, :], 0.0)

        @block.tensor
        def _(pe):
            pe.wait_ge(T.loaded["tok"], 16)
            pe.wait_ge(patches_in, 32)
            for u in range(4):
                m, s = u // 2, HALF * (u % 2)
                for k in range(PATCH_K):
                    mm = pe.matmul(T.bank[u][0:Q, 0:HALF], W[:, k, Q * m:Q * m + Q], wtok[:, k, s:s + HALF],
                                   start=(k == 0), stop=(k == PATCH_K - 1))
                mm.then_inc(products, 1)

        @block.scalar
        def _(act):
            for u in range(4):
                m, s = u // 2, HALF * (u % 2)
                act.wait_ge(products, u + 1)
                act.activation(T.h[:, m, s:s + HALF], T.bank[u][0:Q, 0:HALF], ACT.Identity,
                               bias=T.p["tokb"][:, m:m + 1])


def wake(T, bank, n):
    for _ in range(n):
        T.nc.tensor.matmul(bank[:, :], T.p["ones"], T.packed["const"][:, 0:512], start=True, stop=True)


def layer_norm(T, name, x, out, meanwhile=None, on_pool=None, affine=(), func=None):
    nc = T.nc
    HT = TILES // 2
    with ExitStack() as ctx:
        xc = ctx.enter_context(nc.sbuf_tensor(f"{name}_xc", [Q, 2, TOKENS], F32))
        sq = ctx.enter_context(nc.sbuf_tensor(f"{name}_sq", [Q, 2, TOKENS], F32))
        sd = ctx.enter_context(nc.sbuf_tensor(f"{name}_sd", [TILE, TILES], F32))
        inv = ctx.enter_context(nc.sbuf_tensor(f"{name}_inv", [TILE, TILES], F32))
        eps = ctx.enter_context(nc.sbuf_tensor(f"{name}_eps", [Q, 1], F32))
        eps_set = T.sem(f"{name}_eps_set")
        means = T.sem(f"{name}_means")
        centred = T.sem(f"{name}_centred")
        squared = T.sem(f"{name}_squared")
        variances = T.sem(f"{name}_variances")
        deviations = T.sem(f"{name}_deviations")
        inverted = T.sem(f"{name}_inverted")
        spread_out = T.sem(f"{name}_spread_out")
        normalized = T.sem(f"{name}_normalized")
        block = ctx.enter_context(nc.Block())

        if meanwhile:
            @block.sync
            def _(sp):
                meanwhile(sp)

        if on_pool:
            @block.gpsimd
            def _(pool):
                on_pool(pool)

        @block.tensor
        def _(pe):
            for s in range(2):
                for c in range(2):
                    mm = pe.matmul(T.bank[s][0:Q, 0:HALF], T.p["mean192"], x[:, c, HALF * s:HALF * s + HALF],
                                   start=(c == 0), stop=(c == 1))
                mm.then_inc(means, 1)
            wake(T, T.bank[6], LN_WARM[0])
            for s in range(2):
                pe.wait_ge(squared, s + 1)
                for j in range(HT):
                    at = TILE * (HT * s + j)
                    for c in range(2):
                        mm = pe.matmul(T.bank[2 + s][0:TILE, j:j + 1], sq[:, c, at:at + TILE], T.p["mean192"][:, 0:1],
                                       start=(c == 0), stop=(c == 1))
                mm.then_inc(variances, 1)
            for s in range(2):
                pe.wait_ge(inverted, s + 1)
                for j in range(HT):
                    mm = pe.matmul(T.bank[4 + s][0:Q, TILE * j:TILE * j + TILE],
                                   inv[:, HT * s + j:HT * s + j + 1].broadcast_to([TILE, Q]), T.p["ident"][0:TILE, 0:TILE],
                                   start=True, stop=True)
                mm.then_inc(spread_out, 1)
            wake(T, T.bank[7], LN_WARM[1])

        @block.vector
        def _(dve):
            dve.memset(eps[:, :], EPS).then_inc(eps_set, 1)
            for s in range(2):
                at = slice(HALF * s, HALF * s + HALF)
                dve.wait_ge(means, s + 1)
                dve.tensor_tensor(xc[:, :, at], x[:, :, at], spread(T.bank[s][0:Q, 0:HALF], 1, 2), ALU.subtract)\
                    .then_inc(centred, 1)
            for s in range(2):
                dve.wait_ge(deviations, s + 1)
                dve.reciprocal(inv[:, HT * s:HT * s + HT], sd[:, HT * s:HT * s + HT]).then_inc(inverted, 1)
            for s in range(2):
                at = slice(HALF * s, HALF * s + HALF)
                dve.wait_ge(spread_out, s + 1)
                dve.tensor_tensor(out[:, :, at], xc[:, :, at], spread(T.bank[4 + s][0:Q, 0:HALF], 1, 2), ALU.mult)\
                    .then_inc(normalized, 1)

        @block.scalar
        def _(act):
            T.load_table(ACT.Sqrt)
            for s in range(2):
                at = slice(HALF * s, HALF * s + HALF)
                act.wait_ge(centred, s + 1)
                act.activation(sq[:, :, at], xc[:, :, at], ACT.Square).then_inc(squared, 1)
            act.wait_ge(eps_set, 1)
            for s in range(2):
                act.wait_ge(variances, s + 1)
                act.activation(sd[:, HT * s:HT * s + HT], T.bank[2 + s][0:TILE, 0:HT], ACT.Sqrt, bias=eps[:, 0:1])\
                    .then_inc(deviations, 1)
            if func:
                T.load_table(func)
            if affine:
                for s in range(2):
                    at = slice(HALF * s, HALF * s + HALF)
                    act.wait_ge(normalized, s + 1)
                    for y, gb in affine:
                        for c in range(2):
                            act.activation(y[:, c, at], out[:, c, at], ACT.Identity, bias=gb[:, 2 + c:3 + c], scale=gb[:, c:c + 1])


def linear(T, name, outs, terms, lhsT, rhs, by_act=None, by_dve=None, size=Q, after=None, on_pool=None):
    nc = T.nc
    units = [(m, slice(HALF * s, HALF * s + HALF)) for m in range(outs) for s in range(2)]
    on_act = [by_dve is None or (by_act is not None and u % 2 == 0) for u in range(len(units))]
    sizes = size if isinstance(size, list) else [size] * outs
    with ExitStack() as ctx:
        products = T.sem(f"{name}_products")
        act_took = T.sem(f"{name}_act_took")
        dve_took = T.sem(f"{name}_dve_took")
        block = ctx.enter_context(nc.Block())

        @block.tensor
        def _(pe):
            for u, (m, at) in enumerate(units):
                if u >= 8:
                    if on_act[u - 8]:
                        pe.wait_ge(act_took, sum(on_act[:u - 7]))
                    else:
                        pe.wait_ge(dve_took, u - 7 - sum(on_act[:u - 7]))
                for k in range(terms):
                    mm = pe.matmul(T.bank[u % 8][0:sizes[m], 0:HALF], lhsT(m, k), rhs(k, at),
                                   start=(k == 0), stop=(k == terms - 1))
                mm.then_inc(products, 1)

        @block.scalar
        def _(act):
            for u, (m, at) in enumerate(units):
                if on_act[u]:
                    act.wait_ge(products, u + 1)
                    by_act(m, at, T.bank[u % 8][0:sizes[m], 0:HALF]).then_inc(act_took, 1)

        @block.vector
        def _(dve):
            for u, (m, at) in enumerate(units):
                if not on_act[u]:
                    dve.wait_ge(products, u + 1)
                    by_dve(m, at, T.bank[u % 8][0:sizes[m], 0:HALF]).then_inc(dve_took, 1)

        if after or on_pool:
            @block.gpsimd
            def _(pool):
                if on_pool:
                    on_pool(pool)
                if after:
                    for u, (m, at) in enumerate(units):
                        pool.wait_ge(dve_took, u + 1)
                        after(m, at)


def values_by_token(T, name, x, w, v, group, bias=None, clear=None):
    nc = T.nc
    units = TOKENS // group // 2
    with ExitStack() as ctx:
        products = T.sem(f"{name}_products")
        taken = T.sem(f"{name}_taken")
        cleared = T.sem(f"{name}_cleared")
        block = ctx.enter_context(nc.Block())

        if clear is not None:
            @block.gpsimd
            def _(pool):
                pool.memset(clear, 0.0).then_inc(cleared, 1)

        @block.tensor
        def _(pe):
            for u in range(units):
                if u >= 8:
                    pe.wait_ge(taken, u - 7)
                for j in range(2):
                    at = group * (2 * u + j)
                    for c in range(2):
                        mm = pe.matmul(T.bank[u % 8][0:group, DIM * j:DIM * j + DIM], x[:, c, at:at + group], w[:, c, :],
                                       start=(c == 0), stop=(c == 1))
                mm.then_inc(products, 1)

        @block.vector
        def _(dve):
            if clear is not None:
                dve.wait_ge(cleared, 1)
            for u in range(units):
                dve.wait_ge(products, u + 1)
                got = cols(T.bank[u % 8][0:group, 0:2 * DIM], 2)
                if bias is None:
                    dve.tensor_copy(v[:, 2 * u:2 * u + 2, :], got).then_inc(taken, 1)
                else:
                    dve.tensor_tensor(v[:, 2 * u:2 * u + 2, :], got, spread(bias, 1, 2), ALU.add).then_inc(taken, 1)


def wide_attention(T, name, qk, v, softmax_scale, linear_scale, take):
    nc = T.nc
    per = PAIRS // 2
    with ExitStack() as ctx:
        sm = ctx.enter_context(nc.sbuf_tensor(f"{name}_sm", [PAIR, PAIRS, PAIR], F32))
        probs_t = ctx.enter_context(nc.sbuf_tensor(f"{name}_pt", [PAIR, PAIRS, PAIR], F32))
        mx = ctx.enter_context(nc.sbuf_tensor(f"{name}_mx", [PAIR, PAIRS], F32))
        total = ctx.enter_context(nc.sbuf_tensor(f"{name}_total", [PAIR, PAIRS], F32))
        sem = lambda what: T.sem(f"{name}_{what}")
        scored, lowered, exps, probs, turned, turned_in, summed = map(
            sem, ("scored", "lowered", "exps", "probs", "turned", "turned_in", "summed"))
        step = sem("dve_step")
        block = ctx.enter_context(nc.Block())

        @block.tensor
        def _(pe):
            for g in range(2):
                for j in range(per):
                    at = slice(PAIR * (per * g + j), PAIR * (per * g + j) + PAIR)
                    a, b = (0, 2) if softmax_scale else (2, 0)
                    for c in range(2):
                        mm = pe.matmul(T.bank[g][0:PAIR, PAIR * j:PAIR * j + PAIR], qk[:, a + c, at], qk[:, b + c, at],
                                       start=(c == 0), stop=(c == 1))
                mm.then_inc(scored, 1)
            if softmax_scale:
                for g in range(2):
                    pe.wait_ge(probs, g + 1)
                    for j in range(per):
                        mm = pe.transpose(T.bank[2 + g][0:PAIR, PAIR * j:PAIR * j + PAIR], sm[:, per * g + j, :],
                                          T.p["ident"][0:PAIR, 0:PAIR])
                    mm.then_inc(turned, 1)
            for g in range(2):
                pe.wait_ge(turned_in, g + 1)
                for m in range(2):
                    for j in range(per):
                        i = per * g + j
                        mm = pe.matmul(T.bank[4 + 2 * g + m][0:Q, PAIR * j:PAIR * j + PAIR],
                                       v[:, i, Q * m:Q * m + Q], probs_t[:, i, :], start=True, stop=True)
                    mm.then_inc(summed, 1)

        @block.vector
        def _(dve):
            link = chained(dve, step)
            for g in range(2):
                dve.wait_ge(scored, g + 1)
                got = cols(T.bank[g][0:PAIR, 0:PAIR * per], per)
                part = sm[:, per * g:per * g + per, :]
                top = mx[:, per * g:per * g + per]
                if softmax_scale:
                    link(dve.tensor_tensor(part, got, spread(T.p["apart"], 1, per), ALU.add))
                    link(dve.tensor_reduce(top, part, AX.X, ALU.max))
                    dve.tensor_tensor(part, part, spread(top, 2, PAIR), ALU.subtract).then_inc(lowered, 1)
                else:
                    dve.scalar_tensor_tensor(probs_t[:, per * g:per * g + per, :], got, linear_scale,
                                             spread(T.p["same"], 1, per), ALU.mult, ALU.mult).then_inc(turned_in, 1)
            if softmax_scale:
                for g in range(2):
                    part = sm[:, per * g:per * g + per, :]
                    tot = total[:, per * g:per * g + per]
                    dve.wait_ge(exps, g + 1)
                    link(dve.tensor_reduce(tot, part, AX.X, ALU.add))
                    link(dve.reciprocal(tot, tot))
                    dve.tensor_tensor(part, part, spread(tot, 2, PAIR), ALU.mult).then_inc(probs, 1)
            for g in range(2):
                for m in range(2):
                    dve.wait_ge(summed, 2 * g + m + 1)
                    take(m, slice(HALF * g, HALF * g + HALF), T.bank[4 + 2 * g + m][0:Q, 0:HALF])

        @block.scalar
        def _(act):
            if softmax_scale:
                for g in range(2):
                    part = sm[:, per * g:per * g + per, :]
                    act.wait_ge(lowered, g + 1)
                    act.activation(part, part, ACT.Exp, scale=softmax_scale).then_inc(exps, 1)
                for g in range(2):
                    act.wait_ge(turned, g + 1)
                    act.copy(probs_t[:, per * g:per * g + per, :], cols(T.bank[2 + g][0:PAIR, 0:PAIR * per], per))\
                        .then_inc(turned_in, 1)


def head_attention(T, name, qk, v, vb, att, sparse):
    nc = T.nc
    H6, ROWS, QUARTERS = 6, 3 * SEQ, 4
    BATCHES = 4
    PER = IMAGES // BATCHES
    CH = PER * QUARTERS
    NG = IMAGES * QUARTERS
    with ExitStack() as ctx:
        def sb(what, shape, dt=F32):
            return ctx.enter_context(nc.sbuf_tensor(f"{name}_{what}", shape, dt))

        sem = lambda what: T.sem(f"{name}_{what}")
        wide = sb("wide", [Q, 2, IMAGES, H6, SEQ])
        sc = sb("sc", [ROWS, NG, SEQ])
        if sparse:
            kept = sb("kept", [ROWS, NG, SEQ])
            top8 = sb("top8", [ROWS, NG, 8])
            next8 = sb("next8", [ROWS, NG, 8])
        mx = sb("mx", [ROWS, NG])
        total = sb("total", [ROWS, NG])
        pt = sb("pt", [128, IMAGES, HEADS * SEQ])
        spread_q, scored, sc_in, lowered, exps, probs, turned, cleared, pt_in, pv, pv_out, mixed, step = map(
            sem, ("spread_q", "scored", "sc_in", "lowered", "exps", "probs", "turned", "cleared", "pt_in", "pv",
                  "pv_out", "mixed", "dve_step"))
        block = ctx.enter_context(nc.Block())

        @block.gpsimd
        def _(pool):
            pool.memset(pt[:, :, :], 0.0).then_inc(cleared, 1)

        @block.tensor
        def _(pe):
            pe.wait_ge(spread_q, 2 * H6)
            for u in range(IMAGES // 2):
                for j in range(2):
                    b = 2 * u + j
                    for g in range(QUARTERS):
                        c, h = g // 2, 3 * (g % 2)
                        col = (j * QUARTERS + g) * SEQ
                        mm = pe.matmul(T.bank[u][0:ROWS, col:col + SEQ], wide[:, c, b, h:h + 3, :].rearrange("p h q -> p (h q)"),
                                       qk[:, 2 + c, SEQ * b:SEQ * b + SEQ], start=True, stop=True)
                mm.then_inc(scored, 1)
            pe.wait_ge(sc_in, IMAGES // 2)

            def turn(b):
                pe.wait_ge(probs, b // PER + 1)
                if b >= 4:
                    pe.wait_ge(pt_in, b - 3)
                for g in range(QUARTERS):
                    mm = pe.transpose(T.bank[b % 4][0:SEQ, ROWS * g:ROWS * g + ROWS], sc[:, QUARTERS * b + g, :],
                                      T.p["ident"][0:ROWS, 0:ROWS])
                mm.then_inc(turned, 1)

            def apply(b):
                pe.wait_ge(pt_in, b + 1)
                if b >= 4:
                    pe.wait_ge(pv_out, b - 3)
                for c in range(2):
                    n = H6 * SEQ
                    mm = pe.matmul(T.bank[4 + b % 4][0:Q, n * c:n * c + n], v[:, b, Q * c:Q * c + Q],
                                   pt[:, b, n * c:n * c + n], start=True, stop=True)
                mm.then_inc(pv, 1)

            for b in range(IMAGES + 2):
                if b < IMAGES:
                    turn(b)
                if b >= 2:
                    apply(b - 2)

        @block.scalar
        def _(act):
            for c in range(2):
                for h in range(0, H6, 2):
                    act.activation(wide[:, c, :, h, :], cols(qk[:, c, :], IMAGES), ACT.Copy, scale=T.p["headmask"][:, h:h + 1])\
                        .then_inc(spread_q, 1)

            T.load_table(ACT.Exp)

            def scores(g):
                for u in range(PER // 2 * g, PER // 2 * (g + 1)):
                    act.wait_ge(scored, u + 1)
                    act.mul(sc[:, 8 * u:8 * u + 8, :], cols(T.bank[u][0:ROWS, 0:8 * SEQ], 8), HEAD_DIM ** -0.5)\
                        .then_inc(sc_in, 1)

            def exponentials(g):
                act.wait_ge(lowered, g + 1)
                part = sc[:, CH * g:CH * g + CH, :]
                act.activation(part, part, ACT.Exp).then_inc(exps, 1)

            def take_turned(g):
                for b in range(PER * g, PER * (g + 1)):
                    act.wait_ge(turned, b + 1)
                    act.copy(pt[0:SEQ, b, :], T.bank[b % 4][0:SEQ, 0:HEADS * SEQ]).then_inc(pt_in, 1)

            scores(0)
            scores(1)
            exponentials(0)
            scores(2)
            exponentials(1)
            scores(3)
            act.wait_ge(cleared, 1)
            take_turned(0)
            exponentials(2)
            take_turned(1)
            exponentials(3)
            take_turned(2)
            take_turned(3)
            for c in range(2):
                act.wait_ge(mixed, 2 * (BATCHES - 1) + c + 1)
                act.activation(att[:, c, :], att[:, c, :], ACT.Identity, bias=vb[:, c:c + 1])

        @block.vector
        def _(dve):
            for c in range(2):
                for h in range(1, H6, 2):
                    dve.tensor_scalar(wide[:, c, :, h, :], cols(qk[:, c, :], IMAGES), T.p["headmask"][:, h:h + 1], None, ALU.mult)\
                        .then_inc(spread_q, 1)
            link = chained(dve, step)

            def lower(g):
                dve.wait_ge(sc_in, PER // 2 * (g + 1))
                n = range(CH * g, CH * g + CH)
                part = sc[:, CH * g:CH * g + CH, :]
                top = mx[:, CH * g:CH * g + CH]
                if sparse:
                    for i in n:
                        ins = dve.max(top8[:, i, :], sc[:, i, :])
                    link(ins)
                    for i in n:
                        ins = dve.match_replace(kept[:, i, :], top8[:, i, :], sc[:, i, :], -3.0e38)
                    link(ins)
                    for i in n:
                        ins = dve.max(next8[:, i, :], kept[:, i, :])
                    link(ins)
                    link(dve.tensor_copy(top, top8[:, CH * g:CH * g + CH, 0]))
                    link(dve.tensor_tensor(kept[:, CH * g:CH * g + CH, :], part,
                                           next8[:, CH * g:CH * g + CH, KEEP - 9:KEEP - 8].broadcast_to([ROWS, CH, SEQ]),
                                           ALU.is_ge))
                else:
                    link(dve.tensor_reduce(top, part, AX.X, ALU.max))
                dve.tensor_tensor(part, part, spread(top, 2, SEQ), ALU.subtract).then_inc(lowered, 1)

            def normalize(g):
                dve.wait_ge(exps, g + 1)
                part = sc[:, CH * g:CH * g + CH, :]
                tot = total[:, CH * g:CH * g + CH]
                if sparse:
                    link(dve.tensor_tensor(part, part, kept[:, CH * g:CH * g + CH, :], ALU.mult))
                link(dve.tensor_reduce(tot, part, AX.X, ALU.add))
                link(dve.reciprocal(tot, tot))
                dve.tensor_tensor(part, part, spread(tot, 2, SEQ), ALU.mult).then_inc(probs, 1)

            def mix(g):
                for b in range(PER * g, PER * (g + 1)):
                    dve.wait_ge(pv, b + 1)
                    got = T.bank[4 + b % 4][0:Q, 0:HEADS * SEQ].rearrange("p (c h q) -> p c h q", c=2, h=H6)
                    mask = T.p["headmask"].unsqueeze(1).unsqueeze(3).broadcast_to([Q, 2, H6, SEQ])
                    dve.tensor_tensor(wide[:, :, b, :, :], got, mask, ALU.mult).then_inc(pv_out, 1)
                dve.wait_ge(pv_out, PER * (g + 1))
                for c in range(2):
                    dve.tensor_reduce(cols(att[:, c, :], IMAGES)[:, PER * g:PER * (g + 1), :],
                                      wide[:, c, PER * g:PER * (g + 1), :, :].rearrange("p b h q -> p b q h"), AX.X, ALU.add)\
                        .then_inc(mixed, 1)

            lower(0)
            lower(1)
            normalize(0)
            lower(2)
            normalize(1)
            mix(0)
            lower(3)
            normalize(2)
            mix(1)
            normalize(3)
            mix(2)
            mix(3)


def residual(T, out, bias):
    def take(m, at, psum):
        return T.nc.vector.scalar_tensor_tensor(out[:, m, at], psum, bias[:, m:m + 1], out[:, m, at], ALU.add, ALU.add)
    return take


def biased(T, out, bias, func=ACT.Identity):
    def take(m, at, psum):
        return T.nc.scalar.activation(out[:, m, at], psum, func, bias=bias[:, m:m + 1])
    return take


def layer0_attention(T):
    nc, p = T.nc, T.p
    with ExitStack() as ctx:
        qk = ctx.enter_context(nc.sbuf_tensor("a0_qk", [Q, 4, TOKENS], F32))
        v = ctx.enter_context(nc.sbuf_tensor("a0_v", [PAIR, PAIRS, DIM], F32))
        att = ctx.enter_context(nc.sbuf_tensor("a0_att", [Q, 2, TOKENS], F32))
        w = cols(T.full["l0qkv"], 2)
        linear(T, "a0_qk_proj", 4, 2, lambda m, k: w[:, k, Q * m:Q * m + Q], lambda k, at: T.x_full[:, k, at],
               by_act=biased(T, qk, p["l0qkvb"]))
        values_by_token(T, "a0_vals", T.x_full, w[:, :, 2 * DIM:3 * DIM], v, PAIR)
        wide_attention(T, "a0_att", qk, v, DIM ** -0.5 / 3.0, None,
                       lambda m, at, psum: nc.vector.tensor_scalar(att[:, m, at], psum, p["l0qkvb"][:, 4 + m:5 + m],
                                                                   None, ALU.add))
        w2 = cols(p["l0proj"], 2)
        linear(T, "a0_proj", 2, 2, lambda m, k: w2[:, k, Q * m:Q * m + Q], lambda k, at: att[:, k, at],
               by_dve=residual(T, T.h, p["l0projb"]))


def layer1_attention(T):
    nc, p = T.nc, T.p
    with ExitStack() as ctx:
        qk = ctx.enter_context(nc.sbuf_tensor("a1_qk", [Q, 4, TOKENS], F32))
        v = ctx.enter_context(nc.sbuf_tensor("a1_v", [PAIR, PAIRS, DIM], F32))
        w = [cols(T.full["l1q"], 2), cols(T.full["l1k"], 2)]
        linear(T, "a1_qk_proj", 4, 2, lambda m, k: w[m // 2][:, k, Q * (m % 2):Q * (m % 2) + Q],
               lambda k, at: T.x_full[:, k, at], by_act=biased(T, qk, p["l1qkb"]))
        values_by_token(T, "a1_vals", T.x_full, cols(T.full["l1v"], 2), v, PAIR, bias=p["l1vb"])
        wide_attention(T, "a1_att", qk, v, None, DIM ** -0.5,
                       lambda m, at, psum: nc.vector.tensor_tensor(T.h[:, m, at], T.h[:, m, at], psum, ALU.add))


def layer1_block(T):
    nc, p = T.nc, T.p
    with ExitStack() as outer:
        x = T.xn
        res = outer.enter_context(nc.sbuf_tensor("b1_res", [Q, 2, TOKENS], F32))
        y = outer.enter_context(nc.sbuf_tensor("b1_y", [Q, 2, TOKENS], F32))
        bits = outer.enter_context(nc.sbuf_tensor("b1_bits", [128, 2, TOKENS], F32))
        sel = outer.enter_context(nc.sbuf_tensor("b1_sel", [128, 2, TOKENS], F32))
        inv = outer.enter_context(nc.sbuf_tensor("b1_inv", [128, 2, TOKENS], F32))
        xa = outer.enter_context(nc.sbuf_tensor("b1_xa", [128, 2, TOKENS], F32))
        with ExitStack() as ctx:
            def sb(what, shape):
                return ctx.enter_context(nc.sbuf_tensor(f"b1_{what}", shape, F32))
            yr = sb("yr", [Q, 2, TOKENS])
            layer_norm(T, "b1_ln", x, y, None, lambda pool: pool.memset(xa[Q:128, :, :], 0.0),
                       affine=[(yr, p["rln"]), (xa[0:Q, :, :], p["ln1"])], func=ACT.Gelu)
            e = sb("e", [128, 1, TOKENS])
            g = sb("g", [128, IMAGES])
            gb = sb("gb", [128, 1, TOKENS])
            h1 = sb("h1", [128, 1, TOKENS])
            h2 = sb("h2", [64, 1, TOKENS])
            lg = sb("lg", [128, 4, TOKENS])
            win = cols(p["rin"], 2)
            linear(T, "b1_rin", 1, 2, lambda m, k: win[:, k, :], lambda k, at: yr[:, k, at],
                   by_act=biased(T, e, p["rinb"], ACT.Gelu), size=128)
            summed = T.sem("b1_summed")
            with nc.Block() as block:

                @block.vector
                def _(dve):
                    ev = e[:, 0, :].rearrange("p (b t) -> p b t", b=IMAGES)
                    dve.tensor_reduce(g[:, :], ev[:, :, 1:SEQ], AX.X, ALU.add).then_inc(summed, 1)
                    dve.wait_ge(summed, 1)
                    dve.tensor_scalar(gb[:, 0, :].rearrange("p (b t) -> p b t", b=IMAGES), spread(g[:, :], 2, SEQ),
                                      1.0 / (SEQ - 1), None, ALU.mult)
            wo1 = cols(p["ro1"], 2)
            linear(T, "b1_ro1", 1, 2, lambda m, k: wo1[:, k, :], lambda k, at: (e if k == 0 else gb)[:, 0, at],
                   by_act=biased(T, h1, p["ro1b"], ACT.Gelu), size=128)
            linear(T, "b1_ro2", 1, 1, lambda m, k: p["ro2"], lambda k, at: h1[:, 0, at],
                   by_act=biased(T, h2, p["ro2b"], ACT.Gelu), size=64)
            linear(T, "b1_ro3", 4, 1, lambda m, k: p["ro3"][:, m:m + 1].broadcast_to([64, 128]),
                   lambda k, at: h2[:, 0, at], by_act=biased(T, lg, p["ro3b"]), size=128)
            chosen = T.sem("b1_chosen")
            with nc.Block() as block:

                @block.vector
                def _(dve):
                    for b in range(2):
                        dve.tensor_tensor(bits[:, b, :], lg[:, 2 * b + 1, :], lg[:, 2 * b, :], ALU.is_gt)\
                            .then_inc(chosen, 1)
                    dve.wait_ge(chosen, 2)
                    for b in range(2):
                        dve.memset(bits[:, b, :].rearrange("p (b t) -> p b t", b=IMAGES)[:, :, 0:1], 1.0)
        with ExitStack() as ctx:
            def sb(what, shape):
                return ctx.enter_context(nc.sbuf_tensor(f"b1_{what}", shape, F32))
            qk = sb("qk", [Q, 4, TOKENS])
            v = sb("v", [128, IMAGES, DIM])
            att = sb("att", [Q, 2, TOKENS])
            w = [cols(T.full["mq"], 2), cols(T.full["mk"], 2)]
            linear(T, "b1_qk", 4, 2, lambda m, k: w[m // 2][:, k, Q * (m % 2):Q * (m % 2) + Q],
                   lambda k, at: xa[:, k, at], by_act=biased(T, qk, p["mqkvb"]))
            values_by_token(T, "b1_vals", xa, cols(T.full["mv"], 2), v[0:SEQ, :, :], SEQ, clear=v[:, :, :])
            head_attention(T, "b1_att", qk, v, p["mqkvb"][:, 4:6], att, False)
            wo = cols(p["mo"], 2)
            linear(T, "b1_wo", 2, 2, lambda m, k: wo[:, k, Q * m:Q * m + Q], lambda k, at: att[:, k, at],
                   by_dve=lambda m, at, psum: nc.vector.scalar_tensor_tensor(
                       res[:, m, at], psum, p["mob"][:, m:m + 1], bits[0:Q, 0, at], ALU.add, ALU.mult),
                   after=add_unit(T, res, x))
        with ExitStack() as ctx:
            def sb(what, shape):
                return ctx.enter_context(nc.sbuf_tensor(f"b1_{what}", shape, F32))
            xf = sb("xf", [128, 2, TOKENS])
            mid = sb("mid", [128, 6, TOKENS])
            ff = sb("ff", [Q, 2, TOKENS])
            step = T.sem("b1_sel_step")

            def select(pool):
                link = chained(pool, step)
                link(pool.memset(xf[Q:128, :, :], 0.0))
                link(pool.tensor_scalar(inv[:, :, :], bits[:, :, :], -1.0, 1.0, ALU.mult, ALU.add))
                link(pool.tensor_tensor(sel[0:64, 0, :], inv[0:64, 0, :], inv[0:64, 1, :], ALU.mult))
                link(pool.tensor_tensor(sel[64:128, 0, :], inv[64:128, 0, :], bits[64:128, 1, :], ALU.mult))
                pool.tensor_tensor(sel[0:64, 1, :], bits[0:64, 0, :], inv[0:64, 1, :], ALU.mult)

            layer_norm(T, "b1_lnf", res, y, None, select,
                       affine=[(xf[0:Q, :, :], p["ln2"])], func=ACT.Gelu)
            w1, w2 = cols(T.full["fc1"], 2), cols(p["fc2"], 6)
            linear(T, "b1_fc1", 6, 2, lambda m, k: w1[:, k, 128 * m:128 * m + 128], lambda k, at: xf[:, k, at],
                   by_act=biased(T, mid, p["fc1b"], ACT.Gelu), size=128)
            linear(T, "b1_fc2", 2, 6, lambda m, k: w2[:, k, Q * m:Q * m + Q], lambda k, at: mid[:, k, at],
                   by_dve=lambda m, at, psum: nc.vector.scalar_tensor_tensor(
                       ff[:, m, at], psum, p["fc2b"][:, m:m + 1], bits[0:Q, 1, at], ALU.add, ALU.mult),
                   after=add_unit(T, res, ff))
        with ExitStack() as ctx:
            def sb(what, shape):
                return ctx.enter_context(nc.sbuf_tensor(f"b1_{what}", shape, F32))
            d01 = sb("d01", [128, TOKENS])
            d2 = sb("d2", [64, TOKENS])

            def take_down(m, at, psum):
                out, chosen = ((d01, sel[:, 0, :]), (d2, sel[0:64, 1, :]))[m]
                return nc.vector.tensor_tensor(out[:, at], psum, chosen[:, at], ALU.mult)

            down = cols(p["ldown"], 2)
            linear(T, "b1_down", 2, 2, lambda m, k: down[:, k, 128 * m:min(128 * m + 128, DIM)], lambda k, at: res[:, k, at],
                   by_dve=take_down, size=[128, 64],
                   on_pool=lambda pool: pool.tensor_tensor(T.h[:, :, :], T.h[:, :, :], res[:, :, :], ALU.add))
            linear(T, "b1_up", 2, 2, lambda m, k: (p["lup01"] if k == 0 else p["lup2"])[:, Q * m:Q * m + Q],
                   lambda k, at: (d01 if k == 0 else d2)[:, at],
                   by_dve=lambda m, at, psum: nc.vector.tensor_tensor(T.h[:, m, at], T.h[:, m, at], psum, ALU.add))


def add_unit(T, out, x):
    def add(m, at):
        return T.nc.gpsimd.tensor_tensor(out[:, m, at], out[:, m, at], x[:, m, at], ALU.add)
    return add


def selective_scan(T):
    nc, p = T.nc, T.p
    FLAT = 2 * TOKENS
    with ExitStack() as ctx:
        def sb(what, shape, dt=F32):
            return ctx.enter_context(nc.sbuf_tensor(f"ssm_{what}", shape, dt))

        sem = lambda what: T.sem(f"ssm_{what}")
        pre, mag, delta = sb("pre", [Q, 2, TOKENS]), sb("mag", [Q, 2, TOKENS]), sb("delta", [Q, 2, TOKENS])
        inv_a = sb("inv_a", [Q, 2 * STATES])
        yacc = sb("y", [Q, FLAT])
        wbc = [sb(f"wbc{i}", [128, 4 * DIM]) for i in range(2)]
        w_high = [sb(f"w_high{i}", [128, 4 * DIM], F32R) for i in range(2)]
        w_low = [sb(f"w_low{i}", [128, 4 * DIM], F32R) for i in range(2)]
        x_high, x_low = (sb(x, [128, 2, TOKENS], F32R) for x in ("x_high", "x_low"))
        decay = [sb(f"decay{i}", [Q, FLAT]) for i in range(2)]
        bsel = [sb(f"bsel{i}", [Q, FLAT]) for i in range(2)]
        drive = [sb(f"drive{i}", [Q, FLAT]) for i in range(2)]
        bx = [sb(f"bx{i}", [Q, FLAT]) for i in range(2)]
        state = [sb(f"state{i}", [Q, FLAT]) for i in range(2)]
        out = [sb(f"out{i}", [Q, FLAT]) for i in range(2)]
        wd = cols(T.full["sD"], 2)
        linear(T, "ssm_delta", 2, 2, lambda m, k: wd[:, k, Q * m:Q * m + Q], lambda k, at: T.x_full[:, k, at],
               by_act=biased(T, pre, p["sDb"]))
        soft, high_x = sem("soft"), sem("high_x")
        with nc.Block() as block:

            @block.scalar
            def _(act):
                link = chained(act, soft)
                link(act.activation(mag[:, :, :], pre[:, :, :], ACT.Abs))
                link(act.activation(mag[:, :, :], mag[:, :, :], ACT.Exp, scale=-1.0))
                link(act.activation(mag[:, :, :], mag[:, :, :], ACT.Ln, bias=1.0))

            @block.vector
            def _(dve):
                dve.memset(yacc[:, :], 0.0)
                dve.reciprocal(inv_a[:, :], p["sA"])
                dve.tensor_copy(x_high[:, :, :], T.x_full[:, :, :]).then_inc(high_x, 1)
                dve.wait_ge(high_x, 1)
                dve.tensor_tensor(x_low[:, :, :], T.x_full[:, :, :], x_high[:, :, :], ALU.subtract)
                for j in range(2):
                    dve.memset(wbc[j][Q:128, :], 0.0)
                dve.wait_ge(soft, 3)
                dve.scalar_tensor_tensor(delta[:, :, :], pre[:, :, :], 0.0, mag[:, :, :], ALU.max, ALU.add)
        loaded = [sem(f"loaded{i}") for i in range(2)]
        b_made, c_made, decayed, b_out, driven, bx_made, scanned, read_out, added, pool_added, cleared, reset, act_seen, high, low_b, low_c = map(
            sem, ("b_made", "c_made", "decayed", "b_out", "driven", "bx_made", "scanned", "read_out", "added", "pool_added", "cleared", "reset", "act_seen",
                  "high", "low_b", "low_c"))
        block = ctx.enter_context(nc.Block())

        def next_state(i, j):
            return 1 - j, 16 * i + 16 + 16 * j

        HALF_W = 2 * DIM

        def load(sp, j, state):
            sp.dma_start(wbc[j][0:Q, :], T.dram["wBC"][state, :, :].rearrange("n p m -> (n p) m")).then_inc(loaded[j], 16)

        def split_high(act, j):
            act.copy(w_high[j][:, :], wbc[j][:, :]).then_inc(high, 1)

        def split_low(eng, j, at, low):
            eng.tensor_tensor(w_low[j][:, at], wbc[j][:, at], w_high[j][:, at], ALU.subtract).then_inc(low, 1)

        B_W, C_W = slice(0, HALF_W), slice(HALF_W, 2 * HALF_W)

        @block.sync
        def _(sp):
            sp.sem_inc(c_made, 8)
            sp.sem_inc(b_out, 8)
            sp.sem_inc(low_b, 1)
            sp.sem_inc(low_c, 1)
            load(sp, 0, slice(0, 1))
            with sp.Fori(0, STATES // 2) as i:
                for j in range(2):
                    sp.wait_ge(low_b, 2 * i + j + 1)
                    sp.wait_ge(low_c, 2 * i + j + 1)
                    load(sp, 1 - j, bass.ds(2 * i + j + 1, 1))

        @block.tensor
        def _(pe):
            pe.sem_inc(read_out, 4)
            with pe.Fori(0, STATES // 2) as i:
                for j in range(2):
                    for a in range(2):
                        pe.wait_ge(low_c if a else low_b, 2 * i + j + 2)
                        for u in range(4):
                            c, s = u // 2, HALF * (u % 2)
                            if a:
                                pe.wait_ge(read_out, 8 * i + 4 * j + u + 1)
                            else:
                                pe.wait_ge(b_out, 8 * i + 4 * j + u + 5)
                            for k in range(2):
                                w_at = DIM * (2 * a + k) + Q * c
                                for n, (w, x) in enumerate(((w_high, x_high), (w_high, x_low), (w_low, x_high))):
                                    mm = pe.matmul(T.bank[4 * a + u][0:Q, 0:HALF], w[j][:, w_at:w_at + Q],
                                                   x[:, k, s:s + HALF], start=(k == 0 and n == 0), stop=(k == 1 and n == 2))
                            mm.then_inc(c_made if a else b_made, 1)

        @block.scalar
        def _(act):
            act.sem_inc(scanned, 2)
            act.sem_inc(bx_made, 2)
            act.wait_ge(loaded[0], 16)
            split_high(act, 0)
            with act.Fori(0, STATES // 2) as i:
                for j in range(2):
                    other, loads = next_state(i, j)
                    act.wait_ge(loaded[other], loads)
                    act.wait_ge(c_made, 8 * i + 4 * j + 8)
                    split_high(act, other)
                    act.wait_ge(scanned, 2 * i + j + 1)
                    act.sem_inc(act_seen, 1)
                    for c in range(2):
                        act.activation(decay[j][:, TOKENS * c:TOKENS * c + TOKENS], delta[:, c, :], ACT.Exp,
                                       scale=p["sA"][:, bass.ds(4 * i + 2 * j + c, 1)]).then_inc(decayed, 1)
                    act.wait_ge(bx_made, 2 * i + j + 1)
                    for u in range(4):
                        c, s = u // 2, HALF * (u % 2)
                        act.wait_ge(b_made, 8 * i + 4 * j + u + 1)
                        act.sem_inc(act_seen, 1)
                        act.activation(bsel[j][:, HALF * u:HALF * u + HALF], T.bank[u][0:Q, 0:HALF], ACT.Copy,
                                       scale=inv_a[:, bass.ds(4 * i + 2 * j + c, 1)]).then_inc(b_out, 1)

        @block.gpsimd
        def _(pool):
            xflat = T.xn[:, :, :].rearrange("p c t -> p (c t)")
            pool.sem_inc(driven, 2)
            pool.memset(out[1][:, TOKENS:FLAT], 0.0).then_inc(cleared, 1)
            pool.wait_ge(cleared, 1)
            pool.wait_ge(high, 1)
            split_low(pool, 0, C_W, low_c)

            def add(j, last):
                pool.wait_ge(read_out, last)
                pool.tensor_tensor(yacc[:, TOKENS:FLAT], yacc[:, TOKENS:FLAT], out[j][:, TOKENS:FLAT], ALU.add)\
                    .then_inc(pool_added, 1)

            with pool.Fori(0, STATES // 2) as i:
                for j in range(2):
                    n = 2 * i + j
                    pool.wait_ge(high, n + 2)
                    split_low(pool, 1 - j, C_W, low_c)
                    pool.wait_ge(b_out, 8 * i + 4 * j + 12)
                    pool.wait_ge(driven, n + 1)
                    pool.tensor_tensor(bx[j][:, :], bsel[j][:, :], xflat, ALU.mult).then_inc(bx_made, 1)
                    pool.wait_ge(pool_added, n + 1)
                    add(1 - j, 8 * i + 4 * j + 4)
            pool.wait_ge(pool_added, STATES + 1)
            add((STATES - 1) % 2, 4 * STATES + 4)

        @block.vector
        def _(dve):
            dve.sem_inc(pool_added, 1)
            dve.wait_ge(high, 1)
            split_low(dve, 0, B_W, low_b)
            with dve.Fori(0, STATES // 2) as i:
                for j in range(2):
                    n = 2 * i + j
                    dve.wait_ge(high, n + 2)
                    split_low(dve, 1 - j, B_W, low_b)
                    dve.wait_ge(decayed, 4 * i + 2 * j + 2)
                    dve.wait_ge(bx_made, n + 3)
                    dve.scalar_tensor_tensor(drive[j][:, :], decay[j][:, :], 1.0, bx[j][:, :], ALU.subtract, ALU.mult)\
                        .then_inc(driven, 1)
                    dve.wait_ge(driven, n + 3)
                    first = decay[j][:, :].rearrange("p (b t) -> p b t", t=SEQ)[:, :, 0:1]
                    dve.memset(first, 0.0).then_inc(reset, 1)
                    dve.wait_ge(reset, n + 1)
                    dve.tensor_tensor_scan(state[j][:, :], decay[j][:, :], drive[j][:, :], 0.0, ALU.mult, ALU.add)\
                        .then_inc(scanned, 1)
                    dve.wait_ge(scanned, n + 3)
                    dve.wait_ge(pool_added, n + 1)
                    for u in range(4):
                        at = slice(HALF * u, HALF * u + HALF)
                        dve.wait_ge(c_made, 8 * i + 4 * j + u + 9)
                        dve.tensor_tensor(out[j][:, at], state[j][:, at], T.bank[4 + u][0:Q, 0:HALF], ALU.mult)\
                            .then_inc(read_out, 1)
                    dve.wait_ge(read_out, 8 * i + 4 * j + 8)
                    dve.tensor_tensor(yacc[:, 0:TOKENS], yacc[:, 0:TOKENS], out[j][:, 0:TOKENS], ALU.add).then_inc(added, 1)
                    dve.wait_ge(added, n + 1)
            dve.wait_ge(pool_added, STATES + 2)
            dve.tensor_tensor(T.h[:, :, :].rearrange("p c t -> p (c t)"), T.h[:, :, :].rearrange("p c t -> p (c t)"),
                              yacc[:, :], ALU.add)


def experts(T, key):
    nc, m = T.nc, MOE[key]
    K, B, N = m["top"], m["blocks"], m["width"] // m["chunks"]
    C = m["chunks"] * m["shared"]
    with ExitStack() as ctx:
        def sb(what, shape, dt=F32):
            return ctx.enter_context(nc.sbuf_tensor(f"{key}_{what}", shape, dt))

        weight = sb("weight", [TILE, TILES, K])
        slot = sb("slot", [TILE, K, TILES], U32)
        fetch = sb("fetch", [TILE, K, TILES], U32)
        plan = sb("plan", [1, B + 2], U32)
        shared_in = T.sem(f"{key}_shared_in")
        xt = sb("xt", [TILE, TILES, DIM])
        scattered = [T.sem(f"{key}_scattered{i}") for i in range(2)]
        with ExitStack() as inner:
            first, second = T.dram[f"{key}s1"], T.dram[f"{key}s2"]
            s1 = inner.enter_context(nc.sbuf_tensor(f"{key}_s1", [128, first.shape[1]], F32))
            s2 = inner.enter_context(nc.sbuf_tensor(f"{key}_s2", list(second.shape), F32))

            def meanwhile(sp):
                sp.dma_start(s1[0:Q, :], first).then_inc(shared_in, 16)
                sp.dma_start(s2[:, :], second).then_inc(shared_in, 16)
                sp.wait_ge(T.loaded[f"{key}a"], 16)
                sp.wait_ge(T.zeroed, 16 * sum(-(-x["rows"] // (128 * ZEROS)) for x in MOE.values()))
                sp.wait_ge(shared_in, 32)

            layer_norm(T, f"{key}f_ln", T.h, T.xn, meanwhile, lambda pool: pool.memset(s1[Q:128, :], 0.0),
                       func=ACT.Sigmoid if key == "L2" else ACT.Exp)
            route(T, key, weight, slot, fetch, plan, s1, s2, xt, scattered)
        run_blocks(T, key, T.rows[key], plan, xt, slot, scattered)
        combine(T, key, T.rows[key], weight, fetch)


def route(T, key, weight, slot, fetch, plan, s1, s2, xt, scattered):
    nc, p, m = T.nc, T.p, MOE[key]
    E, K, B, R, CAP = m["experts"], m["top"], m["blocks"], m["block"], m["cap"]
    N = m["width"] // m["chunks"]
    C = m["chunks"] * m["shared"]
    normed = key == "L3"
    HT = TILES // 2
    rows = T.rows[key]
    BIG = float(2 ** 20)
    RING = 5
    parts = 1 if normed else 2
    units = [(f, s, a) for f in range(C) for s in range(2) for a in range(parts)]
    with ExitStack() as ctx:
        def sb(what, shape, dt=F32):
            return ctx.enter_context(nc.sbuf_tensor(f"{key}_{what}", shape, dt))

        sem = lambda what: T.sem(f"{key}_{what}")
        value = sb("value", [TILE, TILES, E])
        choice = sb("choice", [TILE, TILES, E]) if key == "L2" else value
        best, best_at, at_f = sb("best", [TILE, TILES, 8]), sb("best_at", [TILE, TILES, 8], U32), sb("at_f", [TILE, TILES, 8])
        one_hot = sb("one_hot", [TILE, K, TILES, E])
        prod = sb("prod", [TILE, TILES, E])
        before = sb("before_tile", [TILE, TILES + 1, E])
        mask = sb("mask", [TILE, TILES, E])
        row_of, late = sb("row_of", [TILE, TILES, E]), sb("late", [TILE, TILES, E])
        stat = sb("stat", [TILE, TILES])
        k_row, k_w, keep, k_spare = (sb(x, [TILE, K, TILES]) for x in ("k_row", "k_w", "keep", "k_spare"))
        lost = sb("lost", [TILE, TILES])
        count, over, nblk, first, last = sb("count", [128, 1]), sb("over", [128, TILES]), sb("nblk", [128, 1]), sb("first", [128, 1]), sb("last", [128, 1])
        member, member2 = sb("member", [128, B]), sb("member2", [128, B])
        start_row = sb("start_row", [TILE, E])
        hid = sb("s_hid", [N, C, TOKENS])
        upv = sb("s_up", [N, C, TOKENS]) if not normed else sb("s_xc", [N, C, TOKENS])
        if normed:
            stat_s, eps = sb("s_stat", [N, 2, HALF]), sb("s_eps", [128, 1])
            mean_made, mean_in, centred, squared, var_made, dev_in, inverted, scaled, eps_set = map(
                sem, ("s_mean_made", "s_mean_in", "s_centred", "s_squared", "s_var_made", "s_dev_in", "s_inverted",
                      "s_scaled", "s_eps_set"))
        (x_turned, xt_in, logits_made, scored, soft, masked, located, counted, blocks_known, starts_made, members,
         planned, step, s_made, s_out, s_hidden, s_down, slots_known) = map(
            sem, ("x_turned", "xt_in", "logits_made", "scored", "soft", "masked", "located", "counted", "blocks_known",
                  "starts_made", "members", "planned", "dve_step", "s_made", "s_out", "s_hidden", "s_down",
                  "slots_known"))
        block = ctx.enter_context(nc.Block())
        w = cols(p[f"{key}gate"], 2)
        w1 = cols(s1[:, :], 2)
        w2 = cols(s2[:, 0:C * DIM], C)
        WIDE = C * N

        @block.tensor
        def _(pe):
            for g in range(2):
                for j in range(HT):
                    i = HT * g + j
                    for c in range(2):
                        mm = pe.matmul(T.bank[g][0:TILE, E * j:E * j + E], T.xn[:, c, TILE * i:TILE * i + TILE],
                                       w[:, c, :], start=(c == 0), stop=(c == 1))
                mm.then_inc(logits_made, 1)
            for i in range(TILES):
                for c in range(2):
                    mm = pe.transpose(T.bank[5 + i // 2][0:TILE, DIM * (i % 2) + Q * c:DIM * (i % 2) + Q * c + Q],
                                      T.xn[:, c, TILE * i:TILE * i + TILE], p["ident"][0:Q, 0:Q])
                if i % 2:
                    mm.then_inc(x_turned, 1)

            def shared_units(a, b):
                for u in range(a, min(b, len(units))):
                    f, s, part = units[u]
                    if 2 <= u < RING:
                        pe.wait_ge(xt_in, u - 1)
                    if u >= RING:
                        pe.wait_ge(s_out, u - RING + 1)
                    for c in range(2):
                        mm = pe.matmul(T.bank[3 + u % RING][0:N, 0:HALF],
                                       w1[:, c, WIDE * part + N * f:WIDE * part + N * f + N],
                                       T.x_full[:, c, HALF * s:HALF * s + HALF], start=(c == 0), stop=(c == 1))
                    mm.then_inc(s_made, 1)

            def positions():
                pe.wait_ge(masked, 1)
                pe.matmul(T.bank[2][0:E, 0:1], before[:, TILES, :], p["ones"][0:TILE, 0:1], start=True, stop=True)\
                    .then_inc(counted, 1)
                for g in range(2):
                    for j in range(HT):
                        i = HT * g + j
                        pe.matmul(T.bank[g][0:TILE, E * j:E * j + E], p["ones"][0:TILE, 0:TILE], before[:, i, :],
                                  start=True, stop=False)
                        mm = pe.matmul(T.bank[g][0:TILE, E * j:E * j + E], p["before"][0:TILE, 0:TILE], mask[:, i, :],
                                       start=False, stop=True)
                    mm.then_inc(located, 1)

            def starts():
                pe.wait_ge(blocks_known, 1)
                pe.matmul(T.bank[2][0:TILE, 0:E], nblk[0:E, 0:1].broadcast_to([E, TILE]), p["before"][0:E, 0:E],
                          start=True, stop=True)
                pe.matmul(T.bank[2][0:E, 128:129], p["before"][0:E, 0:E], nblk[0:E, 0:1], start=True, stop=True)\
                    .then_inc(starts_made, 1)

            def plans():
                pe.wait_ge(members, 1)
                pe.matmul(T.bank[2][0:1, 0:B], p["ecol"][0:E, 0:1], member[0:E, :], start=True, stop=True)
                pe.matmul(T.bank[2][0:1, B:B + 1], p["ones"][0:E, 0:1], nblk[0:E, 0:1], start=True, stop=True)\
                    .then_inc(planned, 1)

            half = len(units) // 2
            shared_units(0, half)
            positions()
            shared_units(half, half + 2)
            starts()
            shared_units(half + 2, half + 4)
            plans()
            shared_units(half + 4, len(units))
            if normed:
                for s in range(2):
                    pe.wait_ge(s_out, len(units))
                    for f in range(C):
                        mm = pe.matmul(T.bank[3 + s][0:N, 0:HALF], p["mean384"], hid[:, f, HALF * s:HALF * s + HALF],
                                       start=(f == 0), stop=(f == C - 1))
                    mm.then_inc(mean_made, 1)
                for s in range(2):
                    pe.wait_ge(squared, s + 1)
                    for f in range(C):
                        mm = pe.matmul(T.bank[3 + s][0:N, 0:HALF], p["mean384"], hid[:, f, HALF * s:HALF * s + HALF],
                                       start=(f == 0), stop=(f == C - 1))
                    mm.then_inc(var_made, 1)
            for u in range(4):
                mo, s = u // 2, u % 2
                if u < 2:
                    pe.wait_ge(s_hidden, 2 * C if not normed else 2)
                for f in range(C):
                    mm = pe.matmul(T.bank[4 + u][0:Q, 0:HALF], w2[:, f, Q * mo:Q * mo + Q],
                                   upv[:, f, HALF * s:HALF * s + HALF], start=(f == 0), stop=(f == C - 1))
                mm.then_inc(s_down, 1)

        @block.scalar
        def _(act):
            if key == "L2":
                for g in range(2):
                    act.wait_ge(logits_made, g + 1)
                    act.activation(value[:, HT * g:HT * g + HT, :], cols(T.bank[g][0:TILE, 0:HT * E], HT), ACT.Sigmoid)\
                        .then_inc(soft, 1)
            for u in range(TILES // 2):
                act.wait_ge(x_turned, u + 1)
                act.copy(xt[:, 2 * u:2 * u + 2, :], cols(T.bank[5 + u][0:TILE, 0:2 * DIM], 2)).then_inc(xt_in, 1)
            if key != "L2":
                act.wait_ge(scored, 1)
                act.activation(value[:, :, :], value[:, :, :], ACT.Exp).then_inc(soft, 1)
            for u, (f, s, part) in enumerate(units):
                at = slice(HALF * s, HALF * s + HALF)
                act.wait_ge(s_made, u + 1)
                got = T.bank[3 + u % RING][0:N, 0:HALF]
                if normed:
                    act.activation(hid[:, f, at], got, ACT.Gelu, bias=s2[:, C * DIM + f:C * DIM + f + 1]).then_inc(s_out, 1)
                elif part == 0:
                    act.activation(hid[:, f, at], got, ACT.Silu).then_inc(s_out, 1)
                else:
                    act.copy(upv[:, f, at], got).then_inc(s_out, 1)
            if normed:
                act.wait_ge(eps_set, 1)
                for s in range(2):
                    act.wait_ge(mean_made, s + 1)
                    act.copy(stat_s[:, s, :], T.bank[3 + s][0:N, 0:HALF]).then_inc(mean_in, 1)
                for s in range(2):
                    at = slice(HALF * s, HALF * s + HALF)
                    act.wait_ge(centred, s + 1)
                    act.activation(hid[:, :, at], upv[:, :, at], ACT.Square).then_inc(squared, 1)
                for s in range(2):
                    act.wait_ge(var_made, s + 1)
                    act.activation(stat_s[:, s, :], T.bank[3 + s][0:N, 0:HALF], ACT.Sqrt, bias=eps[0:N, 0:1]).then_inc(dev_in, 1)
                for s in range(2):
                    at = slice(HALF * s, HALF * s + HALF)
                    act.wait_ge(scaled, s + 1)
                    for f in range(C):
                        gain = C * DIM + C + f
                        ins = act.activation(upv[:, f, at], hid[:, f, at], ACT.Identity, scale=s2[:, gain:gain + 1],
                                             bias=s2[:, gain + C:gain + C + 1])
                    ins.then_inc(s_hidden, 1)

        @block.gpsimd
        def _(pool):
            if not normed:
                for f in range(C):
                    for s in range(2):
                        at = slice(HALF * s, HALF * s + HALF)
                        pool.wait_ge(s_out, 2 * (2 * f + s) + 2)
                        pool.tensor_tensor(upv[:, f, at], hid[:, f, at], upv[:, f, at], ALU.mult).then_inc(s_hidden, 1)
            else:
                for s in range(2):
                    at = slice(HALF * s, HALF * s + HALF)
                    pool.wait_ge(mean_in, s + 1)
                    pool.tensor_tensor(upv[:, :, at], hid[:, :, at], spread(stat_s[:, s, :], 1, C), ALU.subtract)\
                        .then_inc(centred, 1)
                for s in range(2):
                    at = slice(HALF * s, HALF * s + HALF)
                    pool.wait_ge(inverted, s + 1)
                    pool.tensor_tensor(hid[:, :, at], upv[:, :, at], spread(stat_s[:, s, :], 1, C), ALU.mult)\
                        .then_inc(scaled, 1)
            pool.wait_ge(xt_in, TILES // 2)
            for k in range(m["early"]):
                pool.wait_ge(slots_known, k + 1)
                scatter(pool, rows, xt, slot, k, scattered[k == K - 1])

        @block.vector
        def _(dve):
            link = chained(dve, step)
            if normed:
                dve.memset(eps[:, :], EPS).then_inc(eps_set, 1)
            gate_bias = p[f"{key}gateb"]
            if key == "L2":
                dve.wait_ge(soft, 2)
                link(dve.tensor_tensor(choice[:, :, :], value[:, :, :], spread(gate_bias, 1, TILES), ALU.add))
            else:
                for g in range(2):
                    dve.wait_ge(logits_made, g + 1)
                    link(dve.tensor_tensor(value[:, HT * g:HT * g + HT, :], cols(T.bank[g][0:TILE, 0:HT * E], HT),
                                           spread(gate_bias, 1, HT), ALU.add))
                if key == "L3":
                    link(dve.memset(value[:, :, 0:1], -1.0e9))
                link(dve.tensor_reduce(stat[:, :], value[:, :, :], AX.X, ALU.max))
                dve.tensor_tensor(value[:, :, :], value[:, :, :], spread(stat[:, :], 2, E), ALU.subtract)\
                    .then_inc(scored, 1)
                dve.wait_ge(soft, 1)
                link(dve.tensor_reduce(stat[:, :], value[:, :, :], AX.X, ALU.add))
                link(dve.reciprocal(stat[:, :], stat[:, :]))
                link(dve.tensor_tensor(value[:, :, :], value[:, :, :], spread(stat[:, :], 2, E), ALU.mult))
            for i in range(TILES):
                ins = dve.max(best[:, i, :], choice[:, i, :])
            link(ins)
            for i in range(TILES):
                ins = dve.max_index(best_at[:, i, :], best[:, i, :], choice[:, i, :])
            link(ins)
            link(dve.tensor_copy(at_f[:, :, :], best_at[:, :, :]))
            for k in range(K):
                ins = dve.tensor_tensor(one_hot[:, k, :, :], spread(p["iota"][0:TILE, 0:E], 1, TILES),
                                        at_f[:, :, k:k + 1].broadcast_to([TILE, TILES, E]), ALU.is_equal)
            link(ins)
            link(dve.tensor_tensor(mask[:, :, :], one_hot[:, 0, :, :], one_hot[:, 1, :, :], ALU.add))
            for k in range(2, K):
                link(dve.tensor_tensor(mask[:, :, :], mask[:, :, :], one_hot[:, k, :, :], ALU.add))
            link(dve.memset(before[:, 0, :], 0.0))
            for i in range(TILES):
                link(dve.tensor_tensor(before[:, i + 1, :], before[:, i, :], mask[:, i, :], ALU.add))
            dve.sem_inc(masked, 1)
            dve.wait_ge(counted, 1)
            link(dve.tensor_scalar(count[0:E, :], T.bank[2][0:E, 0:1], float(CAP), None, ALU.min))
            link(dve.tensor_tensor(over[0:E, :], count[0:E, 0:1].broadcast_to([E, TILES]), p[f"levels{R}"][0:E, :], ALU.is_gt))
            dve.tensor_reduce(nblk[0:E, :], over[0:E, :], AX.X, ALU.add).then_inc(blocks_known, 1)
            dve.wait_ge(starts_made, 1)
            link(dve.tensor_scalar(start_row[:, :], T.bank[2][0:TILE, 0:E], float(R), None, ALU.mult))
            link(dve.tensor_copy(first[0:E, :], T.bank[2][0:E, 128:129]))
            link(dve.tensor_tensor(last[0:E, :], first[0:E, :], nblk[0:E, :], ALU.add))
            link(dve.tensor_scalar(member[0:E, :], p["iota"][0:E, 0:B], first[0:E, 0:1], None, ALU.is_ge))
            link(dve.tensor_scalar(member2[0:E, :], p["iota"][0:E, 0:B], last[0:E, 0:1], None, ALU.is_lt))
            dve.tensor_tensor(member[0:E, :], member[0:E, :], member2[0:E, :], ALU.mult).then_inc(members, 1)
            for g in range(2):
                dve.wait_ge(located, g + 1)
                at = slice(HT * g, HT * g + HT)
                got = cols(T.bank[g][0:TILE, 0:HT * E], HT)
                link(dve.tensor_tensor(row_of[:, at, :], got, spread(start_row[:, :], 1, HT), ALU.add))
                if CAP < TOKENS:
                    link(dve.tensor_scalar(late[:, at, :], got, float(CAP), BIG, ALU.is_ge, ALU.mult))
                    link(dve.tensor_tensor(row_of[:, at, :], row_of[:, at, :], late[:, at, :], ALU.add))
            if CAP < TOKENS:
                link(dve.tensor_scalar(k_spare[:, :, :], cols(p["spare"], 6)[:, 0:K, :], float(m["rows"]), None, ALU.add))
            for k in range(K):
                link(dve.tensor_tensor(prod[:, :, :], one_hot[:, k, :, :], row_of[:, :, :], ALU.mult))
                link(dve.tensor_reduce(k_row[:, k, :], prod[:, :, :], AX.X, ALU.add))
                if CAP < TOKENS:
                    link(dve.tensor_scalar(keep[:, k, :], k_row[:, k, :], BIG, None, ALU.is_lt))
                    link(dve.tensor_scalar(lost[:, :], k_row[:, k, :], BIG, None, ALU.is_ge))
                    link(dve.tensor_tensor(k_row[:, k, :], k_row[:, k, :], keep[:, k, :], ALU.mult))
                    link(dve.tensor_tensor(lost[:, :], lost[:, :], k_spare[:, k, :], ALU.mult))
                    link(dve.tensor_tensor(lost[:, :], lost[:, :], k_row[:, k, :], ALU.add))
                    dve.tensor_copy(slot[:, k, :], lost[:, :]).then_inc(slots_known, 1)
                    dve.wait_ge(slots_known, k + 1)
                else:
                    dve.tensor_copy(slot[:, k, :], k_row[:, k, :]).then_inc(slots_known, 1)
            link(dve.tensor_copy(fetch[:, :, :], k_row[:, :, :]))
            if key == "L2":
                for k in range(K):
                    link(dve.tensor_tensor(prod[:, :, :], one_hot[:, k, :, :], value[:, :, :], ALU.mult))
                    link(dve.tensor_reduce(k_w[:, k, :], prod[:, :, :], AX.X, ALU.add))
            else:
                link(dve.tensor_copy(k_w[:, :, :], best[:, :, 0:K].rearrange("p i k -> p k i")))
            if key != "L3":
                link(dve.tensor_reduce(stat[:, :], k_w[:, :, :].rearrange("p k i -> p i k"), AX.X, ALU.add))
                if key == "L2":
                    link(dve.tensor_scalar(stat[:, :], stat[:, :], 1e-20, None, ALU.add))
                link(dve.reciprocal(stat[:, :], stat[:, :]))
                link(dve.tensor_tensor(k_w[:, :, :], k_w[:, :, :], spread(stat[:, :], 1, K), ALU.mult))
                if key == "L2":
                    link(dve.tensor_scalar(k_w[:, :, :], k_w[:, :, :], 2.5, None, ALU.mult))
            if CAP < TOKENS:
                link(dve.tensor_tensor(k_w[:, :, :], k_w[:, :, :], keep[:, :, :], ALU.mult))
            dve.tensor_copy(weight[:, :, :], k_w[:, :, :].rearrange("p k i -> p i k"))
            dve.wait_ge(planned, 1)
            dve.tensor_copy(plan[0:1, 0:B + 1], T.bank[2][0:1, 0:B + 1])
            if normed:
                for s in range(2):
                    dve.wait_ge(dev_in, s + 1)
                    dve.reciprocal(stat_s[:, s, :], stat_s[:, s, :]).then_inc(inverted, 1)
            for u in range(4):
                mo, s = u // 2, u % 2
                at = slice(HALF * s, HALF * s + HALF)
                dve.wait_ge(s_down, u + 1)
                got = T.bank[4 + u][0:Q, 0:HALF]
                if normed:
                    dve.scalar_tensor_tensor(T.h[:, mo, at], got, p["L3b2v"][:, mo:mo + 1], T.h[:, mo, at], ALU.add, ALU.add)
                else:
                    dve.tensor_tensor(T.h[:, mo, at], T.h[:, mo, at], got, ALU.add)


def scatter(pool, rows, xt, slot, k, scattered):
    for i in range(TILES):
        pool.indirect_dma_start(rows[:, :], bass.IndirectOffsetOnAxis(ap=slot[:, k, i:i + 1], axis=0),
                                xt[:, i, :], None).then_inc(scattered, 16)


def run_blocks(T, key, rows, plan, xt_rows, slot, scattered):
    nc, p, m = T.nc, T.p, MOE[key]
    B, R, I, C, K, group = m["blocks"], m["block"], m["width"], m["chunks"], m["top"], m["group"]
    N = I // C
    normed = key == "L3"
    w1_d, w2_d = T.dram[f"{key}w1"], T.dram[f"{key}w2"]
    W1, W2 = w1_d.shape[2], w2_d.shape[2]
    EXPERTS = w1_d.shape[0]
    product = [T.bank[2 * j] for j in range(STEP)]
    other = [T.bank[2 * j + 1] for j in range(STEP)]
    with ExitStack() as ctx:
        def sb(what, shape, n=STEP):
            return [ctx.enter_context(nc.sbuf_tensor(f"{key}_{what}{j}", shape, F32)) for j in range(n)]

        sem = lambda what: T.sem(f"{key}_{what}")
        BUFS = SETS * STEP
        w1, w2, xr, xt, hid, act_out, y = (sb("w1", [128, W1], BUFS), sb("w2", [N, W2], BUFS), sb("xr", [R, DIM], BUFS),
                                           sb("xtb", [128, 2, R]), sb("hid", [N, C, R]), sb("act", [N, C, R]), sb("yb", [R, DIM]))
        if normed:
            sq, sd, yb2 = sb("sq", [N, C, R]), sb("sd", [N, R]), sb("b2", [1, DIM], BUFS)
            eps = ctx.enter_context(nc.sbuf_tensor(f"{key}_eps", [128, 1], F32))
        loaded = [sem(f"loaded{j}") for j in range(BUFS)]
        stored = [sem(f"stored{j}") for j in range(STEP)]
        turned, xt_in, gate, up, acted, hidden, down, y_in = map(
            sem, ("turned", "xtb_in", "gate", "up", "acted", "hidden", "down", "y_in"))
        means, centred, squared, variances, deviated, inverted, scaled, pool_seen, eps_set = map(
            sem, ("means", "centred", "squared", "variances", "deviated", "inverted", "scaled", "pool_seen", "eps_set"))
        all_stored, padded = sem("all_stored"), sem("padded")
        loads = 64 if normed else 48
        block = ctx.enter_context(nc.Block())

        def steps_in_use(eng, body):
            n = eng.value_load(plan[0:1, B:B + 1], min_val=1, max_val=B)
            with eng.Fori(0, m["groups"]) as g:
                with eng.If(g * (SETS * STEP * group) < n):
                    with eng.Fori(0, group) as i:
                        for h in range(SETS):
                            r = g * group + i
                            q = r * SETS + h
                            with eng.If(q * STEP < n):
                                body(r, q, STEP * h)
            return n

        @block.sync
        def _(sp):
            sp.sem_inc(down, BUFS)

            def step(r, q, s):
                for j in range(STEP):
                    b = q * STEP + j
                    e = sp.value_load(plan[0:1, bass.ds(b, 1)], min_val=0, max_val=EXPERTS - 1)
                    sp.wait_ge(down, b + 1)
                    sp.dma_start(w1[s + j][0:Q, :], w1_d[bass.ds(e, 1), :, :].rearrange("e p n -> (e p) n"))\
                        .then_inc(loaded[s + j], 16)
                    sp.dma_start(w2[s + j][:, :], w2_d[bass.ds(e, 1), :, :].rearrange("e p n -> (e p) n"))\
                        .then_inc(loaded[s + j], 16)
                    if normed:
                        sp.dma_start(yb2[s + j][:, :], T.dram["L3b2"][bass.ds(e, 1), :]).then_inc(loaded[s + j], 16)
                sp.wait_ge(scattered[0], 16 * (K - 1) * TILES)
                sp.wait_ge(scattered[1], 16 * TILES)
                for j in range(STEP):
                    sp.dma_start(xr[s + j][:, :], rows[bass.ds((q * STEP + j) * R, R), :]).then_inc(loaded[s + j], 16)

            steps_in_use(sp, step)

        @block.tensor
        def _(pe):
            pe.sem_inc(y_in, STEP)
            pe.wait_ge(scattered[0], 16 * (K - 1) * TILES)
            wake(T, T.bank[7], WARM)
            pe.wait_ge(padded, STEP + BUFS)

            def step(r, q, s):
                for j in range(STEP):
                    pe.wait_ge(loaded[s + j], r * loads + loads)
                    for c in range(2):
                        mm = pe.transpose(other[j][0:Q, R * c:R * c + R], xr[s + j][:, Q * c:Q * c + Q],
                                          p["ident"][0:R, 0:R])
                    mm.then_inc(turned, 1)
                for j in range(STEP):
                    pe.wait_ge(xt_in, q * STEP + j + 1)
                    pe.wait_ge(y_in, q * STEP + j + 1)
                    w = cols(w1[s + j][:, 0:W1 - W1 % 2], 2)
                    for a in range(1 if normed else 2):
                        for f in range(C):
                            for c in range(2):
                                mm = pe.matmul((other if a else product)[j][0:N, R * f:R * f + R],
                                               w[:, c, I * a + N * f:I * a + N * f + N], xt[j][:, c, :],
                                               start=(c == 0), stop=(c == 1))
                        mm.then_inc(up if a else gate, 1)
                if normed:
                    for j in range(STEP):
                        pe.wait_ge(acted, q * STEP + j + 1)
                        for f in range(C):
                            mm = pe.matmul(other[j][0:N, 0:R], p["mean384"], hid[j][:, f, :],
                                           start=(f == 0), stop=(f == C - 1))
                        mm.then_inc(means, 1)
                    for j in range(STEP):
                        pe.wait_ge(squared, q * STEP + j + 1)
                        for f in range(C):
                            mm = pe.matmul(other[j][0:N, R:2 * R], p["mean384"], sq[j][:, f, :],
                                           start=(f == 0), stop=(f == C - 1))
                        mm.then_inc(variances, 1)
                    wake(T, product[STEP - 1], BRIDGE)
                for j in range(STEP):
                    pe.wait_ge(hidden, q * STEP + j + 1)
                    w = cols(w2[s + j][:, 0:C * DIM], C)
                    if normed:
                        pe.matmul(product[j][0:R, 0:DIM], p["ones"][0:1, 0:R], yb2[s + j][:, :], start=True, stop=False)
                    for f in range(C):
                        mm = pe.matmul(product[j][0:R, 0:DIM], act_out[j][:, f, :], w[:, f, :],
                                       start=(f == 0 and not normed), stop=(f == C - 1))
                    mm.then_inc(down, 1)

            steps_in_use(pe, step)

        @block.scalar
        def _(act):
            for j in range(STEP):
                act.sem_inc(stored[j], 16)
            if normed:
                act.wait_ge(eps_set, 1)

            def step(r, q, s):
                for j in range(STEP):
                    act.wait_ge(gate, q * STEP + j + 1)
                    got = cols(product[j][0:N, 0:C * R], C)
                    if not normed:
                        act.activation(hid[j][:, :, :], got, ACT.Silu).then_inc(acted, 1)
                    else:
                        for f in range(C):
                            ins = act.activation(hid[j][:, f, :], got[:, f, :], ACT.Gelu,
                                                 bias=w2[s + j][:, C * DIM + f:C * DIM + f + 1])
                        ins.then_inc(acted, 1)
                if normed:
                    T.load_table(ACT.Sqrt)
                    for j in range(STEP):
                        act.wait_ge(centred, q * STEP + j + 1)
                        act.activation(sq[j][:, :, :], act_out[j][:, :, :], ACT.Square).then_inc(squared, 1)
                    for j in range(STEP):
                        act.wait_ge(variances, q * STEP + j + 1)
                        act.activation(sd[j][:, :], other[j][0:N, R:2 * R], ACT.Sqrt, bias=eps[:, 0:1])\
                            .then_inc(deviated, 1)
                    T.load_table(ACT.Gelu)
                for j in range(STEP):
                    act.wait_ge(down, q * STEP + j + BUFS + 1)
                    act.wait_ge(stored[j], q * 16 + 16)
                    act.copy(y[j][:, :], product[j][0:R, 0:DIM]).then_inc(y_in, 1)
                    act.wait_ge(y_in, q * STEP + j + STEP + 1)
                    act.dma_start(rows[bass.ds((q * STEP + j) * R, R), :], y[j][:, :]).then_inc(stored[j], 16)

            n = steps_in_use(act, step)
            for j in range(STEP):
                act.wait_ge(stored[j], (n + STEP - 1) // STEP * 16 + 16)
                act.sem_inc(all_stored, 1)

        @block.vector
        def _(dve):
            if normed:
                dve.memset(eps[:, :], EPS).then_inc(eps_set, 1)

            for j in range(STEP):
                dve.memset(xt[j][Q:128, :, :], 0.0).then_inc(padded, 1)
            for j in range(BUFS):
                dve.memset(w1[j][Q:128, :], 0.0).then_inc(padded, 1)

            def step(r, q, s):
                for j in range(STEP):
                    dve.wait_ge(turned, q * STEP + j + 1)
                    dve.tensor_copy(xt[j][0:Q, :, :], cols(other[j][0:Q, 0:2 * R], 2)).then_inc(xt_in, 1)
                if not normed:
                    for j in range(STEP):
                        dve.wait_ge(acted, q * STEP + j + 1)
                        dve.wait_ge(up, q * STEP + j + 1)
                        dve.tensor_tensor(act_out[j][:, :, :], hid[j][:, :, :], cols(other[j][0:N, 0:C * R], C),
                                          ALU.mult).then_inc(hidden, 1)
                else:
                    for j in range(STEP):
                        dve.wait_ge(means, q * STEP + j + 1)
                        dve.tensor_tensor(act_out[j][:, :, :], hid[j][:, :, :],
                                          spread(other[j][0:N, 0:R], 1, C), ALU.subtract).then_inc(centred, 1)
                    for j in range(STEP):
                        dve.wait_ge(deviated, q * STEP + j + 1)
                        dve.reciprocal(sd[j][:, :], sd[j][:, :]).then_inc(inverted, 1)
                        dve.wait_ge(inverted, q * STEP + j + 1)
                        dve.tensor_tensor(hid[j][:, :, :], act_out[j][:, :, :], spread(sd[j][:, :], 1, C), ALU.mult)\
                            .then_inc(scaled, 1)

            steps_in_use(dve, step)

        @block.gpsimd
        def _(pool):
            for k in range(m["early"], K):
                scatter(pool, rows, xt_rows, slot, k, scattered[k == K - 1])
            if normed:
                def step(r, q, s):
                    for j in range(STEP):
                        pool.wait_ge(scaled, q * STEP + j + 1)
                        pool.sem_inc(pool_seen, 1)
                        for f in range(C):
                            gain = C * DIM + C + f
                            ins = pool.tensor_scalar(act_out[j][:, f, :], hid[j][:, f, :], w2[s + j][:, gain:gain + 1],
                                                     w2[s + j][:, gain + C:gain + C + 1], ALU.mult, ALU.add)
                        ins.then_inc(hidden, 1)

                steps_in_use(pool, step)


def combine(T, key, rows, weight, fetch):
    nc, p, m = T.nc, T.p, MOE[key]
    K, B = m["top"], m["blocks"]
    with ExitStack() as ctx:
        def sb(what, shape):
            return ctx.enter_context(nc.sbuf_tensor(f"{key}_{what}", shape, F32))

        sem = lambda what: T.sem(f"{key}_{what}")
        acc = sb("acc", [TILE, TILES, DIM])
        got = sb("got", [TILE, K, TILES, DIM])
        added, turned = map(sem, ("added", "y_turned"))
        fetched = [sem(f"fetched{i}") for i in range(TILES)]
        HT = TILES // 2
        block = ctx.enter_context(nc.Block())

        @block.gpsimd
        def _(pool):
            for i in range(TILES):
                for k in range(K):
                    pool.indirect_dma_start(got[:, k, i, :], None, rows[0:m["rows"], :],
                                            bass.IndirectOffsetOnAxis(ap=fetch[:, k, i:i + 1], axis=0))\
                        .then_inc(fetched[i], 16)

        @block.vector
        def _(dve):
            def into_h(half):
                for c in range(2):
                    at = slice(HALF * half, HALF * half + HALF)
                    dve.wait_ge(turned, 2 * half + c + 1)
                    dve.tensor_tensor(T.h[:, c, at], T.h[:, c, at], T.bank[2 * half + c][0:Q, 0:HALF], ALU.add)

            for i in range(TILES):
                dve.wait_ge(fetched[i], 16 * K)
                for k in range(K):
                    if k == 0:
                        ins = dve.tensor_scalar(acc[:, i, :], got[:, 0, i, :], weight[:, i, 0:1], None, ALU.mult)
                    else:
                        dve.wait_ge(added, K * i + k)
                        ins = dve.scalar_tensor_tensor(acc[:, i, :], got[:, k, i, :], weight[:, i, k:k + 1], acc[:, i, :],
                                                       ALU.mult, ALU.add)
                    ins.then_inc(added, 1)
                if i == HT:
                    into_h(0)
            into_h(1)

        @block.tensor
        def _(pe):
            for half in range(2):
                if half:
                    wake(T, T.bank[7], WARM)
                for c in range(2):
                    for j in range(HT):
                        pe.wait_ge(added, K * (HT * half + j + 1))
                        mm = pe.transpose(T.bank[2 * half + c][0:Q, TILE * j:TILE * j + TILE],
                                          acc[:, HT * half + j, Q * c:Q * c + Q], p["ident"][0:TILE, 0:TILE])
                    mm.then_inc(turned, 1)


def layer3_attention(T):
    nc, p = T.nc, T.p
    with ExitStack() as ctx:
        def sb(what, shape):
            return ctx.enter_context(nc.sbuf_tensor(f"a3_{what}", shape, F32))
        qk, v, att = sb("qk", [Q, 4, TOKENS]), sb("v", [128, IMAGES, DIM]), sb("att", [Q, 2, TOKENS])
        w = cols(T.full["aqkv"], 2)
        linear(T, "a3_qk", 4, 2, lambda m, k: w[:, k, Q * m:Q * m + Q], lambda k, at: T.x_full[:, k, at],
               by_act=biased(T, qk, p["aqkvb"]))
        values_by_token(T, "a3_vals", T.x_full, w[:, :, 2 * DIM:3 * DIM], v[0:SEQ, :, :], SEQ,
                        clear=v[:, :, :])
        head_attention(T, "a3_att", qk, v, p["aqkvb"][:, 4:6], att, True)
        w2 = cols(p["aproj"], 2)
        linear(T, "a3_proj", 2, 2, lambda m, k: w2[:, k, Q * m:Q * m + Q], lambda k, at: att[:, k, at],
               by_dve=residual(T, T.h, p["aprojb"]))


def store_output(T):
    nc, p = T.nc, T.p
    with ExitStack() as ctx:
        out = ctx.enter_context(nc.sbuf_tensor("out_rows", [TILE, TILES, DIM], F32))
        turned = T.sem("out_turned")
        taken = T.sem("out_taken")
        stored = T.sem("out_stored")
        block = ctx.enter_context(nc.Block())

        @block.tensor
        def _(pe):
            for i in range(TILES):
                for c in range(2):
                    mm = pe.transpose(T.bank[i // 2][0:TILE, DIM * (i % 2) + Q * c:DIM * (i % 2) + Q * c + Q],
                                      T.h[:, c, TILE * i:TILE * i + TILE], p["ident"][0:Q, 0:Q])
                if i % 2:
                    mm.then_inc(turned, 1)

        @block.vector
        def _(dve):
            for u in range(TILES // 2):
                dve.wait_ge(turned, u + 1)
                dve.tensor_copy(out[:, 2 * u:2 * u + 2, :], cols(T.bank[u][0:TILE, 0:2 * DIM], 2)).then_inc(taken, 1)

        @block.sync
        def _(sp):
            sp.wait_ge(taken, TILES // 2)
            sp.dma_start(T.dram["out"].rearrange("(i p) d -> p i d", p=TILE), out[:, :, :]).then_inc(stored, 16)
            sp.wait_ge(stored, 16)


STAGES = ["tok", "L0a", "L0f", "L1a", "L1f", "L2a", "L2f", "L3a", "L3f"]


def build(nc, dram, stages=STAGES):
    with ExitStack() as ctx:
        T = Tower(nc, ctx, dram)
        load_all(T)
        T.end_layer()
        plain = {"L0a": layer0_attention, "L1a": layer1_attention, "L1f": layer1_block, "L2a": selective_scan,
                 "L3a": layer3_attention}
        for s in stages:
            if s in plain:
                layer_norm(T, f"{s}_ln", T.h, T.xn, lambda sp: sp.wait_ge(T.loaded[s], 16),
                           func=ACT.Exp if s in ("L0a", "L2a", "L3a") else None)
                plain[s](T)
                T.end_layer()
            elif s.endswith("f"):
                experts(T, s[:2])
                T.end_layer()
        store_output(T)


def fm(w):
    return np.concatenate([w[:Q], w[Q:]], axis=1)


def vec(*bs):
    return np.concatenate([b.reshape(-1, Q).T for b in bs], axis=1)


def chunks(w, n):
    return w.reshape(-1, n, w.shape[1]).transpose(1, 0, 2).reshape(n, -1)


def constants():
    i = np.arange(128)
    pair = np.arange(PAIR) // SEQ
    same = (pair[:, None] == pair[None, :])
    k, t, q = np.meshgrid(np.arange(6), np.arange(TILES), np.arange(TILE), indexing="ij")
    return {
        "ident": np.eye(128), "ones": np.ones((128, 128)), "mean192": np.full((Q, Q), 1 / DIM),
        "mean384": np.full((128, 128), 1 / 384), "before": i[:, None] < i[None, :],
        "iota": np.broadcast_to(np.arange(MAX_BLOCKS), (128, MAX_BLOCKS)), "ecol": i[:, None],
        "levels96": np.broadcast_to(96 * np.arange(TILES), (128, TILES)),
        "levels128": np.broadcast_to(128 * np.arange(TILES), (128, TILES)),
        "spare": (TOKENS * k + TILE * t + q).transpose(2, 0, 1).reshape(TILE, -1),
        "apart": np.where(same, 0.0, -1.0e30), "same": same,
        "headmask": (np.arange(Q) // HEAD_DIM)[:, None] == np.arange(6)[None, :],
    }


def layout(x):
    def rows(b, n):
        return np.broadcast_to(b.reshape(1, -1), (n, b.size))

    f = constants()
    f.update(tokW=chunks(x["L0_tok_W"], 128), tokb=vec(x["L0_tok_b"]),
             l0qkv=fm(x["L0_attn_w_qkv"].T), l0qkvb=vec(x["L0_attn_b_qkv"]), l0proj=fm(x["L0_attn_w_proj"].T),
             l0projb=vec(x["L0_attn_b_proj"]), L0gate=fm(x["L0_ffn_w_gate"]), L0gateb=rows(x["L0_ffn_expert_bias"], TILE),
             l1q=fm(x["L1_attn_Wq"].T), l1k=fm(x["L1_attn_Wk"].T), l1v=fm(x["L1_attn_Wv"].T),
             l1qkb=vec(x["L1_attn_bq"], x["L1_attn_bk"]), l1vb=rows(x["L1_attn_bv"], PAIR))
    b = {k[7:]: v for k, v in x.items() if k.startswith("L1_ffn_")}
    f.update(mq=fm(b["wq"].T), mk=fm(b["wk"].T), mv=fm(b["wv"].T), mo=fm(b["wo"].T), mqkvb=vec(b["bq"], b["bk"], b["bv"]),
             mob=vec(b["bo"]), ln1=vec(b["ln1_g"], b["ln1_b"]), ln2=vec(b["ln2_g"], b["ln2_b"]),
             rln=vec(b["r_ln_g"], b["r_ln_b"]), fc1=fm(b["fc1_w"].T), fc1b=b["fc1_b"].reshape(6, 128).T,
             fc2=chunks(b["fc2_w"].T, 128), fc2b=vec(b["fc2_b"]), rin=fm(b["r_in_w"].T), rinb=b["r_in_b"][:, None],
             ro1=chunks(b["r_o1_w"].T, 128), ro1b=b["r_o1_b"][:, None], ro2=b["r_o2_w"].T, ro2b=b["r_o2_b"][:, None],
             ro3=b["r_o3_w"].T, ro3b=rows(b["r_o3_b"], 128), ldown=fm(b["lra_down"].reshape(192, DIM).T),
             lup01=b["lra_up"][:2].transpose(0, 2, 1).reshape(128, DIM), lup2=b["lra_up"][2].T)
    A = x["L2_attn_A"]
    f.update(sD=fm(x["L2_attn_W_delta"].T), sDb=vec(x["L2_attn_delta_bias"]),
             sA=A.reshape(2, Q, STATES).transpose(1, 2, 0).reshape(Q, 2 * STATES),
             L2gate=fm(x["L2_ffn_Wg"].T), L2gateb=rows(x["L2_ffn_e_bias"], TILE),
             aqkv=fm(x["L3_attn_W_qkv"]), aqkvb=vec(x["L3_attn_b_qkv"]), aproj=fm(x["L3_attn_W_proj"]),
             aprojb=vec(x["L3_attn_b_proj"]), L3gate=fm(x["L3_ffn_gate_w"]), L3gateb=rows(x["L3_ffn_gate_b"], TILE), L3b2v=vec(x["L3_ffn_fc2_b"][0]))
    out = {}
    for g, items in GROUPS.items():
        t = out[g] = np.zeros((128, WIDTHS[g]), np.float32)
        at = 0
        for name, parts, n in items:
            t[0:parts, at:at + n] = f[name]
            at += n
    im = x["x"].reshape(IMAGES, 3, 6, 16, 6, 16).transpose(1, 3, 5, 0, 2, 4).reshape(PATCH_K, 128, TOKENS)
    out["patches"] = np.ascontiguousarray(im.transpose(1, 0, 2))
    bc = np.stack([x["L2_attn_W_B"], x["L2_attn_W_C"]]).reshape(2, DIM, STATES, 2, Q)
    bc = bc.transpose(2, 4, 0, 3, 1).reshape(STATES, Q, 4 * DIM)
    out["wBC"] = np.concatenate([bc, np.zeros_like(bc[:1])])

    def first(w):
        return w.reshape(w.shape[0], 2, Q, w.shape[2]).transpose(0, 2, 1, 3).reshape(w.shape[0], Q, -1)

    def second(w, n):
        return w.reshape(w.shape[0], -1, n, DIM).transpose(0, 2, 1, 3).reshape(w.shape[0], n, -1)

    out["L0w1"] = first(np.concatenate([x["L0_ffn_wg"], x["L0_ffn_wu"]], axis=2))
    out["L0w2"] = second(x["L0_ffn_wd"], 128)
    out["L0s1"] = first(np.concatenate([x["L0_ffn_swg"], x["L0_ffn_swu"]], axis=1)[None])[0]
    out["L0s2"] = second(x["L0_ffn_swd"][None], 128)[0]
    out["L2w1"] = first(x["L2_ffn_W_gate_up"])
    out["L2w2"] = second(x["L2_ffn_W_down"], 116)
    out["L2s1"] = first(np.concatenate([x["L2_ffn_Wsg"], x["L2_ffn_Wsu"]], axis=1)[None])[0]
    out["L2s2"] = second(x["L2_ffn_Wsd"][None], 116)[0]
    out["L3w1"] = first(x["L3_ffn_fc1_w"])
    cols3 = [x[k].reshape(16, 3, 128).transpose(0, 2, 1) for k in ("L3_ffn_fc1_b", "L3_ffn_ln_w", "L3_ffn_ln_b")]
    out["L3w2"] = np.concatenate([second(x["L3_ffn_fc2_w"], 128)] + cols3, axis=2)
    out["L3s1"], out["L3s2"] = out["L3w1"][0], out["L3w2"][0]
    out["L3b2"] = x["L3_ffn_fc2_b"]
    return {k: np.ascontiguousarray(v) for k, v in out.items()}


def kernel(**inputs):
    import concourse.bacc as bacc
    from concourse.bass_utils import run_bass_kernel_spmd

    nc = bacc.Bacc("TRN2", target_bir_lowering=False, num_devices=1)
    arrays = layout({k: np.asarray(v) for k, v in inputs.items()})
    dram = {k: nc.dram_tensor(f"in_{k}", a.shape, F32, kind="ExternalInput").ap() for k, a in arrays.items()}
    dram["out"] = nc.dram_tensor("out_h", (TOKENS, DIM), F32, kind="ExternalOutput").ap()
    build(nc, dram)
    r = run_bass_kernel_spmd(nc, [{f"in_{k}": a for k, a in arrays.items()}], core_ids=[0])
    return r.results[0]["out_h"].reshape(IMAGES, SEQ, DIM)
```
